# Optimizing a Trainium2 kernel written in Bass

```python
import numpy as np
import jax
import jax.numpy as jnp

def _softmax(x, axis=-1):
    return jax.nn.softmax(x, axis=axis)

def _gelu(x):
    return jax.nn.gelu(x, approximate=True)

def _silu(x):
    return jax.nn.silu(x)

def _sigmoid(x):
    return jax.nn.sigmoid(x)

def _layernorm(x, axis=-1, eps=1e-05):
    m = jnp.mean(x, axis=axis, keepdims=True)
    v = jnp.var(x, axis=axis, keepdims=True)
    return (x - m) / jnp.sqrt(v + eps)

def _scatter_add(tgt, idx, src, axis=0):
    return tgt.at[idx].add(src)

def _segment_sum(src, seg, n):
    return jax.ops.segment_sum(src, seg, n)
kernel_name = 'mk_gnn_resnorm_d4_gnn_r64_f1e9b1'

def setup_inputs(seed: int=0):
    np.random.seed(seed)
    _w = jnp.asarray

    def _rec_inputs():
        import jax
        import jax.numpy as jnp
        _gk = jax.random.key(seed)
        x = -0.0006008 + 1.001 * jax.random.normal(jax.random.fold_in(_gk, 1), (100000, 64), jnp.float32)
        src = jax.random.randint(jax.random.fold_in(_gk, 2), (25000,), 0, 100000, jnp.int32)
        dst = jax.random.randint(jax.random.fold_in(_gk, 3), (25000,), 0, 100000, jnp.int32)
        _o = jnp.argsort(dst, stable=True)
        src = src[_o]
        dst = dst[_o]
        edge_attr_128 = 2.93046e-05 + 1.00006 * jax.random.normal(jax.random.fold_in(_gk, 12), (25000, 128), jnp.float32)
        edge_attr_4 = jax.random.uniform(jax.random.fold_in(_gk, 13), (25000, 4), jnp.float32, 0.0, 1)
        node_vec = jax.random.uniform(jax.random.fold_in(_gk, 15), (100000,), jnp.float32, 0.0, 31.9963)
        return (x, src, dst, edge_attr_128, edge_attr_4, node_vec)
    x, src, dst, edge_attr_128, edge_attr_4, node_vec = _rec_inputs()

    def _L0_gnn_setup():
        import jax, jax.numpy as jnp
        import numpy as np
        N_NODES = 625
        N_EDGES = 10000
        CH = 64
        DIM = 128
        Z = 2 * CH + DIM
        key = jax.random.key(seed)
        ks = jax.random.split(key, 7)
        x = jax.random.normal(ks[0], (N_NODES, CH), dtype=jnp.float32)
        edge_index = jax.random.randint(ks[1], (2, N_EDGES), 0, N_NODES, dtype=jnp.int32)
        edge_attr = jax.random.normal(ks[2], (N_EDGES, DIM), dtype=jnp.float32)
        W_f = jax.random.normal(ks[3], (Z, CH), dtype=jnp.float32) * (1.0 / np.sqrt(Z))
        b_f = jnp.zeros((CH,), dtype=jnp.float32)
        W_s = jax.random.normal(ks[4], (Z, CH), dtype=jnp.float32) * (1.0 / np.sqrt(Z))
        b_s = jnp.zeros((CH,), dtype=jnp.float32)
        return {'x': x, 'edge_index': edge_index, 'edge_attr': edge_attr, 'W_f': W_f, 'b_f': b_f, 'W_s': W_s, 'b_s': b_s}
    _L0_gnn_all = _L0_gnn_setup()
    _L0_gnn_in = {k: v for k, v in _L0_gnn_all.items() if k in ('W_f', 'b_f', 'W_s', 'b_s')}
    del _L0_gnn_all

    def _L1_gnn_setup():
        import jax, jax.numpy as jnp
        import numpy as np
        N_NODES = 100000
        N_EDGES = 1250000
        D_IN = 64
        H = 8
        HD = 8
        NEG_SLOPE = 0.2
        key = jax.random.key(seed)
        k1, k2, k3, k4, k5 = jax.random.split(key, 5)
        x = jax.random.normal(k1, (N_NODES, D_IN), dtype=jnp.float32)
        edge_indices = jax.random.randint(k2, (2, N_EDGES), 0, N_NODES)
        w_scale = np.sqrt(6.0 / (D_IN + HD)).astype(np.float32)
        a_scale = np.sqrt(6.0 / (2 * HD + 1)).astype(np.float32)
        W = jax.random.uniform(k3, (H * HD, D_IN), jnp.float32, -w_scale, w_scale)
        src_attn = jax.random.uniform(k4, (1, H, HD), jnp.float32, -a_scale, a_scale)
        dst_attn = jax.random.uniform(k5, (1, H, HD), jnp.float32, -a_scale, a_scale)
        return {'x': x, 'edge_indices': edge_indices, 'W': W, 'src_attn': src_attn, 'dst_attn': dst_attn}
    _L1_gnn_all = _L1_gnn_setup()
    _L1_gnn_in = {k: v for k, v in _L1_gnn_all.items() if k in ('W', 'src_attn', 'dst_attn')}
    del _L1_gnn_all

    def _L2_gnn_setup():
        import jax, jax.numpy as jnp
        import numpy as np
        N_NODES = 100000
        N_EDGES = 15625
        IN_FEATS = 64
        OUT_FEATS = 64

        def _gcn_agg(features, src, dst, n_nodes):
            ones = jnp.ones(src.shape[0], dtype=features.dtype)
            deg_out = jax.ops.segment_sum(ones, src, num_segments=n_nodes)
            deg_in = jax.ops.segment_sum(ones, dst, num_segments=n_nodes)
            norm_out = jnp.where(deg_out > 0, jax.lax.rsqrt(jnp.maximum(deg_out, 1.0)), 0.0)
            norm_in = jnp.where(deg_in > 0, jax.lax.rsqrt(jnp.maximum(deg_in, 1.0)), 0.0)
            msg = (features * norm_out[:, None])[src]
            agg = jax.ops.segment_sum(msg, dst, num_segments=n_nodes)
            return agg * norm_in[:, None]
        key = jax.random.key(seed)
        k1, k2, k3, k4 = jax.random.split(key, 4)
        features = jax.random.normal(k1, (N_NODES, IN_FEATS), dtype=jnp.float32)
        src = jax.random.randint(k2, (N_EDGES,), 0, N_NODES, dtype=jnp.int64)
        dst = jax.random.randint(k3, (N_EDGES,), 0, N_NODES, dtype=jnp.int64)
        W = jax.random.normal(k4, (OUT_FEATS, IN_FEATS), dtype=jnp.float32) / np.sqrt(IN_FEATS)
        b = jnp.zeros((OUT_FEATS,), dtype=jnp.float32)
        return {'features': features, 'W': W, 'b': b, 'src': src, 'dst': dst}
    _L2_gnn_all = _L2_gnn_setup()
    _L2_gnn_in = {k: v for k, v in _L2_gnn_all.items() if k in ('W', 'b')}
    del _L2_gnn_all

    def _L3_gnn_setup():
        import jax, jax.numpy as jnp
        import numpy as np
        N = 50000
        E = 12500
        C = 64
        key = jax.random.key(seed)
        ks = jax.random.split(key, 16)
        s = 0.05
        x = jax.random.normal(ks[0], (N, C), jnp.float32)
        edge_attr = jax.random.uniform(ks[1], (E, 4), dtype=jnp.float32)
        edge_index = jax.random.randint(ks[2], (2, E), 0, N)
        deg_hist = jax.random.uniform(ks[3], (N,), dtype=jnp.float32) * 32.0
        W = jax.random.normal(ks[4], (C, C), jnp.float32) * s
        We = jax.random.normal(ks[5], (3, C), jnp.float32) * s
        be = jnp.zeros((C,), jnp.float32)
        Wpre = jax.random.normal(ks[6], (3 * C, C), jnp.float32) * s
        bpre = jnp.zeros((C,), jnp.float32)
        A_S = 4 * 3
        Wpost = jax.random.normal(ks[7], ((A_S + 1) * C, C), jnp.float32) * s
        bpost = jnp.zeros((C,), jnp.float32)
        Wih = jax.random.normal(ks[8], (C, 3 * C), jnp.float32) * s
        bih = jnp.zeros((3 * C,), jnp.float32)
        Whh = jax.random.normal(ks[9], (C, 3 * C), jnp.float32) * s
        bhh = jnp.zeros((3 * C,), jnp.float32)
        return dict(x=x, edge_attr=edge_attr, deg_hist=deg_hist, W=W, We=We, be=be, Wpre=Wpre, bpre=bpre, Wpost=Wpost, bpost=bpost, Wih=Wih, bih=bih, Whh=Whh, bhh=bhh, edge_index=edge_index)
    _L3_gnn_all = _L3_gnn_setup()
    _L3_gnn_in = {k: v for k, v in _L3_gnn_all.items() if k in ('W', 'We', 'be', 'Wpre', 'bpre', 'Wpost', 'bpost', 'Wih', 'bih', 'Whh', 'bhh')}
    del _L3_gnn_all
    return {'x': x, 'src': src, 'dst': dst, 'edge_attr_128': edge_attr_128, 'edge_attr_4': edge_attr_4, 'node_vec': node_vec, 'L0_gnn_W_f': _L0_gnn_in['W_f'], 'L0_gnn_b_f': _L0_gnn_in['b_f'], 'L0_gnn_W_s': _L0_gnn_in['W_s'], 'L0_gnn_b_s': _L0_gnn_in['b_s'], 'L1_gnn_W': _L1_gnn_in['W'], 'L1_gnn_src_attn': _L1_gnn_in['src_attn'], 'L1_gnn_dst_attn': _L1_gnn_in['dst_attn'], 'L2_gnn_W': _L2_gnn_in['W'], 'L2_gnn_b': _L2_gnn_in['b'], 'L3_gnn_W': _L3_gnn_in['W'], 'L3_gnn_We': _L3_gnn_in['We'], 'L3_gnn_be': _L3_gnn_in['be'], 'L3_gnn_Wpre': _L3_gnn_in['Wpre'], 'L3_gnn_bpre': _L3_gnn_in['bpre'], 'L3_gnn_Wpost': _L3_gnn_in['Wpost'], 'L3_gnn_bpost': _L3_gnn_in['bpost'], 'L3_gnn_Wih': _L3_gnn_in['Wih'], 'L3_gnn_bih': _L3_gnn_in['bih'], 'L3_gnn_Whh': _L3_gnn_in['Whh'], 'L3_gnn_bhh': _L3_gnn_in['bhh']}

def reference(x, src, dst, edge_attr_128, edge_attr_4, node_vec, L0_gnn_W_f, L0_gnn_b_f, L0_gnn_W_s, L0_gnn_b_s, L1_gnn_W, L1_gnn_src_attn, L1_gnn_dst_attn, L2_gnn_W, L2_gnn_b, L3_gnn_W, L3_gnn_We, L3_gnn_be, L3_gnn_Wpre, L3_gnn_bpre, L3_gnn_Wpost, L3_gnn_bpost, L3_gnn_Wih, L3_gnn_bih, L3_gnn_Whh, L3_gnn_bhh):
    import jax
    import jax.numpy as jnp

    def _L0_gnn_ref(x, edge_index, edge_attr, W_f, b_f, W_s, b_s):
        import jax, jax.numpy as jnp
        import numpy as np
        N_NODES = 625
        N_EDGES = 10000
        CH = 64
        DIM = 128
        Z = 2 * CH + DIM
        src, dst = (edge_index[0], edge_index[1])
        z = jnp.concatenate([x[dst], x[src], edge_attr], axis=-1)
        gate = jax.nn.sigmoid(z @ W_f + b_f)
        core = jax.nn.softplus(z @ W_s + b_s)
        msg = gate * core
        agg = jax.ops.segment_sum(msg, dst, num_segments=x.shape[0])
        out = x + agg
        return jax.nn.relu(out)

    def _L1_gnn_ref(x, edge_indices, W, src_attn, dst_attn):
        import jax, jax.numpy as jnp
        import numpy as np
        N_NODES = 100000
        N_EDGES = 1250000
        D_IN = 64
        H = 8
        HD = 8
        NEG_SLOPE = 0.2
        n = x.shape[0]
        row, col = (edge_indices[0], edge_indices[1])
        xp = (x @ W.T).reshape(n, H, HD)
        src_score = (xp * src_attn).sum(-1)
        dst_score = (xp * dst_attn).sum(-1)
        e = jax.nn.leaky_relu(src_score[row] + dst_score[col], negative_slope=NEG_SLOPE)
        m = jax.ops.segment_max(e, row, num_segments=n)
        ex = jnp.exp(e - m[row])
        den = jax.ops.segment_sum(ex, row, num_segments=n)
        alpha = ex / den[row]
        vals = xp[col] * alpha[:, :, None]
        out = jax.ops.segment_sum(vals, row, num_segments=n)
        return out.reshape(n, H * HD)

    def _L2_gnn_ref(features, W, b, src, dst):
        import jax, jax.numpy as jnp
        import numpy as np
        N_NODES = 100000
        N_EDGES = 15625
        IN_FEATS = 64
        OUT_FEATS = 64

        def _gcn_agg(features, src, dst, n_nodes):
            ones = jnp.ones(src.shape[0], dtype=features.dtype)
            deg_out = jax.ops.segment_sum(ones, src, num_segments=n_nodes)
            deg_in = jax.ops.segment_sum(ones, dst, num_segments=n_nodes)
            norm_out = jnp.where(deg_out > 0, jax.lax.rsqrt(jnp.maximum(deg_out, 1.0)), 0.0)
            norm_in = jnp.where(deg_in > 0, jax.lax.rsqrt(jnp.maximum(deg_in, 1.0)), 0.0)
            msg = (features * norm_out[:, None])[src]
            agg = jax.ops.segment_sum(msg, dst, num_segments=n_nodes)
            return agg * norm_in[:, None]
        n_nodes = features.shape[0]
        agg = _gcn_agg(features, src, dst, n_nodes)
        conv_h = features - agg
        h = conv_h @ W.T + b
        return jax.nn.relu(h)

    def _L3_gnn_ref(x, edge_attr, deg_hist, W, We, be, Wpre, bpre, Wpost, bpost, Wih, bih, Whh, bhh, edge_index):
        import jax, jax.numpy as jnp
        import numpy as np
        N = 50000
        E = 12500
        C = 64
        n_nodes = x.shape[0]
        m = x @ W
        src, dst = (edge_index[0], edge_index[1])
        ew = edge_attr[:, 3:4]
        ea = edge_attr[:, :3] @ We + be
        xi = ew * m[dst]
        xj = ew * m[src]
        ea = ew * ea
        h = jnp.concatenate([xi, xj, ea], axis=-1) @ Wpre + bpre
        ones = jnp.ones((h.shape[0],), h.dtype)
        cnt = jax.ops.segment_sum(ones, dst, num_segments=n_nodes)
        safe = jnp.maximum(cnt, 1.0)[:, None]
        s1 = jax.ops.segment_sum(h, dst, num_segments=n_nodes)
        s2 = jax.ops.segment_sum(h * h, dst, num_segments=n_nodes)
        mean = s1 / safe
        mean_sq = s2 / safe
        std = jnp.sqrt(jax.nn.relu(mean_sq - mean * mean) + 1e-05)
        has = (cnt > 0)[:, None]
        mn = jnp.where(has, jax.ops.segment_min(h, dst, num_segments=n_nodes), 0.0)
        mx = jnp.where(has, jax.ops.segment_max(h, dst, num_segments=n_nodes), 0.0)
        agg = jnp.concatenate([mean, mn, mx, std], axis=-1)
        deg = jnp.maximum(cnt, 1.0)[:, None]
        avg_log = jnp.mean(jnp.log(deg_hist + 1.0))
        logd = jnp.log(deg + 1.0)
        o1 = agg
        o2 = o1 * (logd / avg_log)
        o3 = o2 * (avg_log / logd)
        out = jnp.concatenate([o1, o2, o3], axis=-1)
        out = jnp.concatenate([m, out], axis=-1) @ Wpost + bpost
        gi = out @ Wih + bih
        gh = x @ Whh + bhh
        ir, iz, i_n = jnp.split(gi, 3, axis=-1)
        hr, hz, h_n = jnp.split(gh, 3, axis=-1)
        r = jax.nn.sigmoid(ir + hr)
        z = jax.nn.sigmoid(iz + hz)
        n = jnp.tanh(i_n + r * h_n)
        return (1.0 - z) * n + z * x
    edge_index = jnp.stack([src, dst])
    x = _layernorm(x + _L0_gnn_ref(x, edge_index, edge_attr_128, L0_gnn_W_f, L0_gnn_b_f, L0_gnn_W_s, L0_gnn_b_s), axis=-1)
    x = _layernorm(x + _L1_gnn_ref(x, edge_index, L1_gnn_W, L1_gnn_src_attn, L1_gnn_dst_attn), axis=-1)
    x = _layernorm(x + _L2_gnn_ref(x, L2_gnn_W, L2_gnn_b, src, dst), axis=-1)
    x = _layernorm(x + _L3_gnn_ref(x, edge_attr_4, node_vec, L3_gnn_W, L3_gnn_We, L3_gnn_be, L3_gnn_Wpre, L3_gnn_bpre, L3_gnn_Wpost, L3_gnn_bpost, L3_gnn_Wih, L3_gnn_bih, L3_gnn_Whh, L3_gnn_bhh, edge_index), axis=-1)
    return x

_drawn_inputs = setup_inputs


def setup_inputs(seed=0):
    import zlib

    import numpy as np

    out = dict(_drawn_inputs(seed))
    spreads = {'L0_gnn_b_f': (0.0, 0.8),
     'L0_gnn_b_s': (0.0, 0.641),
     'L2_gnn_b': (0.0, 0.1),
     'L3_gnn_be': (0.0, 0.8),
     'L3_gnn_bpre': (0.0, 2.0),
     'L3_gnn_bpost': (0.0, 0.505),
     'L3_gnn_bih': (0.0, 0.1),
     'L3_gnn_bhh': (0.0, 0.374)}
    factors = {'edge_attr_4': 8.0, 'L1_gnn_src_attn': 2.831, 'L3_gnn_We': 8.0, 'L3_gnn_Wpre': 6.786}
    for name, (base, spread) in spreads.items():
        noise = np.random.default_rng([zlib.crc32(name.encode()), seed]).standard_normal(out[name].shape)
        drawn = base * np.exp(spread * noise) if base else spread * noise
        out[name] = jnp.asarray(drawn.astype(out[name].dtype))
    for name, factor in factors.items():
        out[name] = (out[name] * factor).astype(out[name].dtype)
    return out
```

```python
from contextlib import ExitStack

import numpy as np

import concourse.bass as bass
from concourse import mybir

F32 = mybir.dt.float32
I32 = mybir.dt.int32
U32 = mybir.dt.uint32
ALU = mybir.AluOpType
ACT = mybir.ActivationFunctionType
AX_X = mybir.AxisListType.X

P = 128
N = 100000
E = 25000
C = 64
HEADS = 8
CH = 512
NCH = -(-E // CH)
NT = 4 * NCH
TW = C + 2
EW = 2 * C + 5
SF = 256
SN = P * SF
SK = 15
SKIP = 1 << 20
BIG = 1.0e30
EPS = 1e-5
MID = N / 2 + 0.5
MARGIN = 255.5
NODES = 1024
ND = -(-N // NODES)
ROWS1 = 11
R1 = N // P // ROWS1
TAIL1 = N - P * R1 * ROWS1


class Count:

    def __init__(self, sem):
        self.sem, self.n = sem, 0

    def tick(self, ins):
        ins.then_inc(self.sem, 1)
        self.n += 1


class Steps:

    def __init__(self, sem, *names):
        self.sem, self.names, self.n, self.next = sem, names, len(names), 0

    def done(self, name):
        assert self.names[self.next % self.n] == name, (name, self.names[self.next % self.n])
        self.next += 1
        return self.sem

    def at(self, c, name):
        return (c + 2) * self.n + self.names.index(name) + 1


def gnn_kernel(nc, x, src, dst, ea128, ea4, node_vec, Wf, bf, Ws, bs, W1, a_src, a_dst, W2, b2,
               W3, We, be, Wpre, bpre, Wpost, bpost, Wih, bih, Whh, bhh,
               k_mats, k_idx, k_sign, out, T, X3, H1, H3, EC, KD, MK):
    with ExitStack() as ctx:
        ctx.enter_context(nc.allow_non_contiguous_dma(reason="small weights, loaded once, transposed"))
        def sb(name, shape, dt=F32):
            return ctx.enter_context(nc.sbuf_tensor(name, shape, dt))

        def sem(name):
            return ctx.enter_context(nc.semaphore(name))

        ps = [ctx.enter_context(nc.psum_tensor(f"ps{i}", [P, 512], F32)) for i in range(8)]

        mats = sb("mats", [P, 5, P])
        ident, center, mean64, headmask, selw = (mats[:, i, :] for i in range(5))
        eps_col = sb("eps_col", [P, 1])
        one_col = sb("one_col", [P, 1])
        ones = sb("ones", [P, CH])
        avgmat = sb("avgmat", [P, P])

        w_fs_z = sb("w_fs_z", [P, P])
        w_fs_e = sb("w_fs_e", [P, P])
        b_fs = sb("b_fs", [P, 1])
        w1_l = sb("w1_l", [C, P])
        w1_r = sb("w1_r", [C, P])
        w1t = sb("w1t", [P, C])
        att = sb("att", [C, 2])
        att_m = sb("att_m", [C, 2, C])
        w_score = sb("w_score", [P, C])
        w2_bd = sb("w2_bd", [P, P])
        w2_neg = sb("w2_neg", [P, P])
        b2_col = sb("b2_col", [P, 1])
        w3t_l = sb("w3t_l", [C, P])
        w3t_r = sb("w3t_r", [C, P])
        wpre2 = sb("wpre2", [C, 3, P])
        wet = sb("wet", [C, 4])
        be_col = sb("be_col", [C, 1])
        bpre_col = sb("bpre_col", [P, 1])
        w_h = sb("w_h", [P, P])
        w_hea = sb("w_hea", [4, P])
        bew_col = sb("bew_col", [P, 1])
        wp_a1 = sb("wp_a1", [P, P])
        wp_a2 = sb("wp_a2", [P, P])
        wu_a1 = sb("wu_a1", [P, P])
        wu_a2 = sb("wu_a2", [P, P])
        wu_f = sb("wu_f", [P, P])
        wpm = sb("wpm", [C, P])
        wu_x = sb("wu_x", [C, P])
        bpost_col = sb("bpost_col", [P, 1])
        w_g1 = sb("w_g1", [P, P])
        w_g2 = sb("w_g2", [P, P])
        wih2 = sb("wih2", [C, 3, P])
        whh2 = sb("whh2", [P, 3 * C])
        brow = sb("brow", [P, 2, 3])
        b_g1 = sb("b_g1", [P, 1])
        wstd = sb("wstd", [C, 3, C])
        nv = sb("nv", [125, N // 125])
        nvs = sb("nvs", [125, 1])
        avg = sb("avg", [P, 1])
        iavg = sb("iavg", [P, 1])
        fac0 = sb("fac0", [C, 8])
        mmt2 = sb("mmt2", [C, P])
        out0 = sb("out0", [C, 1])
        dg = sb("dg", [P, 4, P])
        dg_b = sb("dg_b", [P, 4])

        s_const = sem("s_const")
        s_wload = sem("s_wload")
        s_wzero = sem("s_wzero")
        s_wpe = sem("s_wpe")
        s_wact = sem("s_wact")
        s_wdve = sem("s_wdve")

        (I_PERMD, I_DSTC, I_DSTR, I_DSTH, I_PERMS, I_SRCC, I_SRCH, I_SRCD, I_SRCF) = range(9)
        idx = sb("idx", [P, 9, NT], U32)
        ea4d = sb("ea4d", [P, NT, 4])

        keys = sb("keys", [P, 2, SF], I32)
        kidx = sb("kidx", [P, 2, SF])
        ksign = sb("ksign", [P, SK, SF])
        sx = sb("sx", [P, 2, SF])
        sy = sb("sy", [P, 2, SF])
        sf = [sb(f"sf{i}", [P, 2, SF]) for i in range(6)]
        si = [sb(f"si{i}", [P, 2, SF], I32) for i in range(3)]
        lists = sb("lists", [P, 7, SF])
        edge_col = sb("edge_col", [2, 2])

        s_keyl = sem("s_keyl")
        s_keym = sem("s_keym")
        s_sort = sem("s_sort")
        s_sortt = sem("s_sortt")
        s_ec = sem("s_ec")
        s_kd = sem("s_kd")
        s_kr = sem("s_kr")
        s_mk = sem("s_mk")
        s_lt = sem("s_lt")
        s_idx = sem("s_idx")

        d1x = sb("d1x", [P, R1, C])
        d1r = sb("d1r", [P, R1, C])
        d1o = sb("d1o", [P, R1, TW])
        d1s = sb("d1s", [P, 4, R1])
        s_d1l = sem("s_d1l")
        s_d1o = sem("s_d1o")
        d1_act = Steps(sem("s_d1act"), "relu", "square", "ln", "rstd")
        d1_dve = Steps(sem("s_d1dve"), "y", "sum", "mean", "centered", "sumsq", "norm")

        def rows1(ap, j, tail):
            if tail:
                return ap[P * R1 * ROWS1:N, :].rearrange("(p r) c -> p r c", r=1)
            return ap[0:P * R1 * ROWS1, :].rearrange("(p r) c -> p r c", p=P)[:, bass.ds(j * R1, R1), :]

        gat = sb("gat", [P, 2, 4, 2 * TW])
        pk = sb("pk", [P, 4, P])
        eca = sb("eca", [P, 2, 4, EW])
        gst = sb("gst", [P, 2, 3, 4], U32)
        sst = sb("sst", [P, 2, 4], U32)
        pst = sb("pst", [P, 2, 4], U32)
        dli = sb("dli", [P, 2, 4], I32)
        eas = sb("eas", [P, 2, 4, 4])
        mk = sb("mk", [P, 2, CH + 1])
        ot = sb("ot", [P, 2, 4, TW])
        ot3 = sb("ot3", [P, 2, 4, P])
        z = sb("z", [P, CH])
        ear = sb("ear", [P, CH])
        negm = sb("negm", [P, CH + 1])
        w = [a[:, :, :].rearrange("p r c -> p (r c)")[:, k * CH:(k + 1) * CH] for a in (d1x, d1r) for k in range(8)]
        w += [sb(f"w{i}", [P, CH]) for i in range(16, 18)]
        sc = [sb(f"sc{i}", [P, 2, CH]) for i in range(4)]
        sm = sb("sm", [P, 8])
        s_tick_pool = sem("s_tick_pool")
        s_tick_pe = sem("s_tick_pe")
        s_tick_sp = sem("s_tick_sp")
        zeros = sb("zeros", [P, CH])
        s_x3z = sem("s_x3z")
        sgn_col = sb("sgn_col", [P, 1])
        bsum = sb("bsum", [P, 3])
        s_wd = sem("s_wd")
        s_lists = sem("s_lists")

        def par_sems(name):
            return [sem(f"{name}0"), sem(f"{name}1")]

        def even_odd(total, per):
            return [16 * per * (-(-total // 2)), 16 * per * (total // 2)]

        class Pass:
            def __init__(self, name, pe, act, dve):
                self.gst = par_sems(f"s_{name}_gst")
                self.sst = par_sems(f"s_{name}_sst")
                self.mk = par_sems(f"s_{name}_mk")
                self.gat = par_sems(f"s_{name}_gat")
                self.sca = par_sems(f"s_{name}_sca")
                self.pe = Steps(sem(f"s_{name}_pe"), *pe)
                self.act = Steps(sem(f"s_{name}_act"), *act)
                self.dve = Steps(sem(f"s_{name}_dve"), *dve)

        L0 = Pass("l0", ("z", "ea", "fs", "center", "var", "out"),
                  ("z", "gate", "sabs", "exps", "log", "sq", "ln", "rstd", "out"),
                  ("ea", "meta", "srelu", "core", "msg", "agg",
                   "t", "y", "x1"))
        ec_sem = par_sems("s_l0_ec")
        psg0 = par_sems("s_l0_pst")
        L1 = Pass("l1", ("z", "score", "xp", "out"),
                  ("pack", "z", "negm", "lrelu", "ex", "carry", "lncnt", "norm", "out"),
                  ("e", "mrun", "mseg", "d", "dcar", "carry", "den", "val", "num", "dmax", "rden", "att", "v2",
                   "cnt", "flag"))
        dl_sem = par_sems("s_l1_dst")
        h1_sem = par_sems("s_l1_h1")
        s_l1_c = sem("s_l1_c")
        psg1 = par_sems("s_l1_pst")
        L2 = Pass("l2", ("z", "center", "var", "norm", "h", "out"),
                  ("pack", "z", "sq", "ln", "rstd", "lncnt", "nin", "relu", "out"),
                  ("x2", "cnt", "msg", "agg", "aggn", "y3", "fsel", "srcf"))
        h3_sem = par_sems("s_l2_h3")
        L3 = Pass("l3", ("z", "ea", "center", "var", "h", "ew", "p", "u", "g1", "g2", "center4", "var4", "out"),
                  ("z", "sq", "ln", "rstd", "ea", "negm", "h", "hneg", "lnvar", "std", "logd", "u",
                   "rz", "n", "sq4", "ln4", "rstd4", "out"),
                  ("x3", "cnt", "ha", "hw", "hsq", "s1", "s2", "mx", "rcnt", "mean", "msq", "ms2", "vard", "var",
                   "f2", "rlog", "f3", "fp", "q", "a", "xn", "zxn", "o", "y4", "x4"))
        eal_sem = par_sems("s_l3_ea")

        dn = sb("dn", [P, 2, 8, TW])
        do = sb("do", [P, 2, 8, C])
        dn_sem = par_sems("s_dn_in")
        do_sem = par_sems("s_dn_out")
        D_pe = Steps(sem("s_dn_pe"), "z", "c2", "v2", "h", "c3", "v3", "gr", "gz", "gi", "gh", "c4", "v4", "out")
        D_act = Steps(sem("s_dn_act"), "pack", "z", "sq2", "ln2", "r2", "relu", "sq3", "ln3", "r3", "r", "zg", "n",
                      "sq4", "ln4", "r4", "out")
        D_dve = Steps(sem("s_dn_dve"), "x2", "y3", "x3", "q", "a",
                      "xn", "zxn", "o", "y4", "x4")

        def dense_rows(d, ap, last):
            if last:
                return ap[(ND - 1) * NODES:N, :].rearrange("(p r) c -> p r c", r=8)
            return ap[bass.ds(d * NODES, NODES), :].rearrange("(p r) c -> p r c", r=8)

        LASTP = (N - (ND - 1) * NODES) // 8

        src_f = src.bitcast(F32).rearrange("(e a) -> e a", a=1)
        dst_r = dst.rearrange("(e a) -> e a", a=1)
        full, rest = E // SF, E % SF

        def col(ap):
            return ap.rearrange("(a b) -> a b", b=1)

        wloads = [
            (mats[:, :, :], k_mats),
            (w_fs_z[:, 0:C], Wf[0:P, :]), (w_fs_z[:, C:P], Ws[0:P, :]),
            (w_fs_e[:, 0:C], Wf[P:2 * P, :]), (w_fs_e[:, C:P], Ws[P:2 * P, :]),
            (b_fs[0:C, :], col(bf)), (b_fs[C:P, :], col(bs)),
            (w1_l[:, 0:C], W1), (w1_r[:, C:P], W1),
            (w1t[C:P, :], W1.rearrange("a b -> b a")),
            (att[:, 0:1], a_src.rearrange("a h d -> (h d) a")), (att[:, 1:2], a_dst.rearrange("a h d -> (h d) a")),
            (w2_bd[0:C, 0:C], W2.rearrange("a b -> b a")), (w2_bd[C:P, C:P], W2.rearrange("a b -> b a")),
            (b2_col[0:C, :], col(b2)), (b2_col[C:P, :], col(b2)),
            (w3t_l[:, 0:C], W3.rearrange("a b -> b a")), (w3t_r[:, C:P], W3.rearrange("a b -> b a")),
            (wpre2[:, :, 0:C], Wpre.rearrange("(k p) c -> p k c", k=3)),
            (wpre2[:, :, C:P], Wpre.rearrange("(k p) c -> p k c", k=3)),
            (wet[:, 0:3], We.rearrange("a b -> b a")),
            (be_col[:, :], col(be)), (bpre_col[0:C, :], col(bpre)), (bpre_col[C:P, :], col(bpre)),
            (wpm[:, C:P], Wpost[0:C, :]),
            (bpost_col[0:C, :], col(bpost)), (bpost_col[C:P, :], col(bpost)),
            (whh2[0:C, :], Whh), (whh2[C:P, :], Whh),
            (w_g1[0:C, 0:C], Whh[:, C:2 * C]), (w_g1[0:C, C:P], Whh[:, 0:C]),
            (w_g1[C:P, 0:C], Wih[:, C:2 * C]), (w_g1[C:P, C:P], Wih[:, 0:C]),
            (w_g2[0:C, C:P], Whh[:, 2 * C:3 * C]), (w_g2[C:P, 0:C], Wih[:, 2 * C:3 * C]),
            (wih2[:, :, 0:C], Wih.rearrange("p (g c) -> p g c", g=3)),
            (wih2[:, :, C:P], Wih.rearrange("p (g c) -> p g c", g=3)),
            (nv[:, :], node_vec.rearrange("(p a) -> p a", p=125)),
        ]
        post = {(s, k): C + 4 * C * s + C * k for s in range(3) for k in range(4)}
        MEAN, MIN, MAX, STD = range(4)
        for half, a1, a2 in ((0, MEAN, MIN), (C, STD, MAX)):
            for s, cols in ((1, slice(0, C)), (2, slice(C, P))):
                wloads.append((wp_a1[half:half + C, cols], Wpost[post[s, a1]:post[s, a1] + C, :]))
                wloads.append((wp_a2[half:half + C, cols], Wpost[post[s, a2]:post[s, a2] + C, :]))
            wloads.append((wu_a1[half:half + C, C:P], Wpost[post[0, a1]:post[0, a1] + C, :]))
            wloads.append((wu_a2[half:half + C, C:P], Wpost[post[0, a2]:post[0, a2] + C, :]))
        for s in range(3):
            wloads.append((wstd[:, s, :], Wpost[post[s, STD]:post[s, STD] + C, :]))
        for h in (0, C):
            for g in range(3):
                wloads.append((brow[h:h + C, 0, g:g + 1], col(bih[g * C:(g + 1) * C])))
                wloads.append((brow[h:h + C, 1, g:g + 1], col(bhh[g * C:(g + 1) * C])))
        NW = 16 * len(wloads)

        zeroed = [w1_l, w1_r, w2_bd, w2_neg, w3t_l, w3t_r, wet, wu_a1, wu_a2, wu_f, wpm, w_g2, dg]

        turn_plan = []

        block = ctx.enter_context(nc.Block())

        tot = even_odd(NCH, 4)

        def again(wait, s, count, i):
            if not (isinstance(i, int) and i == 0):
                wait(s, count * i)

        def pairs_of_chunks(eng, body, lo=0, hi=NCH, peel=2):
            while lo < peel:
                body(lo, lo % 2, lo // 2)
                lo += 1
            n = (hi - lo) // 2
            with eng.Fori(0, n) as i:
                body(2 * i + lo, lo % 2, i + lo // 2)
                body(2 * i + lo + 1, (lo + 1) % 2, i + (lo + 1) // 2)
            if (hi - lo) % 2:
                body(hi - 1, (hi - 1) % 2, (hi - 1) // 2)

        @block.sync
        def _(sp):
            def hold(s, v):
                sp.wait_ge(s, v)
                sp.sem_inc(s_tick_sp, 1)

            def after(steps, c, name):
                hold(steps.sem, steps.at(c, name))

            sp.wait_ge(s_keym, 1)
            for s, a in ((0, dst), (1, src)):
                sp.dma_start(keys[0:full, s, :], a[0:full * SF].rearrange("(p f) -> p f", f=SF)).then_inc(s_keyl, 16)
                sp.dma_start(keys[full:full + 1, s, 0:rest], a[full * SF:E].rearrange("(p f) -> p f", p=1)).then_inc(s_keyl, 16)
            sp.dma_start(kidx[:, :, :], k_idx).then_inc(s_keyl, 16)
            sp.dma_start(ksign[:, :, :], k_sign).then_inc(s_keyl, 16)
            sp.wait_ge(s_wzero, len(zeroed))
            for d, s in wloads:
                sp.dma_start(d, s).then_inc(s_wload, 16)
            sp.dma_start(EC[:, 0:2 * C], ea128).then_inc(s_ec, 16)
            sp.dma_start(EC[:, 2 * C:2 * C + 4], ea4).then_inc(s_ec, 16)
            sp.dma_start(EC[:, 2 * C + 4:EW], src_f).then_inc(s_ec, 16)

            sp.wait_ge(s_const, 3)
            per = N // P * C
            x3_rows = X3[0:P * (N // P), :].rearrange("(p r) c -> p (r c)", p=P)
            sp.dma_start(x3_rows[:, 0:per // CH * CH].rearrange("p (a b) -> p a b", b=CH),
                         zeros[:, :].unsqueeze(1).broadcast_to([P, per // CH, CH])).then_inc(s_x3z, 16)
            sp.dma_start(x3_rows[:, per // CH * CH:per], zeros[:, 0:per % CH]).then_inc(s_x3z, 16)
            sp.dma_start(X3[P * (N // P):N, :], zeros[0:N % P, 0:C]).then_inc(s_x3z, 16)

            with sp.Fori(0, ROWS1) as j:
                after(d1_dve, j - 1, "y")
                sp.dma_start(d1x[:, :, :], rows1(x, j, False)).then_inc(s_d1l, 16)
                after(d1_dve, j, "norm")
                sp.dma_start(rows1(T, j, False), d1o[:, :, :]).then_inc(s_d1o, 16)
            sp.wait_ge(s_d1o, 16 * ROWS1)
            sp.dma_start(d1x[0:TAIL1, 0:1, :], rows1(x, 0, True)).then_inc(s_d1l, 16)
            after(d1_dve, ROWS1, "norm")
            sp.dma_start(rows1(T, 0, True), d1o[0:TAIL1, 0:1, :]).then_inc(s_d1o, 16)
            sp.wait_ge(s_d1o, 16 * (ROWS1 + 1))

            sp.wait_ge(s_kd, 1)
            for s in range(2):
                sp.dma_start(KD[s, 1:SN + 1].rearrange("(p f) -> p f", p=P), sf[0][:, s, :]).then_inc(s_kr, 16)
                sp.dma_start(KD[s:s + 1, 0:1], edge_col[0:1, 0:1]).then_inc(s_kr, 16)
                sp.dma_start(KD[s:s + 1, SN + 1:SN + 2], edge_col[0:1, 1:2]).then_inc(s_kr, 16)
            sp.wait_ge(s_kr, 6 * 16)
            for s in range(2):
                sp.dma_start(sf[1][:, s, :], KD[s, 0:SN].rearrange("(p f) -> p f", p=P)).then_inc(s_kr, 16)
                sp.dma_start(sf[2][:, s, :], KD[s, 2:SN + 2].rearrange("(p f) -> p f", p=P)).then_inc(s_kr, 16)
            sp.wait_ge(s_kd, 2)
            for s in range(2):
                sp.dma_start(MK[s, 0:SN].rearrange("(p f) -> p f", p=P), sf[3][:, s, :]).then_inc(s_mk, 16)
            sp.wait_ge(s_mk, 32)
            sp.wait_ge(s_idx, 7)

            def stage(tile, par, row, c, done):
                sp.dma_start(tile, idx[:, row, bass.ds(c * 4, 4)]).then_inc(done[par], 16)

            def heads(L, row, c, par, i):
                again(hold, L.sca[par], 64, i)
                stage(sst[:, par, :], par, row, c, L.sst)

            def load_mask(L, par, s, c):
                sp.dma_start(mk[:, par, 0:CH], MK[s, bass.ds(c * CH, CH)].partition_broadcast(P)).then_inc(L.mk[par], 16)

            def l0(c, par, i):
                after(L0.pe, c - 2, "ea")
                after(L0.dve, c - 2, "agg")
                stage(pst[:, par, :], par, I_PERMD, c, psg0)
                stage(gst[:, par, 0, :], par, I_DSTC, c, L0.gst)
                load_mask(L0, par, 0, c)
            l0(0, 0, 0)
            l0(1, 1, 0)

            def l0_on(c, par, i):
                l0(c, par, i)
                heads(L0, I_DSTH, c - 2, par, i - 1)
            pairs_of_chunks(sp, l0_on, 2, peel=4)
            heads(L0, I_DSTH, NCH - 2, 1, (NCH - 2) // 2)
            heads(L0, I_DSTH, NCH - 1, 0, (NCH - 1) // 2)
            for par in range(2):
                sp.wait_ge(L0.sca[par], tot[par])

            def l1(c, par, i):
                after(L1.pe, c - 2, "z")
                after(L1.dve, c - 2, "cnt")
                stage(pst[:, par, :], par, I_PERMS, c, psg1)
                stage(gst[:, par, 0, :], par, I_SRCC, c, L1.gst)
                load_mask(L1, par, 1, c)

            def l1_out(c, par, i):
                after(L1.act, c, "out")
                after(L1.dve, c, "flag")
                sp.dma_start(H1[bass.ds(c * P, P), :].rearrange("p (t k) -> p t k", t=4), ot[:, par, :, :]).then_inc(h1_sem[par], 16)

            def l1_on(c, par, i):
                l1(c, par, i)
                l1_out(c - 1, 1 - par, 0)
            l1(0, 0, 0)
            pairs_of_chunks(sp, l1_on, 1)
            l1_out(NCH - 1, 0, 0)
            for par in range(2):
                sp.wait_ge(h1_sem[par], even_odd(NCH, 1)[par])

            def l1_scatter(c, par, i):
                again(hold, L1.sca[par], 64, i)
                sp.dma_start(ot[:, par, :, :], H1[bass.ds(c * P, P), :].rearrange("p (t k) -> p t k", t=4)).then_inc(L1.sst[par], 16)
                stage(sst[:, par, :], par, I_SRCH, c, L1.sst)
            pairs_of_chunks(sp, l1_scatter)
            for par in range(2):
                sp.wait_ge(L1.sca[par], tot[par])

            def dense(d, par, last=False):
                after(D_act, d - 2, "pack")
                n = LASTP if last else P
                sp.dma_start(dn[0:n, par, :, :], dense_rows(d, T, last)).then_inc(dn_sem[par], 16)

            def dense_out(d, par, last=False):
                after(D_act, d, "out")
                n = LASTP if last else P
                sp.dma_start(dense_rows(d, out, last), do[0:n, par, :, :]).then_inc(do_sem[par], 16)

            def dense_on(d, par, i):
                dense(d, par)
                dense_out(d - 1, 1 - par)
            dense(0, 0)
            pairs_of_chunks(sp, dense_on, 1, ND - 1)
            dense(ND - 1, 1, True)
            dense_out(ND - 2, 0)
            dense_out(ND - 1, 1, True)
            for par in range(2):
                sp.wait_ge(do_sem[par], 16 * (ND // 2))

            def l2(c, par, i):
                after(L2.pe, c - 2, "norm")
                after(L2.dve, c - 2, "srcf")
                stage(gst[:, par, 0, :], par, I_DSTC, c, L2.gst)
                stage(gst[:, par, 1, :], par, I_SRCD, c, L2.gst)
                load_mask(L2, par, 0, c)

            def l2_out(c, par):
                after(L2.act, c, "out")
                sp.dma_start(H3[bass.ds(c * P, P), :].rearrange("p (t k) -> p t k", t=4), ot3[:, par, :, C:P]).then_inc(h3_sem[par], 16)

            def l2_on(c, par, i):
                l2(c, par, i)
                heads(L2, I_DSTH, c - 1, 1 - par, i - 1 + par)
                l2_out(c - 1, 1 - par)
            l2(0, 0, 0)
            pairs_of_chunks(sp, l2_on, 1, peel=4)
            heads(L2, I_DSTH, NCH - 1, 0, (NCH - 1) // 2)
            l2_out(NCH - 1, 0)
            for par in range(2):
                sp.wait_ge(h3_sem[par], even_odd(NCH, 1)[par])
                sp.wait_ge(L2.sca[par], tot[par])
            after(L2.dve, NCH - 1, "srcf")

            def l3(c, par, i):
                after(L3.pe, c - 2, "ea")
                after(L3.dve, c - 2, "mx")
                sp.dma_start(gat[:, par, :, C:P], H3[bass.ds(c * P, P), :].rearrange("p (t k) -> p t k", t=4)).then_inc(L3.gst[par], 16)
                stage(gst[:, par, 0, :], par, I_DSTR, c, L3.gst)
                stage(gst[:, par, 1, :], par, I_SRCF, c, L3.gst)
                sp.dma_start(eas[:, par, :, :], ea4d[:, bass.ds(c * 4, 4), :]).then_inc(eal_sem[par], 16)
                load_mask(L3, par, 0, c)
            def l3_on(c, par, i):
                l3(c, par, i)
                heads(L3, I_DSTH, c - 1, 1 - par, i - 1 + par)
            l3(0, 0, 0)
            pairs_of_chunks(sp, l3_on, 1, peel=4)
            heads(L3, I_DSTH, NCH - 1, 0, (NCH - 1) // 2)
            for par in range(2):
                sp.wait_ge(L3.sca[par], tot[par])

        @block.gpsimd
        def _(pool):
            for a in zeroed:
                pool.memset(a[(slice(None),) * len(a.shape)], 0.0).then_inc(s_wzero, 1)
            def hold(s, v):
                pool.wait_ge(s, v)
                pool.sem_inc(s_tick_pool, 1)

            def hold_after(steps, c, name):
                hold(steps.sem, steps.at(c, name))

            node_bound = pool.to_reg(N - 1)

            def gather(dest, table, index, done):
                pool.indirect_dma_start(out=dest, out_offset=None, in_=table,
                                        in_offset=bass.IndirectOffsetOnAxis(ap=index, axis=0),
                                        bounds_check=node_bound, oob_is_err=False).then_inc(done, 16)

            def scatter(table, index, source, done):
                pool.indirect_dma_start(out=table, out_offset=bass.IndirectOffsetOnAxis(ap=index, axis=0),
                                        in_=source, in_offset=None,
                                        bounds_check=node_bound, oob_is_err=False).then_inc(done, 16)

            pool.wait_ge(s_ec, 48)

            def edge_rows(c, par, i):
                hold(psg0[par], 16 * (i + 1))
                hold_after(L0.pe, c - 2, "ea")
                hold_after(L0.dve, c - 2, "meta")
                for t in range(4):
                    gather(eca[:, par, t, :], EC, pst[:, par, t:t + 1], ec_sem[par])

            def gathers0(c, par, i):
                hold(L0.gst[par], 16 * (i + 1))
                hold(ec_sem[par], 64 * (i + 1))
                hold_after(L0.pe, c - 2, "z")
                for t in range(4):
                    gather(gat[:, par, t, 0:C], x, gst[:, par, 0, t:t + 1], L0.gat[par])
                    gather(gat[:, par, t, C:P], x, eca[:, par, t, EW - 1:EW].bitcast(U32), L0.gat[par])

            def scatters0(c, par, i):
                hold_after(L0.act, c, "out")
                hold(L0.sst[par], 16 * (i + 1))
                for t in range(4):
                    scatter(T, sst[:, par, t:t + 1], ot[:, par, t, :], L0.sca[par])

            edge_rows(0, 0, 0)
            edge_rows(1, 1, 0)
            gathers0(0, 0, 0)
            edge_rows(2, 0, 1)
            gathers0(1, 1, 0)
            pool.wait_ge(s_d1o, 16 * (ROWS1 + 1))
            with pool.Fori(0, (NCH - 3) // 2) as i:
                edge_rows(2 * i + 3, 1, i + 1)
                gathers0(2 * i + 2, 0, i + 1)
                scatters0(2 * i, 0, i)
                edge_rows(2 * i + 4, 0, i + 2)
                gathers0(2 * i + 3, 1, i + 1)
                scatters0(2 * i + 1, 1, i)
            gathers0(NCH - 1, 0, (NCH - 1) // 2)
            scatters0(NCH - 3, 0, (NCH - 3) // 2)
            scatters0(NCH - 2, 1, (NCH - 3) // 2)
            scatters0(NCH - 1, 0, (NCH - 1) // 2)
            for par in range(2):
                pool.wait_ge(L0.sca[par], tot[par])

            def dst_rows(c, par, i):
                hold(psg1[par], 16 * (i + 1))
                again(hold, L1.gat[par], 128, i)
                for t in range(4):
                    gather(dli[:, par, t:t + 1], dst_r, pst[:, par, t:t + 1], dl_sem[par])

            def gathers1(c, par, i):
                hold(L1.gst[par], 16 * (i + 1))
                hold(dl_sem[par], 64 * (i + 1))
                hold_after(L1.act, c - 2, "pack")
                hold_after(L1.dve, c - 2, "flag")
                for t in range(4):
                    gather(gat[:, par, t, 0:TW], T, gst[:, par, 0, t:t + 1], L1.gat[par])
                    gather(gat[:, par, t, TW:2 * TW], T, dli[:, par, t:t + 1].bitcast(U32), L1.gat[par])

            def gathers1_on(c, par, i):
                dst_rows(c + 1, 1 - par, i + par)
                gathers1(c, par, i)
            dst_rows(0, 0, 0)
            pairs_of_chunks(pool, gathers1_on, 0, NCH - 1)
            gathers1(NCH - 1, 0, (NCH - 1) // 2)

            def scatters1(c, par, i):
                hold(L1.sst[par], 32 * (i + 1))
                for t in range(4):
                    scatter(T, sst[:, par, t:t + 1], ot[:, par, t, :], L1.sca[par])
            pairs_of_chunks(pool, scatters1)
            for par in range(2):
                pool.wait_ge(L1.sca[par], tot[par])

            def run(gathers, scatters):
                gathers(0, 0, 0)
                gathers(1, 1, 0)
                with pool.Fori(0, (NCH - 3) // 2) as i:
                    for par in range(2):
                        gathers(2 * i + 2 + par, par, i + 1)
                        scatters(2 * i + par, par, i)
                gathers(NCH - 1, 0, (NCH - 1) // 2)
                scatters(NCH - 3, 0, (NCH - 3) // 2)
                scatters(NCH - 2, 1, (NCH - 3) // 2)
                scatters(NCH - 1, 0, (NCH - 1) // 2)

            def gathers2(c, par, i):
                hold(L2.gst[par], 32 * (i + 1))
                hold_after(L2.act, c - 2, "pack")
                hold_after(L2.pe, c - 2, "norm")
                hold_after(L2.dve, c - 2, "srcf")
                for t in range(4):
                    gather(gat[:, par, t, 0:TW], T, gst[:, par, 0, t:t + 1], L2.gat[par])
                    gather(gat[:, par, t, TW:2 * TW], T, gst[:, par, 1, t:t + 1], L2.gat[par])

            def scatters2(c, par, i):
                hold_after(L2.act, c, "out")
                hold(L2.sst[par], 16 * (i + 1))
                for t in range(4):
                    scatter(X3, sst[:, par, t:t + 1], ot3[:, par, t, 0:C], L2.sca[par])
            pool.wait_ge(s_x3z, 48)
            run(gathers2, scatters2)
            for par in range(2):
                pool.wait_ge(L2.sca[par], tot[par])

            for par in range(2):
                pool.wait_ge(do_sem[par], 16 * (ND // 2))

            def gathers3(c, par, i):
                hold(L3.gst[par], 48 * (i + 1))
                hold_after(L3.pe, c - 2, "z")
                for t in range(4):
                    gather(gat[:, par, t, 0:C], X3, gst[:, par, 0, t:t + 1], L3.gat[par])
                    gather(gat[:, par, t, C:P], X3, gst[:, par, 1, t:t + 1], L3.gat[par])

            def scatters3(c, par, i):
                hold_after(L3.act, c, "out")
                hold(L3.sst[par], 16 * (i + 1))
                for t in range(4):
                    scatter(out, sst[:, par, t:t + 1], ot3[:, par, t, 0:C], L3.sca[par])
            run(gathers3, scatters3)
            for par in range(2):
                pool.wait_ge(L3.sca[par], tot[par])

        blk = [slice(128 * t, 128 * (t + 1)) for t in range(4)]

        @block.vector
        def _(dve):
            H = slice(0, C)
            U = slice(C, P)

            def after_(steps, c, name):
                dve.wait_ge(steps.sem, steps.at(c, name))

            def tt(done, out_, a, b, op):
                dve.tensor_tensor(out_, a, b, op).then_inc(done, 1)

            def ts(done, out_, a, s1, s2, op0, op1=None):
                if op1 is None:
                    dve.tensor_scalar(out_, a, s1, None, op0).then_inc(done, 1)
                else:
                    dve.tensor_scalar(out_, a, s1, s2, op0, op1).then_inc(done, 1)

            def stt(done, out_, a, s, b, op0, op1):
                dve.scalar_tensor_tensor(out=out_, in0=a, scalar=s, in1=b, op0=op0, op1=op1).then_inc(done, 1)

            def scan(done, out_, d0, d1, initial, op0, op1):
                dve.tensor_tensor_scan(out=out_, data0=d0, data1=d1, initial=initial, op0=op0, op1=op1).then_inc(done, 1)

            for S in (d1_dve, L0.dve, L1.dve, L2.dve, L3.dve, D_dve):
                dve.sem_inc(S.sem, 2 * S.n)

            dve.memset(keys[:, :, :], N).then_inc(s_keym, 1)
            dve.memset(eps_col[:, :], EPS).then_inc(s_const, 1)
            dve.memset(one_col[:, :], 1.0).then_inc(s_const, 1)
            dve.memset(sgn_col[0:C, :], -1.0)
            dve.memset(sgn_col[C:P, :], 1.0)
            for a in (gat, ot, ot3, dn):
                dve.memset(a[:, :, :, :], 0.0)
            dve.memset(ones[:, :], 1.0)
            dve.memset(zeros[:, :], 0.0)
            for a in sc:
                dve.memset(a[:, :, :], 0.0)
            dve.memset(negm[:, CH:CH + 1], 0.0)
            dve.memset(edge_col[0:1, 0:1], -1.0)
            dve.memset(edge_col[0:1, 1:2], -2.0)
            dve.memset(d1o[:, :, C:TW], 0.0).then_inc(s_const, 1)

            setup = Count(s_wd)
            dve.wait_ge(s_wload, NW)
            dve.wait_ge(s_const, 3)
            setup.tick(dve.memset(ot[:, :, :, TW - 1:TW], 1.0))
            for k in range(2):
                setup.tick(dve.tensor_scalar(att_m[:, k, :], headmask[0:C, 0:C], att[:, k:k + 1], None, ALU.mult))
            dve.memset(avgmat[:, :], 1.0 / N).then_inc(s_wdve, 1)
            dve.wait_ge(s_wact, 1)
            dve.reduce_sum(nvs[:, :], nv[:, :], AX_X).then_inc(s_wdve, 1)
            dve.wait_ge(s_wd, setup.n)
            dve.tensor_scalar(w2_neg[C:P, 0:C], w2_bd[C:P, C:P], -1.0, None, ALU.mult).then_inc(s_wdve, 1)
            for a in (wp_a2[0:C, :], wu_a2[0:C, C:P]):
                setup.tick(dve.tensor_scalar(a, a, -1.0, None, ALU.mult))
            for h in (0, C):
                setup.tick(dve.tensor_copy(wu_f[h:h + C, C:P], ident[h:h + C, h:h + C]))
            setup.tick(dve.tensor_tensor(bsum[:, :], brow[:, 0, :], brow[:, 1, :], ALU.add))
            dve.wait_ge(s_wd, setup.n)
            setup.tick(dve.tensor_copy(b_g1[0:C, :], bsum[0:C, 1:2]))
            setup.tick(dve.tensor_copy(b_g1[C:P, :], bsum[C:P, 0:1]))
            dve.wait_ge(s_wpe, 1)
            setup.tick(dve.tensor_copy(w_score[:, :], ps[0][:, 0:C]))
            setup.tick(dve.tensor_copy(w_h[:, :], ps[1][:, 0:P]))
            setup.tick(dve.tensor_copy(w_hea[:, :], ps[2][0:4, 0:P]))
            setup.tick(dve.tensor_copy(bew_col[:, :], ps[2][:, 256:257]))
            setup.tick(dve.tensor_copy(wu_x[:, :], ps[3][0:C, 0:P]))
            setup.tick(dve.tensor_copy(avg[:, :], ps[4][:, 0:1]))
            setup.tick(dve.reciprocal(iavg[:, :], ps[4][:, 0:1]))
            dve.wait_ge(s_wact, 4)
            dve.wait_ge(s_wd, setup.n)
            setup.tick(dve.tensor_scalar(fac0[:, 2:3], fac0[:, 1:2], iavg[0:C, :], None, ALU.mult))
            setup.tick(dve.reciprocal(fac0[:, 3:4], fac0[:, 1:2]))
            dve.wait_ge(s_wd, setup.n)
            setup.tick(dve.tensor_scalar(fac0[:, 5:6], fac0[:, 2:3], fac0[:, 4:5], None, ALU.mult))
            setup.tick(dve.tensor_scalar(fac0[:, 7:8], fac0[:, 3:4], avg[0:C, :], None, ALU.mult))
            dve.wait_ge(s_wd, setup.n)
            dve.tensor_scalar(fac0[:, 6:7], fac0[:, 7:8], fac0[:, 5:6], None, ALU.mult).then_inc(s_wdve, 1)
            setup.tick(dve.tensor_copy(mmt2[:, 0:C], ps[3][0:C, 256:256 + C]))
            setup.tick(dve.tensor_copy(mmt2[:, C:P], ps[3][0:C, 256:256 + C]))
            dve.wait_ge(s_wd, setup.n)
            dve.wait_ge(s_wpe, 2)
            dve.tensor_tensor(out0[:, :], ps[5][0:C, 0:1], bpost_col[0:C, :], ALU.add).then_inc(s_wdve, 1)
            dve.wait_ge(s_wpe, 3)
            for g in range(2):
                setup.tick(dve.tensor_scalar(dg_b[:, g:g + 1], ps[6][:, 8 * g:8 * g + 1], bsum[:, g:g + 1], None, ALU.add))
            setup.tick(dve.tensor_scalar(dg_b[:, 2:3], ps[6][:, 16:17], brow[:, 0, 2:3], None, ALU.add))
            setup.tick(dve.tensor_copy(dg_b[:, 3:4], brow[:, 1, 2:3]))
            for h in (0, C):
                r = slice(h, h + C)
                for g in range(2):
                    setup.tick(dve.tensor_tensor(dg[r, g, r], ps[7][r, g * C:(g + 1) * C], whh2[r, g * C:(g + 1) * C], ALU.add))
                setup.tick(dve.tensor_copy(dg[r, 2, r], ps[7][r, 2 * C:3 * C]))
                setup.tick(dve.tensor_copy(dg[r, 3, r], whh2[r, 2 * C:3 * C]))
            dve.wait_ge(s_wd, setup.n)

            def dense1(j, r=R1, n=P):
                o = d1o[0:n, 0:r, 0:C]
                dve.wait_ge(d1_act.sem, d1_act.at(j, "relu"))
                again(dve.wait_ge, s_d1o, 16, j)
                tt(d1_dve.done("y"), o, d1x[0:n, 0:r, :], d1r[0:n, 0:r, :], ALU.add)
                after_(d1_dve, j, "y")
                dve.reduce_sum(d1s[0:n, 0, 0:r], o, AX_X).then_inc(d1_dve.done("sum"), 1)
                after_(d1_dve, j, "sum")
                ts(d1_dve.done("mean"), d1s[0:n, 0, 0:r], d1s[0:n, 0, 0:r], 1.0 / C, None, ALU.mult)
                after_(d1_dve, j, "mean")
                tt(d1_dve.done("centered"), o, o, d1s[0:n, 0, 0:r].unsqueeze(2).broadcast_to([n, r, C]), ALU.subtract)
                after_(d1_act, j, "square")
                dve.reduce_sum(d1s[0:n, 1, 0:r], d1r[0:n, 0:r, :], AX_X).then_inc(d1_dve.done("sumsq"), 1)
                after_(d1_act, j, "rstd")
                tt(d1_dve.done("norm"), o, o, d1s[0:n, 3, 0:r].unsqueeze(2).broadcast_to([n, r, C]), ALU.mult)
            dense1(0)
            with dve.Fori(1, ROWS1) as j:
                dense1(j)
            dense1(ROWS1, 1, TAIL1)

            cnt_ = Count(s_sort)

            def go(ins):
                cnt_.tick(ins)
                dve.wait_ge(s_sort, cnt_.n)

            dve.wait_ge(s_keyl, 96)
            f = [a[:, :, :] for a in sf]
            i_ = [a[:, :, :] for a in si]
            go(dve.tensor_copy(f[0], keys[:, :, :]))
            go(dve.tensor_scalar(f[1], f[0], MID, None, ALU.subtract))
            go(dve.tensor_scalar(f[2], f[0], MID, None, ALU.is_lt))
            go(dve.scalar_tensor_tensor(out=f[5], in0=f[1], scalar=-1.0, in1=f[1], op0=ALU.mult, op1=ALU.max))
            go(dve.tensor_scalar(i_[0], f[5], MARGIN, None, ALU.add))
            go(dve.tensor_scalar(f[3], kidx[:, :, :], -2.0, float(SN - 1), ALU.mult, ALU.add))
            go(dve.tensor_tensor(f[4], f[3], f[2], ALU.mult))
            go(dve.tensor_tensor(i_[1], f[4], kidx[:, :, :], ALU.add))
            go(dve.tensor_copy(i_[2], f[2]))
            go(dve.tensor_scalar(i_[0], i_[0], SK, None, ALU.logical_shift_left))
            go(dve.tensor_scalar(i_[2], i_[2], 31, None, ALU.logical_shift_left))
            go(dve.tensor_tensor(i_[0], i_[0], i_[1], ALU.bitwise_or))
            go(dve.tensor_tensor(sx[:, :, :].bitcast(I32), i_[0], i_[2], ALU.bitwise_or))
            cur, oth = sx, sy
            turns = 0

            def compare(view, d):
                nonlocal cur, oth
                a, b = view(cur, d), view(oth, d)
                cnt_.tick(dve.tensor_tensor(b[:, :, 0, :], a[:, :, 0, :], a[:, :, 1, :], ALU.min))
                go(dve.tensor_tensor(b[:, :, 1, :], a[:, :, 0, :], a[:, :, 1, :], ALU.max))
                cur, oth = oth, cur

            def view(a, d):
                return a[:, :, :].rearrange("p s (n two d) -> p (s n) two d", two=2, d=d)

            def view_t(a, d):
                return a[:, :, :].rearrange("p s (h n two d) -> p (s h n) two d", h=2, two=2, d=d)

            def turn():
                nonlocal cur, oth, turns
                turn_plan.append((cur, cnt_.n))
                turns += 1
                dve.wait_ge(s_sortt, turns)
                go(dve.tensor_copy(oth[:, :, :].rearrange("p s f -> p (s f)"), ps[0][:, :]))
                cur, oth = oth, cur

            for k in range(1, SK + 1):
                cnt_.tick(dve.tensor_tensor(oth[:, 0, :], cur[:, 0, :], ksign[:, k - 1, :], ALU.mult))
                go(dve.tensor_tensor(oth[:, 1, :], cur[:, 1, :], ksign[:, k - 1, :], ALU.mult))
                cur, oth = oth, cur
                if k > 8:
                    turn()
                    for b in range(k - 9, -1, -1):
                        compare(view_t, 1 << b)
                    turn()
                for b in range(min(k, 8) - 1, -1, -1):
                    compare(view, 1 << b)

            bits = cur[:, :, :].bitcast(I32)
            go(dve.tensor_scalar(i_[0], bits, SK, 0xFFFF, ALU.logical_shift_right, ALU.bitwise_and))
            go(dve.tensor_scalar(i_[1], bits, SN - 1, None, ALU.bitwise_and))
            go(dve.tensor_scalar(i_[2], bits, 31, 1, ALU.logical_shift_right, ALU.bitwise_and))
            go(dve.tensor_scalar(f[1], i_[0], MARGIN, None, ALU.subtract))
            go(dve.tensor_copy(f[2], i_[2]))
            go(dve.tensor_scalar(f[3], f[2], -2.0, 1.0, ALU.mult, ALU.add))
            go(dve.tensor_tensor(f[4], f[1], f[3], ALU.mult))
            go(dve.tensor_copy(f[5], i_[1]))
            go(dve.tensor_scalar(f[3], f[5], -2.0, float(SN - 1), ALU.mult, ALU.add))
            go(dve.tensor_tensor(f[3], f[3], f[2], ALU.mult))
            go(dve.tensor_tensor(f[5], f[5], f[3], ALU.add))
            for s, k in ((0, I_PERMD), (1, I_PERMS)):
                go(dve.tensor_scalar(lists[:, k, :], sf[5][:, s, :], float(E - 1), None, ALU.min))
            dve.tensor_scalar(f[0], f[4], MID, None, ALU.add).then_inc(s_kd, 1)
            dve.wait_ge(s_kd, 1)
            dve.wait_ge(s_kr, 160)
            dve.tensor_tensor(f[3], f[0], f[1], ALU.is_equal).then_inc(s_kd, 1)
            go(dve.tensor_tensor(f[4], f[0], f[2], ALU.is_equal))
            for s, k in ((0, I_DSTC), (1, I_SRCC)):
                go(dve.tensor_scalar(lists[:, k, :], sf[0][:, s, :], float(N - 1), None, ALU.min))
            go(dve.tensor_copy(lists[:, I_DSTR, :], sf[0][:, 0, :]))
            for s, k in ((0, I_DSTH), (1, I_SRCH)):
                ins = dve.scalar_tensor_tensor(out=lists[:, k, :], in0=sf[4][:, s, :], scalar=float(SKIP),
                                               in1=sf[0][:, s, :], op0=ALU.mult, op1=ALU.add)
                go(ins)
            dve.sem_inc(s_lists, 1)
            for k in range(7):
                dve.wait_ge(s_lt, k + 1)
                dve.tensor_copy(idx[:, k, :].rearrange("q (p h) -> q h p", h=2),
                                ps[k][:, 0:2 * P].rearrange("q (h p) -> q h p", h=2)[:, :, 0:NT // 2]).then_inc(s_idx, 1)

            def last_of(a, par, rows):
                return a[rows, 1 - par, CH - 1:CH]

            def l0(c, par, i):
                L = L0
                after_(L.pe, c, "ea")
                after_(L.pe, c - 1, "fs")
                dve.tensor_copy(ear[:, :], ps[1][:, :]).then_inc(L.dve.done("ea"), 1)
                dve.wait_ge(ec_sem[par], 64 * (i + 1))
                dve.tensor_copy(ea4d[:, bass.ds(c * 4, 4), :], eca[:, par, :, 2 * C:2 * C + 4])
                dve.tensor_copy(idx[:, I_SRCD, bass.ds(c * 4, 4)],
                                eca[:, par, :, EW - 1].bitcast(U32)).then_inc(L.dve.done("meta"), 1)
                after_(L.pe, c, "fs")
                after_(L.act, c, "sabs")
                after_(L.dve, c - 1, "core")
                ts(L.dve.done("srelu"), w[6][H, :], ps[2][U, :], b_fs[U, :], 0.0, ALU.add, ALU.max)
                after_(L.act, c, "log")
                after_(L.dve, c, "srelu")
                tt(L.dve.done("core"), w[9][H, :], w[6][H, :], w[2][H, :], ALU.add)
                after_(L.dve, c, "core")
                tt(L.dve.done("msg"), w[10][H, :], w[9][H, :], w[8][H, :], ALU.mult)
                dve.wait_ge(L.mk[par], 16 * (i + 1))
                after_(L.dve, c, "msg")
                scan(L.dve.done("agg"), sc[0][H, par, :], mk[H, par, 0:CH], w[10][H, :], last_of(sc[0], par, H), ALU.mult, ALU.add)
                after_(L.dve, c, "agg")
                after_(L.act, c, "z")
                tt(L.dve.done("t"), w[11][H, :], sc[0][H, par, :], z[H, :], ALU.add)
                after_(L.dve, c, "t")
                after_(L.pe, c - 1, "center")
                stt(L.dve.done("y"), w[12][H, :], w[11][H, :], 0.0, z[H, :], ALU.max, ALU.add)
                after_(L.act, c, "rstd")
                after_(L.pe, c - 1, "out")
                tt(L.dve.done("x1"), w[13][H, :], ps[3][H, :], w[5][H, :], ALU.mult)
            pairs_of_chunks(dve, l0)

            def l1(c, par, i):
                L = L1
                after_(L.act, c, "lrelu")
                after_(L.dve, c - 1, "d")
                tt(L.dve.done("e"), w[1][H, :], ps[1][H, :], w[0][H, :], ALU.max)
                after_(L.dve, c, "e")
                after_(L.act, c, "negm")
                scan(L.dve.done("mrun"), sc[0][H, par, :], negm[H, 0:CH], w[1][H, :], last_of(sc[0], par, H), ALU.add, ALU.max)
                after_(L.dve, c, "mrun")
                scan(L.dve.done("mseg"), w[3][H, ::-1], negm[H, CH:0:-1], sc[0][H, par, ::-1], -BIG, ALU.add, ALU.max)
                after_(L.dve, c, "mseg")
                after_(L.act, c - 1, "ex")
                tt(L.dve.done("d"), w[4][H, :], w[1][H, :], w[3][H, :], ALU.subtract)
                after_(L.act, c - 1, "carry")
                ts(L.dve.done("dcar"), sm[H, 0:1], last_of(sc[0], par, H), w[3][H, 0:1], 0.0, ALU.subtract, ALU.min)
                after_(L.act, c, "carry")
                tt(s_l1_c, sm[H, 2:3], last_of(sc[1], par, H), sm[H, 1:2], ALU.mult)
                tt(L.dve.done("carry"), sm[H, 3:4], last_of(sc[2], par, H), sm[H, 1:2], ALU.mult)
                after_(L.dve, c, "carry")
                after_(L.act, c, "ex")
                dve.wait_ge(L.mk[par], 16 * (i + 1))
                scan(L.dve.done("den"), sc[1][H, par, :], mk[H, par, 0:CH], w[5][H, :], sm[H, 2:3], ALU.mult, ALU.add)
                after_(L.pe, c, "xp")
                after_(L.dve, c - 1, "num")
                tt(L.dve.done("val"), w[7][H, :], ps[2][H, :], w[5][H, :], ALU.mult)
                after_(L.dve, c, "val")
                scan(L.dve.done("num"), sc[2][H, par, :], mk[H, par, 0:CH], w[7][H, :], sm[H, 3:4], ALU.mult, ALU.add)
                after_(L.dve, c, "den")
                ts(L.dve.done("dmax"), w[8][H, :], sc[1][H, par, :], 1e-30, None, ALU.max)
                after_(L.dve, c, "dmax")
                dve.reciprocal(w[9][H, :], w[8][H, :]).then_inc(L.dve.done("rden"), 1)
                after_(L.dve, c, "rden")
                tt(L.dve.done("att"), w[10][H, :], sc[2][H, par, :], w[9][H, :], ALU.mult)
                after_(L.dve, c, "att")
                after_(L.pe, c - 1, "out")
                after_(L.act, c, "z")
                tt(L.dve.done("v2"), w[13][H, :], w[10][H, :], z[H, :], ALU.add)
                scan(L.dve.done("cnt"), sc[3][C:C + 1, par, :], mk[C:C + 1, par, 0:CH], ones[C:C + 1, :],
                     sc[3][C:C + 1, 1 - par, CH - 1:CH], ALU.mult, ALU.add)
                again(dve.wait_ge, h1_sem[par], 16, i)
                dve.wait_ge(L.gat[par], 128 * (i + 1))
                dve.tensor_copy(ot[:, par, :, TW - 1:TW], gat[:, par, :, TW - 1:TW]).then_inc(L.dve.done("flag"), 1)
            for k in range(2):
                dve.wait_ge(L0.sca[k], tot[k])
            pairs_of_chunks(dve, l1)

            def dense(d, par, i):
                S = D_dve
                after_(D_act, d, "r2")
                after_(D_pe, d - 1, "h")
                tt(S.done("x2"), w[3][:, :], ps[1][:, :], w[2][:, :], ALU.mult)
                after_(D_act, d, "relu")
                after_(S, d, "x2")
                tt(S.done("y3"), w[5][:, :], w[3][:, :], w[4][:, :], ALU.add)
                after_(D_act, d, "r3")
                after_(D_pe, d - 1, "gh")
                tt(S.done("x3"), w[6][:, :], ps[4][:, :], w[2][:, :], ALU.mult)
                after_(D_pe, d, "gh")
                after_(D_act, d, "r")
                stt(S.done("q"), w[9][:, :], ps[3][:, :], dg_b[:, 3:4], w[7][:, :], ALU.add, ALU.mult)
                after_(S, d, "q")
                tt(S.done("a"), w[11][:, :], ps[7][:, :], w[9][:, :], ALU.add)
                after_(D_act, d, "n")
                tt(S.done("xn"), w[9][:, :], w[6][:, :], w[10][:, :], ALU.subtract)
                after_(S, d, "xn")
                tt(S.done("zxn"), w[9][:, :], w[9][:, :], w[8][:, :], ALU.mult)
                after_(S, d, "zxn")
                tt(S.done("o"), w[9][:, :], w[9][:, :], w[10][:, :], ALU.add)
                after_(S, d, "o")
                tt(S.done("y4"), w[12][:, :], w[9][:, :], w[6][:, :], ALU.add)
                after_(D_act, d, "r4")
                after_(D_pe, d - 1, "out")
                tt(S.done("x4"), w[13][:, :], ps[1][:, :], w[2][:, :], ALU.mult)
            for k in range(2):
                dve.wait_ge(L1.sca[k], tot[k])
            pairs_of_chunks(dve, dense, 0, ND)

            def l2(c, par, i):
                L = L2
                S = L.dve
                after_(L.act, c, "rstd")
                after_(L.pe, c - 1, "h")
                tt(S.done("x2"), w[5][:, :], ps[1][:, :], w[2][:, :], ALU.mult)
                dve.wait_ge(L.mk[par], 16 * (i + 1))
                scan(S.done("cnt"), sc[1][U, par, :], mk[U, par, 0:CH], ones[U, :], last_of(sc[1], par, U), ALU.mult, ALU.add)
                after_(L.pe, c, "norm")
                after_(S, c, "x2")
                tt(S.done("msg"), w[6][U, :], ps[3][U, :], w[5][U, :], ALU.mult)
                after_(S, c, "msg")
                scan(S.done("agg"), sc[0][U, par, :], mk[U, par, 0:CH], w[6][U, :], last_of(sc[0], par, U), ALU.mult, ALU.add)
                after_(S, c, "agg")
                after_(L.act, c, "nin")
                tt(S.done("aggn"), w[7][U, :], sc[0][U, par, :], w[4][U, :], ALU.mult)
                after_(L.act, c, "relu")
                after_(L.pe, c - 1, "out")
                tt(S.done("y3"), w[9][:, :], w[5][:, :], w[8][:, :], ALU.add)
                dve.wait_ge(L.gat[par], 128 * (i + 1))
                ts(S.done("fsel"), sm[:, 4:8], gat[:, par, :, 2 * TW - 1], -float(SKIP), float(SKIP), ALU.mult, ALU.add)
                after_(S, c, "fsel")
                dve.wait_ge(L.gst[par], 32 * (i + 1))
                tt(S.done("srcf"), idx[:, I_SRCF, bass.ds(c * 4, 4)], sm[:, 4:8], gst[:, par, 1, :], ALU.add)
            for k in range(2):
                dve.wait_ge(do_sem[k], 16 * (ND // 2))
            pairs_of_chunks(dve, l2)

            def l3(c, par, i):
                L = L3
                S = L.dve
                after_(L.act, c, "rstd")
                after_(L.pe, c - 1, "g2")
                tt(S.done("x3"), w[4][:, :], ps[1][:, :], w[2][:, :], ALU.mult)
                dve.wait_ge(L.mk[par], 16 * (i + 1))
                scan(S.done("cnt"), sc[3][:, par, :], mk[:, par, 0:CH], ones[:, :], last_of(sc[3], par, slice(0, P)), ALU.mult, ALU.add)
                after_(L.pe, c, "h")
                after_(L.act, c - 1, "n")
                ts(S.done("ha"), w[5][:, :], ps[4][:, :], bew_col[:, :], None, ALU.add)
                after_(S, c, "ha")
                after_(L.pe, c, "ew")
                tt(S.done("hw"), w[5][:, :], ps[5][:, :], w[5][:, :], ALU.mult)
                after_(L.act, c, "h")
                tt(S.done("hsq"), w[8][U, :], w[6][U, :], w[6][U, :], ALU.mult)
                after_(S, c, "hsq")
                scan(S.done("s1"), sc[0][:, par, :], mk[:, par, 0:CH], w[6][:, :], last_of(sc[0], par, slice(0, P)), ALU.mult, ALU.add)
                scan(S.done("s2"), sc[1][U, par, :], mk[U, par, 0:CH], w[8][U, :], last_of(sc[1], par, U), ALU.mult, ALU.add)
                after_(L.act, c, "hneg")
                after_(L.act, c, "negm")
                scan(S.done("mx"), sc[2][:, par, :], negm[:, 0:CH], w[7][:, :], last_of(sc[2], par, slice(0, P)), ALU.add, ALU.max)
                after_(S, c, "cnt")
                dve.reciprocal(w[15][:, :], sc[3][:, par, :]).then_inc(S.done("rcnt"), 1)
                after_(S, c, "rcnt")
                after_(L.pe, c - 1, "u")
                tt(S.done("mean"), w[9][:, :], sc[0][:, par, :], w[15][:, :], ALU.mult)
                after_(S, c, "mean")
                tt(S.done("msq"), w[11][U, :], w[9][U, :], w[9][U, :], ALU.mult)
                tt(S.done("ms2"), w[12][U, :], sc[1][U, par, :], w[15][U, :], ALU.mult)
                after_(S, c, "ms2")
                tt(S.done("vard"), w[12][U, :], w[12][U, :], w[11][U, :], ALU.subtract)
                after_(S, c, "vard")
                ts(S.done("var"), w[12][U, :], w[12][U, :], 0.0, None, ALU.max)
                after_(L.act, c, "logd")
                ts(S.done("f2"), w[16][:, :], w[10][:, :], iavg[:, :], None, ALU.mult)
                dve.reciprocal(w[17][U, :], w[10][U, :]).then_inc(S.done("rlog"), 1)
                after_(S, c, "rlog")
                stt(S.done("f3"), w[16][U, :], w[17][U, :], avg[U, :], w[16][U, :], ALU.mult, ALU.mult)
                after_(S, c, "f3")
                after_(L.pe, c, "p")
                tt(S.done("fp"), w[14][:, :], ps[6][:, :], w[16][:, :], ALU.mult)
                after_(L.act, c, "rz")
                after_(L.pe, c, "g2")
                stt(S.done("q"), w[15][H, :], ps[5][U, :], brow[U, 1, 2:3], w[10][U, :], ALU.add, ALU.mult)
                after_(S, c, "q")
                tt(S.done("a"), w[11][H, :], ps[5][H, :], w[15][H, :], ALU.add)
                after_(L.act, c, "n")
                tt(S.done("xn"), w[15][H, :], w[4][H, :], w[6][H, :], ALU.subtract)
                after_(S, c, "xn")
                tt(S.done("zxn"), w[15][H, :], w[15][H, :], w[10][H, :], ALU.mult)
                after_(S, c, "zxn")
                tt(S.done("o"), w[15][H, :], w[15][H, :], w[6][H, :], ALU.add)
                after_(S, c, "o")
                tt(S.done("y4"), w[12][H, :], w[15][H, :], w[4][H, :], ALU.add)
                after_(L.act, c, "rstd4")
                after_(L.pe, c - 1, "out")
                tt(S.done("x4"), w[13][H, :], ps[6][H, :], w[2][H, :], ALU.mult)
            for k in range(2):
                dve.wait_ge(L2.sca[k], tot[k])
            pairs_of_chunks(dve, l3)

        @block.tensor
        def _(pe):
            def hold(s, v):
                pe.wait_ge(s, v)
                pe.sem_inc(s_tick_pe, 1)

            def hold_after(steps, c, name):
                hold(steps.sem, steps.at(c, name))

            def product(dest, parts, done=None):
                for k, (lhsT, rhs) in enumerate(parts):
                    m = pe.matmul(dest, lhsT, rhs, start=(k == 0), stop=(k == len(parts) - 1))
                if done is not None:
                    m.then_inc(done, 1)

            for S in (L0.pe, L1.pe, L2.pe, L3.pe, D_pe):
                pe.sem_inc(S.sem, 2 * S.n)

            pe.wait_ge(s_wload, NW)
            pe.wait_ge(s_wdve, 3)
            product(ps[0][:, 0:C], [(w1_l[:, :], att_m[:, 0, :]), (w1_r[:, :], att_m[:, 1, :])])
            product(ps[1][:, 0:P], [(w3t_l[:, :], wpre2[:, 0, :]), (w3t_r[:, :], wpre2[:, 1, :])])
            product(ps[2][0:4, 0:P], [(wet[:, :], wpre2[:, 2, :])])
            product(ps[2][:, 256:257], [(wpre2[:, 2, :], be_col[:, :])])
            product(ps[3][0:C, 0:P], [(w3t_l[:, 0:C], wpm[:, :])])
            product(ps[3][0:C, 256:256 + C], [(wpm[:, C:P], w3t_l[:, 0:C])])
            product(ps[4][:, 0:1], [(avgmat[0:125, :], nvs[:, :])], s_wpe)
            pe.wait_ge(s_wdve, 4)
            product(ps[5][0:C, 0:1], [(wstd[:, s, :], fac0[:, 4 + s:5 + s]) for s in range(3)], s_wpe)
            pe.wait_ge(s_wdve, 5)
            for g in range(3):
                product(ps[6][:, 8 * g:8 * g + 1], [(wih2[:, g, :], out0[:, :])])
            product(ps[7][:, 0:3 * C].rearrange("p (g c) -> p g c", g=3), [(mmt2[:, :], wih2[:, :, 0:C])], s_wpe)

            for n, (src_tile, level) in enumerate(turn_plan):
                pe.wait_ge(s_sort, level)
                for s in range(2):
                    for h in range(2):
                        m = pe.transpose(ps[0][:, (2 * s + h) * P:(2 * s + h + 1) * P],
                                         src_tile[:, s, h * P:(h + 1) * P], ident)
                m.then_inc(s_sortt, 1)
            pe.wait_ge(s_lists, 1)
            for m_ in range(7):
                for h in range(2):
                    m = pe.transpose(ps[m_][:, h * P:(h + 1) * P], lists[:, m_, h * P:(h + 1) * P], ident)
                m.then_inc(s_lt, 1)

            def turn(dest, tiles, done):
                for t, a in enumerate(tiles):
                    m = pe.transpose(dest[:, blk[t]], a, ident)
                m.then_inc(done, 1)

            def turn_back(dest, a, rows, done):
                for t in range(4):
                    m = pe.transpose(dest[:, rows * t:rows * (t + 1)], a[0:rows, blk[t]], ident[0:rows, 0:rows])
                m.then_inc(done, 1)

            pe.wait_ge(s_idx, 7)
            def l0(c, par, i):
                L = L0
                hold(L.gat[par], 128 * (i + 1))
                hold_after(L.act, c - 1, "z")
                turn(ps[0], [gat[:, par, t, 0:P] for t in range(4)], L.pe.done("z"))
                hold(ec_sem[par], 64 * (i + 1))
                hold_after(L.dve, c - 1, "ea")
                turn(ps[1], [eca[:, par, t, 0:P] for t in range(4)], L.pe.done("ea"))
                hold_after(L.act, c, "z")
                hold_after(L.dve, c, "ea")
                hold_after(L.dve, c - 1, "srelu")
                hold_after(L.act, c - 1, "sabs")
                product(ps[2][:, :], [(w_fs_z[:, :], z[:, :]), (w_fs_e[:, :], ear[:, :])], L.pe.done("fs"))
                hold_after(L.dve, c, "y")
                product(ps[3][0:C, :], [(center[0:C, 0:C], w[12][0:C, :])], L.pe.done("center"))
                hold_after(L.act, c, "sq")
                product(ps[4][0:C, :], [(mean64[0:C, 0:C], w[3][0:C, :])], L.pe.done("var"))
                hold_after(L.dve, c, "x1")
                hold_after(L.act, c - 1, "out")
                turn_back(ps[5], w[13], C, L.pe.done("out"))
            pairs_of_chunks(pe, l0)

            def l1(c, par, i):
                L = L1
                hold_after(L.act, c, "pack")
                turn(ps[0], [pk[:, t, :] for t in range(4)], L.pe.done("z"))
                hold_after(L.act, c, "z")
                hold_after(L.dve, c - 1, "e")
                product(ps[1][0:C, :], [(w_score[:, :], z[:, :])], L.pe.done("score"))
                hold_after(L.dve, c - 1, "val")
                product(ps[2][0:C, :], [(w1t[C:P, :], z[C:P, :])], L.pe.done("xp"))
                hold_after(L.dve, c, "v2")
                hold_after(L.act, c, "norm")
                hold_after(L.act, c - 1, "out")
                turn_back(ps[3], w[13], C + 1, L.pe.done("out"))
            for k in range(2):
                pe.wait_ge(L0.sca[k], tot[k])
            pairs_of_chunks(pe, l1)

            def dense(d, par, i):
                hold_after(D_act, d, "pack")
                hold_after(D_act, d - 1, "out")
                turn(ps[0], [pk[:, k, :] for k in range(4)], D_pe.done("z"))
                hold_after(D_act, d, "z")
                hold_after(D_dve, d - 1, "x4")
                product(ps[1][:, :], [(center, z[:, :])], D_pe.done("c2"))
                hold_after(D_act, d, "sq2")
                product(ps[2][:, :], [(mean64, w[0][:, :])], D_pe.done("v2"))
                hold_after(D_dve, d, "x2")
                product(ps[3][:, :], [(w2_bd[:, :], w[3][:, :])], D_pe.done("h"))
                hold_after(D_dve, d, "y3")
                product(ps[4][:, :], [(center, w[5][:, :])], D_pe.done("c3"))
                hold_after(D_act, d, "sq3")
                product(ps[2][:, :], [(mean64, w[0][:, :])], D_pe.done("v3"))
                hold_after(D_dve, d, "x3")
                hold_after(D_dve, d - 1, "a")
                for g, (bank, name) in enumerate(((5, "gr"), (6, "gz"), (7, "gi"), (3, "gh"))):
                    product(ps[bank][:, :], [(dg[:, g, :], w[6][:, :])], D_pe.done(name))
                hold_after(D_dve, d, "y4")
                product(ps[1][:, :], [(center, w[12][:, :])], D_pe.done("c4"))
                hold_after(D_act, d, "sq4")
                product(ps[2][:, :], [(mean64, w[0][:, :])], D_pe.done("v4"))
                hold_after(D_dve, d, "x4")
                turn_back(ps[0], w[13], P, D_pe.done("out"))
            for k in range(2):
                pe.wait_ge(L1.sca[k], tot[k])
            pairs_of_chunks(pe, dense, 0, ND)

            def l2(c, par, i):
                L = L2
                hold_after(L.act, c, "pack")
                turn(ps[0], [pk[:, t, :] for t in range(4)], L.pe.done("z"))
                hold_after(L.act, c, "z")
                hold_after(L.dve, c - 1, "x2")
                product(ps[1][:, :], [(center, z[:, :])], L.pe.done("center"))
                hold_after(L.act, c, "sq")
                product(ps[2][:, :], [(mean64, w[0][:, :])], L.pe.done("var"))
                hold_after(L.dve, c - 1, "msg")
                hold(L.gat[par], 128 * (i + 1))
                for t in range(4):
                    m = pe.matmul(ps[3][:, blk[t]], gat[:, par, t, TW + C:TW + C + 1].broadcast_to([P, P]), ident,
                                  start=True, stop=True)
                m.then_inc(L.pe.done("norm"), 1)
                hold_after(L.dve, c, "aggn")
                hold_after(L.act, c - 1, "relu")
                product(ps[4][:, :], [(w2_bd[:, :], w[5][:, :]), (w2_neg[C:P, :], w[7][C:P, :])], L.pe.done("h"))
                hold_after(L.dve, c, "y3")
                hold_after(L.act, c - 1, "out")
                turn_back(ps[5], w[9], P, L.pe.done("out"))
            for k in range(2):
                pe.wait_ge(do_sem[k], 16 * (ND // 2))
            pairs_of_chunks(pe, l2)

            def l3(c, par, i):
                L = L3
                hold(L.gat[par], 128 * (i + 1))
                hold(eal_sem[par], 16 * (i + 1))
                hold_after(L.act, c - 1, "z")
                turn(ps[0], [gat[:, par, t, 0:P] for t in range(4)], L.pe.done("z"))
                hold_after(L.act, c - 1, "ea")
                for t in range(4):
                    m = pe.transpose(ps[3][0:4, blk[t]], eas[:, par, t, :], ident)
                m.then_inc(L.pe.done("ea"), 1)
                hold_after(L.act, c, "z")
                product(ps[1][:, :], [(center, z[:, :])], L.pe.done("center"))
                hold_after(L.act, c, "sq")
                product(ps[2][:, :], [(mean64, w[0][:, :])], L.pe.done("var"))
                hold_after(L.act, c, "ea")
                hold_after(L.dve, c, "x3")
                hold_after(L.dve, c - 1, "a")
                product(ps[4][:, :], [(w_h[:, :], w[4][:, :]), (w_hea[:, :], w[3][0:4, :])], L.pe.done("h"))
                product(ps[5][:, :], [(selw[0:4, :], w[3][0:4, :])], L.pe.done("ew"))
                hold_after(L.act, c, "std")
                hold_after(L.dve, c, "mx")
                hold_after(L.dve, c - 1, "x4")
                product(ps[6][:, :], [(wp_a1[:, :], w[9][:, :]), (wp_a2[:, :], sc[2][:, par, :])], L.pe.done("p"))
                hold_after(L.dve, c, "fp")
                hold_after(L.act, c - 1, "out")
                product(ps[7][:, :], [(wu_x[:, :], w[4][0:C, :]), (wu_a1[:, :], w[9][:, :]),
                                      (wu_a2[:, :], sc[2][:, par, :]), (wu_f[:, :], w[14][:, :])], L.pe.done("u"))
                hold_after(L.act, c, "u")
                product(ps[4][:, :], [(w_g1[:, :], w[4][:, :])], L.pe.done("g1"))
                product(ps[5][:, :], [(w_g2[:, :], w[4][:, :])], L.pe.done("g2"))
                hold_after(L.dve, c, "y4")
                product(ps[6][0:C, :], [(center[0:C, 0:C], w[12][0:C, :])], L.pe.done("center4"))
                hold_after(L.act, c, "sq4")
                product(ps[2][0:C, :], [(mean64[0:C, 0:C], w[0][0:C, :])], L.pe.done("var4"))
                hold_after(L.dve, c, "x4")
                turn_back(ps[7], w[13], C, L.pe.done("out"))
            for k in range(2):
                pe.wait_ge(L2.sca[k], tot[k])
            pairs_of_chunks(pe, l3)

        @block.scalar
        def _(act):
            def run(name_done, *args, **kw):
                act.activation(*args, **kw).then_inc(name_done, 1)

            def after_act(steps, c, name):
                act.wait_ge(steps.sem, steps.at(c, name))

            for S in (d1_act, L0.act, L1.act, L2.act, L3.act, D_act):
                act.sem_inc(S.sem, 2 * S.n)

            act.wait_ge(s_wload, NW)
            act.wait_ge(s_const, 3)
            run(s_wact, nv[:, :], nv[:, :], ACT.Ln, bias=one_col[0:125, :])
            run(s_wact, fac0[:, 0:1], eps_col[0:C, :], ACT.Ln)
            act.wait_ge(s_wact, 2)
            run(s_wact, fac0[:, 4:5], fac0[:, 0:1], ACT.Exp, scale=0.5)
            run(s_wact, fac0[:, 1:2], one_col[0:C, :], ACT.Ln, bias=one_col[0:C, :])

            def dense1(j, r=R1, n=P, last=False):
                act.wait_ge(s_d1l, 16 * (j + 1))
                after_act(d1_dve, j - 1, "norm")
                run(d1_act.done("relu"), d1r[0:n, 0:r, :], d1x[0:n, 0:r, :], ACT.Relu)
                after_act(d1_dve, j, "centered")
                run(d1_act.done("square"), d1r[0:n, 0:r, :], d1o[0:n, 0:r, 0:C], ACT.Square)
                after_act(d1_dve, j, "sumsq")
                run(d1_act.done("ln"), d1s[0:n, 2, 0:r], d1s[0:n, 1, 0:r], ACT.Ln, scale=1.0 / C, bias=eps_col[0:n, :])
                after_act(d1_act, j, "ln")
                run(d1_act.done("rstd"), d1s[0:n, 3, 0:r], d1s[0:n, 2, 0:r], ACT.Exp, scale=-0.5)
            with act.Fori(0, ROWS1) as j:
                dense1(j)
            dense1(ROWS1, 1, TAIL1)

            def rstd(L, c, names, centered, sq, var, ln, out_, rows=slice(0, P), ready="center", vready="var", pe_=None,
                     free=()):
                pe_ = pe_ or L.pe
                after_act(pe_, c, ready)
                run(L.act.done(names[0]), sq[rows, :], centered[rows, :], ACT.Square)
                after_act(pe_, c, vready)
                run(L.act.done(names[1]), ln[rows, :], var[rows, :], ACT.Ln, bias=eps_col[rows, :])
                after_act(L.act, c, names[1])
                for f in free:
                    after_act(*f)
                run(L.act.done(names[2]), out_[rows, :], ln[rows, :], ACT.Exp, scale=-0.5)

            H = slice(0, C)
            U = slice(C, P)

            def l0(c, par, i):
                L = L0
                after_act(L.pe, c, "z")
                after_act(L.pe, c - 1, "fs")
                after_act(L.dve, c - 1, "y")
                run(L.act.done("z"), z[:, :], ps[0][:, :], ACT.Copy)
                after_act(L.pe, c, "fs")
                after_act(L.dve, c - 1, "msg")
                run(L.act.done("gate"), w[8][H, :], ps[2][H, :], ACT.Sigmoid, bias=b_fs[H, :])
                run(L.act.done("sabs"), w[0][U, :], ps[2][U, :], ACT.Abs, bias=b_fs[U, :])
                after_act(L.act, c, "sabs")
                run(L.act.done("exps"), w[1][U, :], w[0][U, :], ACT.Exp, scale=-1.0)
                after_act(L.act, c, "exps")
                after_act(L.dve, c - 1, "core")
                run(L.act.done("log"), w[2][H, :], w[1][U, :], ACT.Ln, bias=one_col[U, :])
                rstd(L, c, ("sq", "ln", "rstd"), ps[3], w[3], ps[4], w[4], w[5], H, free=((L.dve, c - 1, "x1"),))
                after_act(L.pe, c, "out")
                again(act.wait_ge, L.sca[par], 64, i)
                run(L.act.done("out"), ot[:, par, :, 0:C], ps[5][:, 0:4 * C].rearrange("p (t k) -> p t k", t=4), ACT.Copy)
            pairs_of_chunks(act, l0)

            def l1(c, par, i):
                L = L1
                act.wait_ge(L.gat[par], 128 * (i + 1))
                after_act(L.pe, c - 1, "z")
                run(L.act.done("pack"), pk[:, :, :].rearrange("p t (a k) -> p t a k", a=2),
                    gat[:, par, :, :].rearrange("p t (a k) -> p t a k", a=2)[:, :, :, 0:C], ACT.Copy)
                after_act(L.pe, c, "z")
                after_act(L.pe, c - 1, "xp")
                after_act(L.dve, c - 1, "v2")
                run(L.act.done("z"), z[:, :], ps[0][:, :], ACT.Copy)
                act.wait_ge(L.mk[par], 16 * (i + 1))
                after_act(L.dve, c - 1, "mseg")
                run(L.act.done("negm"), negm[H, 0:CH], mk[H, par, 0:CH], ACT.Copy, scale=BIG, bias=-BIG)
                after_act(L.pe, c, "score")
                after_act(L.dve, c - 1, "e")
                run(L.act.done("lrelu"), w[0][H, :], ps[1][H, :], ACT.Copy, scale=0.2)
                after_act(L.dve, c, "d")
                after_act(L.dve, c - 1, "val")
                run(L.act.done("ex"), w[5][H, :], w[4][H, :], ACT.Exp)
                after_act(L.dve, c, "dcar")
                after_act(L.dve, c - 1, "carry")
                run(L.act.done("carry"), sm[H, 1:2], sm[H, 0:1], ACT.Exp)
                after_act(L.dve, c, "cnt")
                run(L.act.done("lncnt"), w[6][C:C + 1, :], sc[3][C:C + 1, par, :], ACT.Ln)
                after_act(L.act, c, "lncnt")
                after_act(L.pe, c - 1, "out")
                run(L.act.done("norm"), w[13][C:C + 1, :], w[6][C:C + 1, :], ACT.Exp, scale=-0.5)
                after_act(L.pe, c, "out")
                again(act.wait_ge, h1_sem[par], 16, i)
                run(L.act.done("out"), ot[:, par, :, 0:C + 1],
                    ps[3][:, 0:4 * (C + 1)].rearrange("p (t k) -> p t k", t=4), ACT.Copy)
            for k in range(2):
                act.wait_ge(L0.sca[k], tot[k])
            pairs_of_chunks(act, l1)

            class D:
                pe, act = D_pe, D_act

            def dense(d, par, i):
                act.wait_ge(dn_sem[par], 16 * (i + 1))
                after_act(D_pe, d - 1, "z")
                run(D_act.done("pack"), pk[:, :, :].rearrange("p k (a c) -> p k a c", a=2),
                    dn[:, par, :, :].rearrange("p (a k) c -> p k a c", a=2)[:, :, :, 0:C], ACT.Copy)
                after_act(D_pe, d, "z")
                after_act(D_pe, d - 1, "c2")
                run(D_act.done("z"), z[:, :], ps[0][:, :], ACT.Copy)
                rstd(D, d, ("sq2", "ln2", "r2"), ps[1], w[0], ps[2], w[1], w[2], ready="c2", vready="v2",
                     free=((D_dve, d - 1, "x4"), (D_pe, d - 1, "v4")))
                after_act(D_pe, d, "h")
                run(D_act.done("relu"), w[4][:, :], ps[3][:, :], ACT.Relu, bias=b2_col[:, :])
                rstd(D, d, ("sq3", "ln3", "r3"), ps[4], w[0], ps[2], w[1], w[2], ready="c3", vready="v3",
                     free=((D_dve, d, "x2"),))
                for g, (bank, t, name) in enumerate(((5, 7, "r"), (6, 8, "zg"))):
                    after_act(D_pe, d, ("gr", "gz")[g])
                    run(D_act.done(name), w[t][:, :], ps[bank][:, :], ACT.Sigmoid, bias=dg_b[:, g:g + 1])
                after_act(D_dve, d, "a")
                run(D_act.done("n"), w[10][:, :], w[11][:, :], ACT.Tanh, bias=dg_b[:, 2:3])
                rstd(D, d, ("sq4", "ln4", "r4"), ps[1], w[0], ps[2], w[1], w[2], ready="c4", vready="v4",
                     free=((D_dve, d, "x3"),))
                after_act(D_pe, d, "out")
                again(act.wait_ge, do_sem[par], 16, i)
                run(D_act.done("out"), do[:, par, :, :].rearrange("p (a k) c -> p k a c", a=2),
                    ps[0][:, :].rearrange("p (k a c) -> p k a c", k=4, a=2), ACT.Copy)
            for k in range(2):
                act.wait_ge(L1.sca[k], tot[k])
            pairs_of_chunks(act, dense, 0, ND)

            def l2(c, par, i):
                L = L2
                act.wait_ge(L.gat[par], 128 * (i + 1))
                after_act(L.pe, c - 1, "z")
                run(L.act.done("pack"), pk[:, :, :].rearrange("p t (a k) -> p t a k", a=2),
                    gat[:, par, :, :].rearrange("p t (a k) -> p t a k", a=2)[:, :, :, 0:C], ACT.Copy)
                after_act(L.pe, c, "z")
                after_act(L.pe, c - 1, "center")
                run(L.act.done("z"), z[:, :], ps[0][:, :], ACT.Copy)
                rstd(L, c, ("sq", "ln", "rstd"), ps[1], w[0], ps[2], w[1], w[2], free=((L.dve, c - 1, "x2"),))
                after_act(L.dve, c, "cnt")
                run(L.act.done("lncnt"), w[3][U, :], sc[1][U, par, :], ACT.Ln)
                after_act(L.act, c, "lncnt")
                after_act(L.dve, c - 1, "aggn")
                run(L.act.done("nin"), w[4][U, :], w[3][U, :], ACT.Exp, scale=-0.5)
                after_act(L.pe, c, "h")
                after_act(L.dve, c - 1, "y3")
                run(L.act.done("relu"), w[8][:, :], ps[4][:, :], ACT.Relu, bias=b2_col[:, :])
                after_act(L.pe, c, "out")
                again(act.wait_ge, L.sca[par], 64, i)
                again(act.wait_ge, h3_sem[par], 16, i)
                run(L.act.done("out"), ot3[:, par, :, :], ps[5][:, :].rearrange("p (t k) -> p t k", t=4), ACT.Copy)
            for k in range(2):
                act.wait_ge(do_sem[k], 16 * (ND // 2))
            pairs_of_chunks(act, l2)

            def l3(c, par, i):
                L = L3
                after_act(L.pe, c, "z")
                after_act(L.pe, c - 1, "center")
                run(L.act.done("z"), z[:, :], ps[0][:, :], ACT.Copy)
                rstd(L, c, ("sq", "ln", "rstd"), ps[1], w[0], ps[2], w[1], w[2], free=((L.dve, c - 1, "x4"),))
                after_act(L.pe, c, "ea")
                after_act(L.pe, c - 1, "ew")
                run(L.act.done("ea"), w[3][0:4, :], ps[3][0:4, :], ACT.Copy)
                act.wait_ge(L.mk[par], 16 * (i + 1))
                after_act(L.dve, c - 1, "mx")
                run(L.act.done("negm"), negm[:, 0:CH], mk[:, par, 0:CH], ACT.Copy, scale=BIG, bias=-BIG)
                after_act(L.dve, c, "hw")
                after_act(L.dve, c - 1, "o")
                run(L.act.done("h"), w[6][:, :], w[5][:, :], ACT.Identity, bias=bpre_col[:, :])
                after_act(L.act, c, "h")
                run(L.act.done("hneg"), w[7][:, :], w[6][:, :], ACT.Identity, scale=sgn_col[:, :])
                after_act(L.dve, c, "var")
                run(L.act.done("lnvar"), w[8][U, :], w[12][U, :], ACT.Ln, bias=eps_col[U, :])
                after_act(L.act, c, "lnvar")
                run(L.act.done("std"), w[9][U, :], w[8][U, :], ACT.Exp, scale=0.5)
                after_act(L.dve, c - 1, "zxn")
                run(L.act.done("logd"), w[10][:, :], sc[3][:, par, :], ACT.Ln, bias=one_col[:, :])
                after_act(L.pe, c, "u")
                run(L.act.done("u"), w[4][U, :], ps[7][U, :], ACT.Identity, bias=bpost_col[U, :])
                after_act(L.pe, c, "g1")
                after_act(L.dve, c, "rlog")
                run(L.act.done("rz"), w[10][:, :], ps[4][:, :], ACT.Sigmoid, bias=b_g1[:, :])
                after_act(L.dve, c, "a")
                run(L.act.done("n"), w[6][H, :], w[11][H, :], ACT.Tanh, bias=brow[H, 0, 2:3])
                rstd(L, c, ("sq4", "ln4", "rstd4"), ps[6], w[0], ps[2], w[1], w[2], H, ready="center4", vready="var4",
                     free=((L.dve, c, "x3"),))
                after_act(L.pe, c, "out")
                again(act.wait_ge, L.sca[par], 64, i)
                run(L.act.done("out"), ot3[:, par, :, 0:C], ps[7][:, 0:4 * C].rearrange("p (t k) -> p t k", t=4), ACT.Copy)
            for k in range(2):
                act.wait_ge(L2.sca[k], tot[k])
            pairs_of_chunks(act, l3)


def shape_constants():
    eye = np.eye(P, dtype=np.float32)
    two = np.kron(np.eye(2, dtype=np.float32), np.full((C, C), 1.0 / C, np.float32))
    heads = np.zeros((P, P), np.float32)
    heads[:C, :C] = np.kron(np.eye(HEADS, dtype=np.float32), np.ones((C // HEADS, C // HEADS), np.float32))
    row3 = np.zeros((P, P), np.float32)
    row3[3, :] = 1.0
    mats = np.stack([eye, eye - two, two, heads, row3], 1)
    place = np.arange(SN).reshape(P, SF)
    idx = np.repeat(place[:, None, :], 2, 1).astype(np.float32)
    bit = [1.0 - 2.0 * ((place >> k) & 1) for k in range(SK + 1)]
    bit[0] = np.ones_like(bit[0])
    sign = np.stack([bit[k] * bit[k - 1] for k in range(1, SK + 1)], 1).astype(np.float32)
    return np.ascontiguousarray(mats), np.ascontiguousarray(idx), np.ascontiguousarray(sign)


_INS = ["x", "src", "dst", "edge_attr_128", "edge_attr_4", "node_vec", "L0_gnn_W_f", "L0_gnn_b_f", "L0_gnn_W_s",
        "L0_gnn_b_s", "L1_gnn_W", "L1_gnn_src_attn", "L1_gnn_dst_attn", "L2_gnn_W", "L2_gnn_b", "L3_gnn_W",
        "L3_gnn_We", "L3_gnn_be", "L3_gnn_Wpre", "L3_gnn_bpre", "L3_gnn_Wpost", "L3_gnn_bpost", "L3_gnn_Wih",
        "L3_gnn_bih", "L3_gnn_Whh", "L3_gnn_bhh"]


def kernel(**inputs):
    import concourse.bacc as bacc
    from concourse.bass_utils import run_bass_kernel_spmd

    nc = bacc.Bacc("TRN2", target_bir_lowering=False, num_devices=1)
    arrays, args = {}, []
    named = [(n, np.ascontiguousarray(inputs[n])) for n in _INS]
    named += list(zip(("k_mats", "k_idx", "k_sign"), shape_constants()))
    for name, a in named:
        arrays[f"in_{name}"] = a
        args.append(nc.dram_tensor(f"in_{name}", a.shape, mybir.dt.from_np(a.dtype), kind="ExternalInput").ap())
    args.append(nc.dram_tensor("out_0", (N, C), F32, kind="ExternalOutput").ap())
    for name, shape in (("T", (N, TW)), ("X3", (N, C)), ("H1", (NCH * P, 4 * TW)), ("H3", (NCH * P, 4 * C)),
                        ("EC", (E, EW)), ("KD", (2, SN + 2)), ("MK", (2, SN))):
        args.append(nc.dram_tensor(name, shape, F32, kind="Internal").ap())
    gnn_kernel(nc, *args)
    r = run_bass_kernel_spmd(nc, [arrays], core_ids=[0])
    return r.results[0]["out_0"]
```

```python
from contextlib import ExitStack

import numpy as np

import concourse.bass as bass
from concourse import mybir

F32 = mybir.dt.float32
I32 = mybir.dt.int32
U32 = mybir.dt.uint32
ALU = mybir.AluOpType
ACT = mybir.ActivationFunctionType
AX_X = mybir.AxisListType.X

P = 128
N = 100000
E = 25000
C = 64
HEADS = 8
CH = 512
PAIRS = -(-E // (2 * CH))
NCH = 2 * PAIRS
NT = 4 * NCH
TW = C + 2
EW = 2 * C + 5
SF = 256
SN = P * SF
SK = 15
SKIP = 1 << 20
BIG = 1.0e30
EPS = 1e-5
MID = N / 2 + 0.5
MARGIN = 255.5
NODES = 1024
ND = -(-N // NODES)
DPAIRS = ND // 2
G = range(2)
LN_EXP = "natural_log_exp_and_others"
ROWS1 = 11
R1 = N // P // ROWS1
TAIL1 = N - P * R1 * ROWS1


class Count:

    def __init__(self, sem):
        self.sem, self.n = sem, 0

    def tick(self, ins):
        ins.then_inc(self.sem, 1)
        self.n += 1


class Steps:

    def __init__(self, sem, *names):
        self.sem, self.place, self.n = sem, {}, 0
        for group in names:
            group = (group,) if isinstance(group, str) else group
            for g in G:
                for name in group:
                    self.n += 1
                    self.place[name, g] = self.n
        self.order, self.next = sorted(self.place, key=self.place.get), 0

    def done(self, name):
        assert self.order[self.next % self.n][0] == name, (name, self.order[self.next % self.n])
        self.next += 1
        return self.sem

    def at(self, i, name, g=0):
        return (i + 1) * self.n + self.place[name, g]


class Steps1(Steps):

    def __init__(self, sem, *names):
        self.sem, self.n, self.next = sem, len(names), 0
        self.place = {(name, 0): k + 1 for k, name in enumerate(names)}
        self.order = [(name, 0) for name in names]


def gnn_kernel(nc, x, src, dst, ea128, ea4, node_vec, Wf, bf, Ws, bs, W1, a_src, a_dst, W2, b2,
               W3, We, be, Wpre, bpre, Wpost, bpost, Wih, bih, Whh, bhh,
               k_mats, k_idx, k_sign, out, T, X3, H1, H3, EC, KD, MK):
    with ExitStack() as ctx:
        ctx.enter_context(nc.allow_non_contiguous_dma(reason="small weights, loaded once, transposed"))
        def sb(name, shape, dt=F32):
            return ctx.enter_context(nc.sbuf_tensor(name, shape, dt))

        def sem(name):
            return ctx.enter_context(nc.semaphore(name))

        psum = [ctx.enter_context(nc.psum_tensor(f"ps{i}", [P, 512], F32)) for i in range(8)]
        ps = [psum[0:4], psum[4:8]]

        mats = sb("mats", [P, 5, P])
        ident, center, mean64, headmask, selw = (mats[:, i, :] for i in range(5))
        eps_col = sb("eps_col", [P, 1])
        one_col = sb("one_col", [P, 1])
        ones = sb("ones", [P, CH])
        avgmat = sb("avgmat", [P, P])

        w_fs_z = sb("w_fs_z", [P, P])
        w_fs_e = sb("w_fs_e", [P, P])
        b_fs = sb("b_fs", [P, 1])
        w1_l = sb("w1_l", [C, P])
        w1_r = sb("w1_r", [C, P])
        w1t = sb("w1t", [P, C])
        att = sb("att", [C, 2])
        att_m = sb("att_m", [C, 2, C])
        w_score = sb("w_score", [P, C])
        w2_bd = sb("w2_bd", [P, P])
        w2_neg = sb("w2_neg", [P, P])
        b2_col = sb("b2_col", [P, 1])
        w3t_l = sb("w3t_l", [C, P])
        w3t_r = sb("w3t_r", [C, P])
        wpre2 = sb("wpre2", [C, 3, P])
        wet = sb("wet", [C, 4])
        be_col = sb("be_col", [C, 1])
        bpre_col = sb("bpre_col", [P, 1])
        w_h = sb("w_h", [P, P])
        w_hea = sb("w_hea", [4, P])
        bew_col = sb("bew_col", [P, 1])
        wp_a1 = sb("wp_a1", [P, P])
        wp_a2 = sb("wp_a2", [P, P])
        wu_a1 = sb("wu_a1", [P, P])
        wu_a2 = sb("wu_a2", [P, P])
        wu_f = sb("wu_f", [P, P])
        wpm = sb("wpm", [C, P])
        wu_x = sb("wu_x", [C, P])
        bpost_col = sb("bpost_col", [P, 1])
        w_g1 = sb("w_g1", [P, P])
        w_g2 = sb("w_g2", [P, P])
        wih2 = sb("wih2", [C, 3, P])
        whh2 = sb("whh2", [P, 3 * C])
        brow = sb("brow", [P, 2, 3])
        b_g1 = sb("b_g1", [P, 1])
        wstd = sb("wstd", [C, 3, C])
        nv = sb("nv", [125, N // 125])
        nvs = sb("nvs", [125, 1])
        avg = sb("avg", [P, 1])
        iavg = sb("iavg", [P, 1])
        fac0 = sb("fac0", [C, 8])
        mmt2 = sb("mmt2", [C, P])
        out0 = sb("out0", [C, 1])
        dg = sb("dg", [P, 4, P])
        dg_b = sb("dg_b", [P, 4])

        s_const = sem("s_const")
        s_wload = sem("s_wload")
        s_wzero = sem("s_wzero")
        s_wpe = sem("s_wpe")
        s_wact = sem("s_wact")
        s_wdve = sem("s_wdve")

        (I_PERMD, I_DSTC, I_DSTR, I_DSTH, I_PERMS, I_SRCC, I_SRCH, I_SRCD, I_SRCF) = range(9)
        idx = sb("idx", [P, 9, NT], U32)
        ea4d = sb("ea4d", [P, NT, 4])

        keys = sb("keys", [P, 2, SF], I32)
        kidx = sb("kidx", [P, 2, SF])
        ksign = sb("ksign", [P, SK, SF])
        sx = sb("sx", [P, 2, SF])
        sy = sb("sy", [P, 2, SF])
        sf = [sb(f"sf{i}", [P, 2, SF]) for i in range(6)]
        si = [sb(f"si{i}", [P, 2, SF], I32) for i in range(3)]
        lists = sb("lists", [P, 7, SF])
        edge_col = sb("edge_col", [2, 2])

        s_keyl = sem("s_keyl")
        s_keym = sem("s_keym")
        s_sort = sem("s_sort")
        s_sortt = sem("s_sortt")
        s_ec = sem("s_ec")
        s_kd = sem("s_kd")
        s_kr = sem("s_kr")
        s_mk = sem("s_mk")
        s_lt = sem("s_lt")
        s_idx = sem("s_idx")

        d1x = sb("d1x", [P, R1, C])
        d1r = sb("d1r", [P, R1, C])
        d1o = sb("d1o", [P, R1, TW])
        d1s = sb("d1s", [P, 4, R1])
        s_d1l = sem("s_d1l")
        s_d1o = sem("s_d1o")
        d1_act = Steps1(sem("s_d1act"), "relu", "square", "ln", "rstd")
        d1_dve = Steps1(sem("s_d1dve"), "y", "sum", "mean", "centered", "sumsq", "norm")

        def rows1(ap, j, tail):
            if tail:
                return ap[P * R1 * ROWS1:N, :].rearrange("(p r) c -> p r c", r=1)
            return ap[0:P * R1 * ROWS1, :].rearrange("(p r) c -> p r c", p=P)[:, bass.ds(j * R1, R1), :]

        gat = sb("gat", [P, 2, 4, 2 * TW])
        eca = sb("eca", [P, 2, 4, EW])
        gst = sb("gst", [P, 2, 3, 4], U32)
        sst = sb("sst", [P, 2, 4], U32)
        pst = sb("pst", [P, 2, 4], U32)
        dli = sb("dli", [P, 2, 4], I32)
        eas = sb("eas", [P, 2, 4, 4])
        mk = sb("mk", [P, 2, CH + 1])
        ot = sb("ot", [P, 2, 4, TW])
        ot3 = sb("ot3", [P, 2, 4, P])

        def flat(a):
            return a[:, :, :].rearrange("p a b -> p (a b)")

        z = [sb("z", [P, CH]), flat(si[0]).bitcast(F32)]
        ear = [sb("ear", [P, CH]), flat(si[1]).bitcast(F32)]
        pk = [sb("pk", [P, 4, P]), flat(si[2]).bitcast(F32).rearrange("p (t k) -> p t k", t=4)]
        negm = [sb(f"negm{g}", [P, CH + 1]) for g in G]
        w0 = [flat(a)[:, k * CH:(k + 1) * CH] for a in (d1x, d1r) for k in range(8)]
        w0 += [sb(f"w{i}", [P, CH])[:, :] for i in range(16, 18)]
        w1 = [flat(ksign)[:, k * CH:(k + 1) * CH] for k in range(7)] + [flat(a) for a in sf]
        w1 += [flat(lists)[:, k * CH:(k + 1) * CH] for k in range(3)] + [flat(sx), flat(sy)]
        w = [w0, w1]
        sc = [sb(f"sc{i}", [P, 2, CH]) for i in range(4)]
        sm = [sb(f"sm{g}", [P, 8]) for g in G]
        s_tick_pool = sem("s_tick_pool")
        s_tick_pe = sem("s_tick_pe")
        s_tick_sp = sem("s_tick_sp")
        zeros = sb("zeros", [P, CH])
        s_x3z = sem("s_x3z")
        sgn_col = sb("sgn_col", [P, 1])
        bsum = sb("bsum", [P, 3])
        s_wd = sem("s_wd")
        s_lists = sem("s_lists")

        def par_sems(name):
            return [sem(f"{name}0"), sem(f"{name}1")]

        def after_chunk_before(wait, steps, i, name, g):
            wait(steps.sem, steps.at(i, name, 0) if g else steps.at(i - 1, name, 1))

        class Pass:
            def __init__(self, name, pe, act, dve):
                self.gst = par_sems(f"s_{name}_gst")
                self.sst = par_sems(f"s_{name}_sst")
                self.mk = par_sems(f"s_{name}_mk")
                self.gat = par_sems(f"s_{name}_gat")
                self.sca = par_sems(f"s_{name}_sca")
                self.pe = Steps(sem(f"s_{name}_pe"), *pe)
                self.act = Steps(sem(f"s_{name}_act"), *act)
                self.dve = Steps(sem(f"s_{name}_dve"), *dve)

        L0 = Pass("l0", ("z", "ea", "fs", "center", "var", "out"),
                  ("z", "sabs", "exps", "log", "gate", "sq", "ln", "rstd", "out"),
                  ("ea", "meta", "srelu", "core", "msg", "agg",
                   "t", "y", "x1"))
        ec_sem = par_sems("s_l0_ec")
        psg0 = par_sems("s_l0_pst")
        L1 = Pass("l1", ("z", "score", "xp", "out"),
                  ("pack", "z", "negm", "lncnt", "norm", "lrelu", "carry", "ex", "out"),
                  ("cnt", "e", ("mrun", "mseg", "dcar"), "d", "flag", "val", ("carry", "den", "num"), "dmax", "rden",
                   "att", "v2"))
        dl_sem = par_sems("s_l1_dst")
        h1_sem = par_sems("s_l1_h1")
        s_l1_c = sem("s_l1_c")
        psg1 = par_sems("s_l1_pst")
        L2 = Pass("l2", ("norm", "z", "center", "var", "h", "out"),
                  ("pack", "z", "lncnt", "nin", "sq", "ln", "rstd", "relu", "out"),
                  ("cnt", "fsel", "srcf", "x2", "msg", "agg", "aggn", "y3"))
        h3_sem = par_sems("s_l2_h3")
        L3 = Pass("l3", ("z", "ea", "center", "var", "h", "ew", "p", "u", "g1", "g2", "center4", "var4", "out"),
                  ("z", "sq", "ln", "rstd", "ea", "negm", "h", "hneg", "lnvar", "std", "logd", "u",
                   "rz", "n", "sq4", "ln4", "rstd4", "out"),
                  ("x3", "cnt", "ha", "hw", "hsq", "s1", "s2", "mx", "rcnt", "mean", "msq", "ms2", "vard", "var",
                   "f2", "rlog", "f3", "fp", "q", "a", "xn", "zxn", "o", "y4", "x4"))
        eal_sem = par_sems("s_l3_ea")

        dn = sb("dn", [P, 2, 8, TW])
        do = sb("do", [P, 2, 8, C])
        dn_sem = par_sems("s_dn_in")
        do_sem = par_sems("s_dn_out")
        D_pe = Steps(sem("s_dn_pe"), "z", "c2", "v2", "h", "c3", "v3", "gr", "gz", "gi", "gh", "c4", "v4", "out")
        D_act = Steps(sem("s_dn_act"), "pack", "z", "sq2", "ln2", "r2", "relu", "sq3", "ln3", "r3", "r", "zg", "n",
                      "sq4", "ln4", "r4", "out")
        D_dve = Steps(sem("s_dn_dve"), "x2", "y3", "x3", "q", "a",
                      "xn", "zxn", "o", "y4", "x4")

        def dense_rows(d, ap, last):
            if last:
                return ap[(ND - 1) * NODES:N, :].rearrange("(p r) c -> p r c", r=8)
            return ap[bass.ds(d * NODES, NODES), :].rearrange("(p r) c -> p r c", r=8)

        LASTP = (N - (ND - 1) * NODES) // 8

        src_f = src.bitcast(F32).rearrange("(e a) -> e a", a=1)
        dst_r = dst.rearrange("(e a) -> e a", a=1)
        full, rest = E // SF, E % SF

        def col(ap):
            return ap.rearrange("(a b) -> a b", b=1)

        wloads = [
            (mats[:, :, :], k_mats),
            (w_fs_z[:, 0:C], Wf[0:P, :]), (w_fs_z[:, C:P], Ws[0:P, :]),
            (w_fs_e[:, 0:C], Wf[P:2 * P, :]), (w_fs_e[:, C:P], Ws[P:2 * P, :]),
            (b_fs[0:C, :], col(bf)), (b_fs[C:P, :], col(bs)),
            (w1_l[:, 0:C], W1), (w1_r[:, C:P], W1),
            (w1t[C:P, :], W1.rearrange("a b -> b a")),
            (att[:, 0:1], a_src.rearrange("a h d -> (h d) a")), (att[:, 1:2], a_dst.rearrange("a h d -> (h d) a")),
            (w2_bd[0:C, 0:C], W2.rearrange("a b -> b a")), (w2_bd[C:P, C:P], W2.rearrange("a b -> b a")),
            (b2_col[0:C, :], col(b2)), (b2_col[C:P, :], col(b2)),
            (w3t_l[:, 0:C], W3.rearrange("a b -> b a")), (w3t_r[:, C:P], W3.rearrange("a b -> b a")),
            (wpre2[:, :, 0:C], Wpre.rearrange("(k p) c -> p k c", k=3)),
            (wpre2[:, :, C:P], Wpre.rearrange("(k p) c -> p k c", k=3)),
            (wet[:, 0:3], We.rearrange("a b -> b a")),
            (be_col[:, :], col(be)), (bpre_col[0:C, :], col(bpre)), (bpre_col[C:P, :], col(bpre)),
            (wpm[:, C:P], Wpost[0:C, :]),
            (bpost_col[0:C, :], col(bpost)), (bpost_col[C:P, :], col(bpost)),
            (whh2[0:C, :], Whh), (whh2[C:P, :], Whh),
            (w_g1[0:C, 0:C], Whh[:, C:2 * C]), (w_g1[0:C, C:P], Whh[:, 0:C]),
            (w_g1[C:P, 0:C], Wih[:, C:2 * C]), (w_g1[C:P, C:P], Wih[:, 0:C]),
            (w_g2[0:C, C:P], Whh[:, 2 * C:3 * C]), (w_g2[C:P, 0:C], Wih[:, 2 * C:3 * C]),
            (wih2[:, :, 0:C], Wih.rearrange("p (g c) -> p g c", g=3)),
            (wih2[:, :, C:P], Wih.rearrange("p (g c) -> p g c", g=3)),
            (nv[:, :], node_vec.rearrange("(p a) -> p a", p=125)),
        ]
        post = {(s, k): C + 4 * C * s + C * k for s in range(3) for k in range(4)}
        MEAN, MIN, MAX, STD = range(4)
        for half, a1, a2 in ((0, MEAN, MIN), (C, STD, MAX)):
            for s, cols in ((1, slice(0, C)), (2, slice(C, P))):
                wloads.append((wp_a1[half:half + C, cols], Wpost[post[s, a1]:post[s, a1] + C, :]))
                wloads.append((wp_a2[half:half + C, cols], Wpost[post[s, a2]:post[s, a2] + C, :]))
            wloads.append((wu_a1[half:half + C, C:P], Wpost[post[0, a1]:post[0, a1] + C, :]))
            wloads.append((wu_a2[half:half + C, C:P], Wpost[post[0, a2]:post[0, a2] + C, :]))
        for s in range(3):
            wloads.append((wstd[:, s, :], Wpost[post[s, STD]:post[s, STD] + C, :]))
        for h in (0, C):
            for g in range(3):
                wloads.append((brow[h:h + C, 0, g:g + 1], col(bih[g * C:(g + 1) * C])))
                wloads.append((brow[h:h + C, 1, g:g + 1], col(bhh[g * C:(g + 1) * C])))
        NW = 16 * len(wloads)

        zeroed = [w1_l, w1_r, w2_bd, w2_neg, w3t_l, w3t_r, wet, wu_a1, wu_a2, wu_f, wpm, w_g2, dg]

        turn_plan = []

        block = ctx.enter_context(nc.Block())

        ALL = 64 * PAIRS

        def again(wait, s, count, i):
            if not (isinstance(i, int) and i == 0):
                wait(s, count * i)

        def over_pairs(eng, body, last=PAIRS):
            body(0)
            with eng.Fori(1, last) as i:
                body(i)

        @block.sync
        def _(sp):
            def hold(s, v):
                sp.wait_ge(s, v)
                sp.sem_inc(s_tick_sp, 1)

            def after(steps, i, name, g=0):
                hold(steps.sem, steps.at(i, name, g))

            sp.wait_ge(s_keym, 1)
            for s, a in ((0, dst), (1, src)):
                sp.dma_start(keys[0:full, s, :], a[0:full * SF].rearrange("(p f) -> p f", f=SF)).then_inc(s_keyl, 16)
                sp.dma_start(keys[full:full + 1, s, 0:rest], a[full * SF:E].rearrange("(p f) -> p f", p=1)).then_inc(s_keyl, 16)
            sp.dma_start(kidx[:, :, :], k_idx).then_inc(s_keyl, 16)
            sp.dma_start(ksign[:, :, :], k_sign).then_inc(s_keyl, 16)
            sp.wait_ge(s_wzero, len(zeroed))
            for d, s in wloads:
                sp.dma_start(d, s).then_inc(s_wload, 16)
            sp.dma_start(EC[:, 0:2 * C], ea128).then_inc(s_ec, 16)
            sp.dma_start(EC[:, 2 * C:2 * C + 4], ea4).then_inc(s_ec, 16)
            sp.dma_start(EC[:, 2 * C + 4:EW], src_f).then_inc(s_ec, 16)

            sp.wait_ge(s_const, 3)
            per = N // P * C
            x3_rows = X3[0:P * (N // P), :].rearrange("(p r) c -> p (r c)", p=P)
            sp.dma_start(x3_rows[:, 0:per // CH * CH].rearrange("p (a b) -> p a b", b=CH),
                         zeros[:, :].unsqueeze(1).broadcast_to([P, per // CH, CH])).then_inc(s_x3z, 16)
            sp.dma_start(x3_rows[:, per // CH * CH:per], zeros[:, 0:per % CH]).then_inc(s_x3z, 16)
            sp.dma_start(X3[P * (N // P):N, :], zeros[0:N % P, 0:C]).then_inc(s_x3z, 16)

            with sp.Fori(0, ROWS1) as j:
                after(d1_dve, j - 1, "y")
                sp.dma_start(d1x[:, :, :], rows1(x, j, False)).then_inc(s_d1l, 16)
                after(d1_dve, j, "norm")
                sp.dma_start(rows1(T, j, False), d1o[:, :, :]).then_inc(s_d1o, 16)
            sp.wait_ge(s_d1o, 16 * ROWS1)
            sp.dma_start(d1x[0:TAIL1, 0:1, :], rows1(x, 0, True)).then_inc(s_d1l, 16)
            after(d1_dve, ROWS1, "norm")
            sp.dma_start(rows1(T, 0, True), d1o[0:TAIL1, 0:1, :]).then_inc(s_d1o, 16)
            sp.wait_ge(s_d1o, 16 * (ROWS1 + 1))

            sp.wait_ge(s_kd, 1)
            for s in range(2):
                sp.dma_start(KD[s, 1:SN + 1].rearrange("(p f) -> p f", p=P), sf[0][:, s, :]).then_inc(s_kr, 16)
                sp.dma_start(KD[s:s + 1, 0:1], edge_col[0:1, 0:1]).then_inc(s_kr, 16)
                sp.dma_start(KD[s:s + 1, SN + 1:SN + 2], edge_col[0:1, 1:2]).then_inc(s_kr, 16)
            sp.wait_ge(s_kr, 6 * 16)
            for s in range(2):
                sp.dma_start(sf[1][:, s, :], KD[s, 0:SN].rearrange("(p f) -> p f", p=P)).then_inc(s_kr, 16)
                sp.dma_start(sf[2][:, s, :], KD[s, 2:SN + 2].rearrange("(p f) -> p f", p=P)).then_inc(s_kr, 16)
            sp.wait_ge(s_kd, 2)
            for s in range(2):
                sp.dma_start(MK[s, 0:SN].rearrange("(p f) -> p f", p=P), sf[3][:, s, :]).then_inc(s_mk, 16)
            sp.wait_ge(s_mk, 32)
            sp.wait_ge(s_idx, 7)

            def stage(tile, g, row, i, done):
                sp.dma_start(tile, idx[:, row, bass.ds((2 * i + g) * 4, 4)]).then_inc(done[g], 16)

            def heads(L, row, i):
                for g in G:
                    again(hold, L.sca[g], 64, i)
                    stage(sst[:, g, :], g, row, i, L.sst)

            def load_mask(L, g, s, i):
                sp.dma_start(mk[:, g, 0:CH], MK[s, bass.ds((2 * i + g) * CH, CH)].partition_broadcast(P)).then_inc(L.mk[g], 16)

            def rows_of(table, i, g):
                return table[bass.ds((2 * i + g) * P, P), :].rearrange("p (t k) -> p t k", t=4)

            def l0_in(i):
                for g in G:
                    again(hold, ec_sem[g], 64, i)
                    stage(pst[:, g, :], g, I_PERMD, i, psg0)
                for g in G:
                    again(hold, L0.gat[g], 128, i)
                    stage(gst[:, g, 0, :], g, I_DSTC, i, L0.gst)
                for g in G:
                    after(L0.dve, i - 1, "agg", g)
                    load_mask(L0, g, 0, i)

            def l0(i):
                l0_in(i + 1)
                heads(L0, I_DSTH, i)
            l0_in(0)
            over_pairs(sp, l0, PAIRS - 1)
            heads(L0, I_DSTH, PAIRS - 1)
            for g in G:
                sp.wait_ge(L0.sca[g], ALL)

            def l1_in(i):
                for g in G:
                    again(hold, dl_sem[g], 64, i)
                    stage(pst[:, g, :], g, I_PERMS, i, psg1)
                for g in G:
                    again(hold, L1.gat[g], 128, i)
                    stage(gst[:, g, 0, :], g, I_SRCC, i, L1.gst)
                for g in G:
                    after(L1.dve, i - 1, "num", g)
                    load_mask(L1, g, 1, i)

            def l1_out(i):
                for g in G:
                    after(L1.act, i, "out", g)
                    after(L1.dve, i, "flag", g)
                    sp.dma_start(rows_of(H1, i, g), ot[:, g, :, :]).then_inc(h1_sem[g], 16)

            def l1(i):
                l1_in(i + 1)
                l1_out(i)
            l1_in(0)
            over_pairs(sp, l1, PAIRS - 1)
            l1_out(PAIRS - 1)
            for g in G:
                sp.wait_ge(h1_sem[g], 16 * PAIRS)

            def l1_scatter(i):
                for g in G:
                    again(hold, L1.sca[g], 64, i)
                    sp.dma_start(ot[:, g, :, :], rows_of(H1, i, g)).then_inc(L1.sst[g], 16)
                    stage(sst[:, g, :], g, I_SRCH, i, L1.sst)
            over_pairs(sp, l1_scatter)
            for g in G:
                sp.wait_ge(L1.sca[g], ALL)

            def dense_in(i, last=False):
                for g in G:
                    after(D_act, i - 1, "pack", g)
                    n = LASTP if last and g else P
                    sp.dma_start(dn[0:n, g, :, :], dense_rows(2 * i + g, T, last and g)).then_inc(dn_sem[g], 16)

            def dense_out(i, last=False):
                for g in G:
                    after(D_act, i, "out", g)
                    n = LASTP if last and g else P
                    sp.dma_start(dense_rows(2 * i + g, out, last and g), do[0:n, g, :, :]).then_inc(do_sem[g], 16)

            def dense(i):
                dense_in(i + 1)
                dense_out(i)
            dense_in(0)
            over_pairs(sp, dense, DPAIRS - 2)
            dense_in(DPAIRS - 1, True)
            dense_out(DPAIRS - 2)
            dense_out(DPAIRS - 1, True)
            for g in G:
                sp.wait_ge(do_sem[g], 16 * DPAIRS)

            def l2_in(i):
                for g in G:
                    again(hold, L2.gat[g], 128, i)
                    after(L2.dve, i - 1, "srcf", g)
                    stage(gst[:, g, 0, :], g, I_DSTC, i, L2.gst)
                    stage(gst[:, g, 1, :], g, I_SRCD, i, L2.gst)
                for g in G:
                    after(L2.dve, i - 1, "agg", g)
                    load_mask(L2, g, 0, i)

            def l2_out(i):
                heads(L2, I_DSTH, i)
                for g in G:
                    after(L2.act, i, "out", g)
                    sp.dma_start(rows_of(H3, i, g), ot3[:, g, :, C:P]).then_inc(h3_sem[g], 16)

            def l2(i):
                l2_in(i + 1)
                l2_out(i)
            l2_in(0)
            over_pairs(sp, l2, PAIRS - 1)
            l2_out(PAIRS - 1)
            for g in G:
                sp.wait_ge(h3_sem[g], 16 * PAIRS)
                sp.wait_ge(L2.sca[g], ALL)

            def l3_in(i):
                for g in G:
                    after(L3.pe, i - 1, "ea", g)
                    sp.dma_start(gat[:, g, :, C:P], rows_of(H3, i, g)).then_inc(L3.gst[g], 16)
                    stage(gst[:, g, 0, :], g, I_DSTR, i, L3.gst)
                    stage(gst[:, g, 1, :], g, I_SRCF, i, L3.gst)
                    sp.dma_start(eas[:, g, :, :], ea4d[:, bass.ds((2 * i + g) * 4, 4), :]).then_inc(eal_sem[g], 16)
                for g in G:
                    after(L3.dve, i - 1, "mx", g)
                    load_mask(L3, g, 0, i)

            def l3(i):
                l3_in(i + 1)
                heads(L3, I_DSTH, i)
            l3_in(0)
            over_pairs(sp, l3, PAIRS - 1)
            heads(L3, I_DSTH, PAIRS - 1)
            for g in G:
                sp.wait_ge(L3.sca[g], ALL)

        @block.gpsimd
        def _(pool):
            for a in zeroed:
                pool.memset(a[(slice(None),) * len(a.shape)], 0.0).then_inc(s_wzero, 1)
            def hold(s, v):
                pool.wait_ge(s, v)
                pool.sem_inc(s_tick_pool, 1)

            def hold_after(steps, i, name, g=0):
                hold(steps.sem, steps.at(i, name, g))

            node_bound = pool.to_reg(N - 1)

            def gather(dest, table, index, done):
                pool.indirect_dma_start(out=dest, out_offset=None, in_=table,
                                        in_offset=bass.IndirectOffsetOnAxis(ap=index, axis=0),
                                        bounds_check=node_bound, oob_is_err=False).then_inc(done, 16)

            def scatter(table, index, source, done):
                pool.indirect_dma_start(out=table, out_offset=bass.IndirectOffsetOnAxis(ap=index, axis=0),
                                        in_=source, in_offset=None,
                                        bounds_check=node_bound, oob_is_err=False).then_inc(done, 16)

            pool.wait_ge(s_ec, 48)

            def edge_rows(i):
                for g in G:
                    hold(psg0[g], 16 * (i + 1))
                    hold_after(L0.pe, i - 1, "ea", g)
                    hold_after(L0.dve, i - 1, "meta", g)
                    for t in range(4):
                        gather(eca[:, g, t, :], EC, pst[:, g, t:t + 1], ec_sem[g])

            def gathers0(i):
                for g in G:
                    hold(L0.gst[g], 16 * (i + 1))
                    hold_after(L0.pe, i - 1, "z", g)
                    for t in range(4):
                        gather(gat[:, g, t, 0:C], x, gst[:, g, 0, t:t + 1], L0.gat[g])
                    hold(ec_sem[g], 64 * (i + 1))
                    for t in range(4):
                        gather(gat[:, g, t, C:P], x, eca[:, g, t, EW - 1:EW].bitcast(U32), L0.gat[g])

            def scatters0(i):
                for g in G:
                    hold_after(L0.act, i, "out", g)
                    hold(L0.sst[g], 16 * (i + 1))
                    for t in range(4):
                        scatter(T, sst[:, g, t:t + 1], ot[:, g, t, :], L0.sca[g])

            edge_rows(0)
            gathers0(0)
            edge_rows(1)
            gathers0(1)
            pool.wait_ge(s_d1o, 16 * (ROWS1 + 1))
            with pool.Fori(2, PAIRS) as i:
                edge_rows(i)
                scatters0(i - 2)
                gathers0(i)
            scatters0(PAIRS - 2)
            scatters0(PAIRS - 1)
            for g in G:
                pool.wait_ge(L0.sca[g], ALL)

            def dst_rows(i):
                for g in G:
                    hold(psg1[g], 16 * (i + 1))
                    again(hold, L1.gat[g], 128, i)
                    for t in range(4):
                        gather(dli[:, g, t:t + 1], dst_r, pst[:, g, t:t + 1], dl_sem[g])

            def gathers1(i):
                for g in G:
                    hold(L1.gst[g], 16 * (i + 1))
                    hold_after(L1.act, i - 1, "pack", g)
                    hold_after(L1.dve, i - 1, "flag", g)
                    for t in range(4):
                        gather(gat[:, g, t, 0:TW], T, gst[:, g, 0, t:t + 1], L1.gat[g])
                    hold(dl_sem[g], 64 * (i + 1))
                    for t in range(4):
                        gather(gat[:, g, t, TW:2 * TW], T, dli[:, g, t:t + 1].bitcast(U32), L1.gat[g])

            def l1(i):
                gathers1(i)
                dst_rows(i + 1)
            dst_rows(0)
            over_pairs(pool, l1, PAIRS - 1)
            gathers1(PAIRS - 1)

            def scatters1(i):
                for g in G:
                    hold(L1.sst[g], 32 * (i + 1))
                    for t in range(4):
                        scatter(T, sst[:, g, t:t + 1], ot[:, g, t, :], L1.sca[g])
            over_pairs(pool, scatters1)
            for g in G:
                pool.wait_ge(L1.sca[g], ALL)

            def gathers2(i):
                for g in G:
                    hold(L2.gst[g], 32 * (i + 1))
                    hold_after(L2.act, i - 1, "pack", g)
                    hold_after(L2.pe, i - 1, "norm", g)
                    hold_after(L2.dve, i - 1, "fsel", g)
                    for t in range(4):
                        gather(gat[:, g, t, 0:TW], T, gst[:, g, 0, t:t + 1], L2.gat[g])
                        gather(gat[:, g, t, TW:2 * TW], T, gst[:, g, 1, t:t + 1], L2.gat[g])

            def scatters2(i):
                for g in G:
                    hold_after(L2.act, i, "out", g)
                    hold(L2.sst[g], 16 * (i + 1))
                    for t in range(4):
                        scatter(X3, sst[:, g, t:t + 1], ot3[:, g, t, 0:C], L2.sca[g])

            def l2(i):
                gathers2(i + 1)
                scatters2(i)
            pool.wait_ge(s_x3z, 48)
            gathers2(0)
            over_pairs(pool, l2, PAIRS - 1)
            scatters2(PAIRS - 1)
            for g in G:
                pool.wait_ge(L2.sca[g], ALL)

            for g in G:
                pool.wait_ge(do_sem[g], 16 * DPAIRS)

            def gathers3(i):
                for g in G:
                    hold(L3.gst[g], 48 * (i + 1))
                    hold_after(L3.pe, i - 1, "z", g)
                    for t in range(4):
                        gather(gat[:, g, t, 0:C], X3, gst[:, g, 0, t:t + 1], L3.gat[g])
                        gather(gat[:, g, t, C:P], X3, gst[:, g, 1, t:t + 1], L3.gat[g])

            def scatters3(i):
                for g in G:
                    hold_after(L3.act, i, "out", g)
                    hold(L3.sst[g], 16 * (i + 1))
                    for t in range(4):
                        scatter(out, sst[:, g, t:t + 1], ot3[:, g, t, 0:C], L3.sca[g])

            def l3(i):
                gathers3(i + 1)
                scatters3(i)
            gathers3(0)
            over_pairs(pool, l3, PAIRS - 1)
            scatters3(PAIRS - 1)
            for g in G:
                pool.wait_ge(L3.sca[g], ALL)

        blk = [slice(128 * t, 128 * (t + 1)) for t in range(4)]

        @block.vector
        def _(dve):
            H = slice(0, C)
            U = slice(C, P)

            def after_(steps, i, name, g=0):
                dve.wait_ge(steps.sem, steps.at(i, name, g))

            def tt(done, out_, a, b, op):
                dve.tensor_tensor(out_, a, b, op).then_inc(done, 1)

            def ts(done, out_, a, s1, s2, op0, op1=None):
                if op1 is None:
                    dve.tensor_scalar(out_, a, s1, None, op0).then_inc(done, 1)
                else:
                    dve.tensor_scalar(out_, a, s1, s2, op0, op1).then_inc(done, 1)

            def stt(done, out_, a, s, b, op0, op1):
                dve.scalar_tensor_tensor(out=out_, in0=a, scalar=s, in1=b, op0=op0, op1=op1).then_inc(done, 1)

            def scan(done, out_, d0, d1, initial, op0, op1):
                dve.tensor_tensor_scan(out=out_, data0=d0, data1=d1, initial=initial, op0=op0, op1=op1).then_inc(done, 1)

            for S in (d1_dve, L0.dve, L1.dve, L2.dve, L3.dve, D_dve):
                dve.sem_inc(S.sem, S.n)

            dve.memset(keys[:, :, :], N).then_inc(s_keym, 1)
            dve.memset(eps_col[:, :], EPS).then_inc(s_const, 1)
            dve.memset(one_col[:, :], 1.0).then_inc(s_const, 1)
            dve.memset(sgn_col[0:C, :], -1.0)
            dve.memset(sgn_col[C:P, :], 1.0)
            for a in (gat, ot, ot3, dn):
                dve.memset(a[:, :, :, :], 0.0)
            dve.memset(ones[:, :], 1.0)
            dve.memset(zeros[:, :], 0.0)
            for a in sc:
                dve.memset(a[:, :, :], 0.0)
            for g in G:
                dve.memset(negm[g][:, CH:CH + 1], 0.0)
            dve.memset(edge_col[0:1, 0:1], -1.0)
            dve.memset(edge_col[0:1, 1:2], -2.0)
            dve.memset(d1o[:, :, C:TW], 0.0).then_inc(s_const, 1)

            setup = Count(s_wd)
            dve.wait_ge(s_wload, NW)
            dve.wait_ge(s_const, 3)
            for a in (w_fs_z[:, 0:C], w_fs_e[:, 0:C], b_fs[0:C, :]):
                setup.tick(dve.tensor_scalar(a, a, -1.0, None, ALU.mult))
            setup.tick(dve.memset(ot[:, :, :, TW - 1:TW], 1.0))
            for k in range(2):
                setup.tick(dve.tensor_scalar(att_m[:, k, :], headmask[0:C, 0:C], att[:, k:k + 1], None, ALU.mult))
            dve.memset(avgmat[:, :], 1.0 / N).then_inc(s_wdve, 1)
            dve.wait_ge(s_wact, 1)
            dve.reduce_sum(nvs[:, :], nv[:, :], AX_X).then_inc(s_wdve, 1)
            dve.wait_ge(s_wd, setup.n)
            dve.tensor_scalar(w2_neg[C:P, 0:C], w2_bd[C:P, C:P], -1.0, None, ALU.mult).then_inc(s_wdve, 1)
            for a in (wp_a2[0:C, :], wu_a2[0:C, C:P]):
                setup.tick(dve.tensor_scalar(a, a, -1.0, None, ALU.mult))
            for h in (0, C):
                setup.tick(dve.tensor_copy(wu_f[h:h + C, C:P], ident[h:h + C, h:h + C]))
            setup.tick(dve.tensor_tensor(bsum[:, :], brow[:, 0, :], brow[:, 1, :], ALU.add))
            dve.wait_ge(s_wd, setup.n)
            setup.tick(dve.tensor_copy(b_g1[0:C, :], bsum[0:C, 1:2]))
            setup.tick(dve.tensor_copy(b_g1[C:P, :], bsum[C:P, 0:1]))
            dve.wait_ge(s_wpe, 1)
            setup.tick(dve.tensor_copy(w_score[:, :], psum[0][:, 0:C]))
            setup.tick(dve.tensor_copy(w_h[:, :], psum[1][:, 0:P]))
            setup.tick(dve.tensor_copy(w_hea[:, :], psum[2][0:4, 0:P]))
            setup.tick(dve.tensor_copy(bew_col[:, :], psum[2][:, 256:257]))
            setup.tick(dve.tensor_copy(wu_x[:, :], psum[3][0:C, 0:P]))
            setup.tick(dve.tensor_copy(avg[:, :], psum[4][:, 0:1]))
            setup.tick(dve.reciprocal(iavg[:, :], psum[4][:, 0:1]))
            dve.wait_ge(s_wact, 4)
            dve.wait_ge(s_wd, setup.n)
            setup.tick(dve.tensor_scalar(fac0[:, 2:3], fac0[:, 1:2], iavg[0:C, :], None, ALU.mult))
            setup.tick(dve.reciprocal(fac0[:, 3:4], fac0[:, 1:2]))
            dve.wait_ge(s_wd, setup.n)
            setup.tick(dve.tensor_scalar(fac0[:, 5:6], fac0[:, 2:3], fac0[:, 4:5], None, ALU.mult))
            setup.tick(dve.tensor_scalar(fac0[:, 7:8], fac0[:, 3:4], avg[0:C, :], None, ALU.mult))
            dve.wait_ge(s_wd, setup.n)
            dve.tensor_scalar(fac0[:, 6:7], fac0[:, 7:8], fac0[:, 5:6], None, ALU.mult).then_inc(s_wdve, 1)
            setup.tick(dve.tensor_copy(mmt2[:, 0:C], psum[3][0:C, 256:256 + C]))
            setup.tick(dve.tensor_copy(mmt2[:, C:P], psum[3][0:C, 256:256 + C]))
            dve.wait_ge(s_wd, setup.n)
            dve.wait_ge(s_wpe, 2)
            dve.tensor_tensor(out0[:, :], psum[5][0:C, 0:1], bpost_col[0:C, :], ALU.add).then_inc(s_wdve, 1)
            dve.wait_ge(s_wpe, 3)
            for g in range(2):
                setup.tick(dve.tensor_scalar(dg_b[:, g:g + 1], psum[6][:, 8 * g:8 * g + 1], bsum[:, g:g + 1], None, ALU.add))
            setup.tick(dve.tensor_scalar(dg_b[:, 2:3], psum[6][:, 16:17], brow[:, 0, 2:3], None, ALU.add))
            setup.tick(dve.tensor_copy(dg_b[:, 3:4], brow[:, 1, 2:3]))
            for h in (0, C):
                r = slice(h, h + C)
                for g in range(2):
                    setup.tick(dve.tensor_tensor(dg[r, g, r], psum[7][r, g * C:(g + 1) * C], whh2[r, g * C:(g + 1) * C], ALU.add))
                setup.tick(dve.tensor_copy(dg[r, 2, r], psum[7][r, 2 * C:3 * C]))
                setup.tick(dve.tensor_copy(dg[r, 3, r], whh2[r, 2 * C:3 * C]))
            dve.wait_ge(s_wd, setup.n)

            def dense1(j, r=R1, n=P):
                o = d1o[0:n, 0:r, 0:C]
                dve.wait_ge(d1_act.sem, d1_act.at(j, "relu"))
                again(dve.wait_ge, s_d1o, 16, j)
                tt(d1_dve.done("y"), o, d1x[0:n, 0:r, :], d1r[0:n, 0:r, :], ALU.add)
                after_(d1_dve, j, "y")
                dve.reduce_sum(d1s[0:n, 0, 0:r], o, AX_X).then_inc(d1_dve.done("sum"), 1)
                after_(d1_dve, j, "sum")
                ts(d1_dve.done("mean"), d1s[0:n, 0, 0:r], d1s[0:n, 0, 0:r], 1.0 / C, None, ALU.mult)
                after_(d1_dve, j, "mean")
                tt(d1_dve.done("centered"), o, o, d1s[0:n, 0, 0:r].unsqueeze(2).broadcast_to([n, r, C]), ALU.subtract)
                after_(d1_act, j, "square")
                dve.reduce_sum(d1s[0:n, 1, 0:r], d1r[0:n, 0:r, :], AX_X).then_inc(d1_dve.done("sumsq"), 1)
                after_(d1_act, j, "rstd")
                tt(d1_dve.done("norm"), o, o, d1s[0:n, 3, 0:r].unsqueeze(2).broadcast_to([n, r, C]), ALU.mult)
            dense1(0)
            with dve.Fori(1, ROWS1) as j:
                dense1(j)
            dense1(ROWS1, 1, TAIL1)

            cnt_ = Count(s_sort)

            def go(ins):
                cnt_.tick(ins)
                dve.wait_ge(s_sort, cnt_.n)

            dve.wait_ge(s_keyl, 96)
            f = [a[:, :, :] for a in sf]
            i_ = [a[:, :, :] for a in si]
            go(dve.tensor_copy(f[0], keys[:, :, :]))
            go(dve.tensor_scalar(f[1], f[0], MID, None, ALU.subtract))
            go(dve.tensor_scalar(f[2], f[0], MID, None, ALU.is_lt))
            go(dve.scalar_tensor_tensor(out=f[5], in0=f[1], scalar=-1.0, in1=f[1], op0=ALU.mult, op1=ALU.max))
            go(dve.tensor_scalar(i_[0], f[5], MARGIN, None, ALU.add))
            go(dve.tensor_scalar(f[3], kidx[:, :, :], -2.0, float(SN - 1), ALU.mult, ALU.add))
            go(dve.tensor_tensor(f[4], f[3], f[2], ALU.mult))
            go(dve.tensor_tensor(i_[1], f[4], kidx[:, :, :], ALU.add))
            go(dve.tensor_copy(i_[2], f[2]))
            go(dve.tensor_scalar(i_[0], i_[0], SK, None, ALU.logical_shift_left))
            go(dve.tensor_scalar(i_[2], i_[2], 31, None, ALU.logical_shift_left))
            go(dve.tensor_tensor(i_[0], i_[0], i_[1], ALU.bitwise_or))
            go(dve.tensor_tensor(sx[:, :, :].bitcast(I32), i_[0], i_[2], ALU.bitwise_or))
            cur, oth = sx, sy
            turns = 0

            def compare(view, d):
                nonlocal cur, oth
                a, b = view(cur, d), view(oth, d)
                cnt_.tick(dve.tensor_tensor(b[:, :, 0, :], a[:, :, 0, :], a[:, :, 1, :], ALU.min))
                go(dve.tensor_tensor(b[:, :, 1, :], a[:, :, 0, :], a[:, :, 1, :], ALU.max))
                cur, oth = oth, cur

            def view(a, d):
                return a[:, :, :].rearrange("p s (n two d) -> p (s n) two d", two=2, d=d)

            def view_t(a, d):
                return a[:, :, :].rearrange("p s (h n two d) -> p (s h n) two d", h=2, two=2, d=d)

            def turn():
                nonlocal cur, oth, turns
                turn_plan.append((cur, cnt_.n))
                turns += 1
                dve.wait_ge(s_sortt, turns)
                go(dve.tensor_copy(oth[:, :, :].rearrange("p s f -> p (s f)"), psum[0][:, :]))
                cur, oth = oth, cur

            for k in range(1, SK + 1):
                cnt_.tick(dve.tensor_tensor(oth[:, 0, :], cur[:, 0, :], ksign[:, k - 1, :], ALU.mult))
                go(dve.tensor_tensor(oth[:, 1, :], cur[:, 1, :], ksign[:, k - 1, :], ALU.mult))
                cur, oth = oth, cur
                if k > 8:
                    turn()
                    for b in range(k - 9, -1, -1):
                        compare(view_t, 1 << b)
                    turn()
                for b in range(min(k, 8) - 1, -1, -1):
                    compare(view, 1 << b)

            bits = cur[:, :, :].bitcast(I32)
            go(dve.tensor_scalar(i_[0], bits, SK, 0xFFFF, ALU.logical_shift_right, ALU.bitwise_and))
            go(dve.tensor_scalar(i_[1], bits, SN - 1, None, ALU.bitwise_and))
            go(dve.tensor_scalar(i_[2], bits, 31, 1, ALU.logical_shift_right, ALU.bitwise_and))
            go(dve.tensor_scalar(f[1], i_[0], MARGIN, None, ALU.subtract))
            go(dve.tensor_copy(f[2], i_[2]))
            go(dve.tensor_scalar(f[3], f[2], -2.0, 1.0, ALU.mult, ALU.add))
            go(dve.tensor_tensor(f[4], f[1], f[3], ALU.mult))
            go(dve.tensor_copy(f[5], i_[1]))
            go(dve.tensor_scalar(f[3], f[5], -2.0, float(SN - 1), ALU.mult, ALU.add))
            go(dve.tensor_tensor(f[3], f[3], f[2], ALU.mult))
            go(dve.tensor_tensor(f[5], f[5], f[3], ALU.add))
            for s, k in ((0, I_PERMD), (1, I_PERMS)):
                go(dve.tensor_scalar(lists[:, k, :], sf[5][:, s, :], float(E - 1), None, ALU.min))
            dve.tensor_scalar(f[0], f[4], MID, None, ALU.add).then_inc(s_kd, 1)
            dve.wait_ge(s_kd, 1)
            dve.wait_ge(s_kr, 160)
            dve.tensor_tensor(f[3], f[0], f[1], ALU.is_equal).then_inc(s_kd, 1)
            go(dve.tensor_tensor(f[4], f[0], f[2], ALU.is_equal))
            for s, k in ((0, I_DSTC), (1, I_SRCC)):
                go(dve.tensor_scalar(lists[:, k, :], sf[0][:, s, :], float(N - 1), None, ALU.min))
            go(dve.tensor_copy(lists[:, I_DSTR, :], sf[0][:, 0, :]))
            for s, k in ((0, I_DSTH), (1, I_SRCH)):
                ins = dve.scalar_tensor_tensor(out=lists[:, k, :], in0=sf[4][:, s, :], scalar=float(SKIP),
                                               in1=sf[0][:, s, :], op0=ALU.mult, op1=ALU.add)
                go(ins)
            dve.sem_inc(s_lists, 1)
            for k in range(7):
                dve.wait_ge(s_lt, k + 1)
                dve.tensor_copy(idx[:, k, :].rearrange("q (p h) -> q h p", h=2),
                                psum[k][:, 0:2 * P].rearrange("q (h p) -> q h p", h=2)[:, :, 0:NT // 2]).then_inc(s_idx, 1)

            def last_of(a, par, rows):
                return a[rows, 1 - par, CH - 1:CH]

            def l0(i):
                L = L0
                for g in G:
                    after_(L.pe, i, "ea", g)
                    after_(L.pe, i - 1, "fs", g)
                    dve.tensor_copy(ear[g][:, :], ps[g][1][:, :]).then_inc(L.dve.done("ea"), 1)
                for g in G:
                    dve.wait_ge(ec_sem[g], 64 * (i + 1))
                    dve.tensor_copy(ea4d[:, bass.ds((2 * i + g) * 4, 4), :], eca[:, g, :, 2 * C:2 * C + 4])
                    dve.tensor_copy(idx[:, I_SRCD, bass.ds((2 * i + g) * 4, 4)],
                                    eca[:, g, :, EW - 1].bitcast(U32)).then_inc(L.dve.done("meta"), 1)
                for g in G:
                    after_(L.pe, i, "fs", g)
                    after_(L.act, i, "sabs", g)
                    after_(L.dve, i - 1, "core", g)
                    ts(L.dve.done("srelu"), w[g][6][:, :], ps[g][2][:, :], b_fs[:, :], 0.0, ALU.add, ALU.max)
                for g in G:
                    after_(L.act, i, "log", g)
                    after_(L.dve, i, "srelu", g)
                    after_(L.act, i - 1, "gate", g)
                    tt(L.dve.done("core"), w[g][9][:, :], w[g][6][:, :], w[g][2][:, :], ALU.add)
                for g in G:
                    after_(L.act, i, "gate", g)
                    after_(L.dve, i, "core", g)
                    tt(L.dve.done("msg"), w[g][10][H, :], w[g][9][U, :], w[g][8][U, :], ALU.mult)
                for g in G:
                    dve.wait_ge(L.mk[g], 16 * (i + 1))
                    after_(L.dve, i, "msg", g)
                    after_chunk_before(dve.wait_ge, L.dve, i, "agg", g)
                    scan(L.dve.done("agg"), sc[0][H, g, :], mk[H, g, 0:CH], w[g][10][H, :], last_of(sc[0], g, H), ALU.mult, ALU.add)
                for g in G:
                    after_(L.dve, i, "agg", g)
                    after_(L.act, i, "z", g)
                    tt(L.dve.done("t"), w[g][11][H, :], sc[0][H, g, :], z[g][H, :], ALU.add)
                for g in G:
                    after_(L.dve, i, "t", g)
                    after_(L.pe, i - 1, "center", g)
                    stt(L.dve.done("y"), w[g][12][H, :], w[g][11][H, :], 0.0, z[g][H, :], ALU.max, ALU.add)
                for g in G:
                    after_(L.act, i, "rstd", g)
                    after_(L.pe, i - 1, "out", g)
                    tt(L.dve.done("x1"), w[g][13][H, :], ps[g][3][H, :], w[g][5][H, :], ALU.mult)
            over_pairs(dve, l0)

            def l1(i):
                L = L1
                for g in G:
                    dve.wait_ge(L.mk[g], 16 * (i + 1))
                    after_(L.pe, i - 1, "out", g)
                    after_chunk_before(dve.wait_ge, L.dve, i, "cnt", g)
                    scan(L.dve.done("cnt"), sc[3][C:C + 1, g, :], mk[C:C + 1, g, 0:CH], ones[C:C + 1, :],
                         sc[3][C:C + 1, 1 - g, CH - 1:CH], ALU.mult, ALU.add)
                for g in G:
                    after_(L.act, i, "lrelu", g)
                    after_(L.dve, i - 1, "d", g)
                    tt(L.dve.done("e"), w[g][1][H, :], ps[g][1][H, :], w[g][0][H, :], ALU.max)
                for g in G:
                    after_(L.dve, i, "e", g)
                    after_(L.act, i, "negm", g)
                    after_chunk_before(dve.wait_ge, L.dve, i, "dcar", g)
                    scan(L.dve.done("mrun"), sc[0][H, g, :], negm[g][H, 0:CH], w[g][1][H, :], last_of(sc[0], g, H), ALU.add, ALU.max)
                    after_(L.dve, i, "mrun", g)
                    scan(L.dve.done("mseg"), w[g][3][H, ::-1], negm[g][H, CH:0:-1], sc[0][H, g, ::-1], -BIG, ALU.add, ALU.max)
                    after_(L.dve, i, "mseg", g)
                    after_(L.act, i - 1, "carry", g)
                    ts(L.dve.done("dcar"), sm[g][H, 0:1], last_of(sc[0], g, H), w[g][3][H, 0:1], 0.0, ALU.subtract, ALU.min)
                for g in G:
                    after_(L.dve, i, "mseg", g)
                    after_(L.act, i - 1, "ex", g)
                    tt(L.dve.done("d"), w[g][4][H, :], w[g][1][H, :], w[g][3][H, :], ALU.subtract)
                for g in G:
                    again(dve.wait_ge, h1_sem[g], 16, i)
                    dve.wait_ge(L.gat[g], 128 * (i + 1))
                    dve.tensor_copy(ot[:, g, :, TW - 1:TW], gat[:, g, :, TW - 1:TW]).then_inc(L.dve.done("flag"), 1)
                for g in G:
                    after_(L.pe, i, "xp", g)
                    after_(L.act, i, "ex", g)
                    after_(L.dve, i - 1, "num", g)
                    tt(L.dve.done("val"), w[g][7][H, :], ps[g][2][H, :], w[g][5][H, :], ALU.mult)
                for g in G:
                    after_chunk_before(dve.wait_ge, L.dve, i, "num", g)
                    after_(L.act, i, "carry", g)
                    tt(s_l1_c, sm[g][H, 2:3], last_of(sc[1], g, H), sm[g][H, 1:2], ALU.mult)
                    tt(L.dve.done("carry"), sm[g][H, 3:4], last_of(sc[2], g, H), sm[g][H, 1:2], ALU.mult)
                    after_(L.dve, i, "carry", g)
                    after_(L.act, i, "ex", g)
                    dve.wait_ge(L.mk[g], 16 * (i + 1))
                    scan(L.dve.done("den"), sc[1][H, g, :], mk[H, g, 0:CH], w[g][5][H, :], sm[g][H, 2:3], ALU.mult, ALU.add)
                    after_(L.dve, i, "carry", g)
                    after_(L.dve, i, "val", g)
                    scan(L.dve.done("num"), sc[2][H, g, :], mk[H, g, 0:CH], w[g][7][H, :], sm[g][H, 3:4], ALU.mult, ALU.add)
                for g in G:
                    after_(L.dve, i, "den", g)
                    ts(L.dve.done("dmax"), w[g][8][H, :], sc[1][H, g, :], 1e-30, None, ALU.max)
                for g in G:
                    after_(L.dve, i, "dmax", g)
                    dve.reciprocal(w[g][9][H, :], w[g][8][H, :]).then_inc(L.dve.done("rden"), 1)
                for g in G:
                    after_(L.dve, i, "rden", g)
                    tt(L.dve.done("att"), w[g][10][H, :], sc[2][H, g, :], w[g][9][H, :], ALU.mult)
                for g in G:
                    after_(L.dve, i, "att", g)
                    after_(L.pe, i - 1, "out", g)
                    after_(L.act, i, "z", g)
                    tt(L.dve.done("v2"), w[g][13][H, :], w[g][10][H, :], z[g][H, :], ALU.add)
            for k in range(2):
                dve.wait_ge(L0.sca[k], ALL)
            over_pairs(dve, l1)

            def dense(i):
                S = D_dve
                for g in G:
                    after_(D_act, i, "r2", g)
                    after_(D_pe, i - 1, "h", g)
                    tt(S.done("x2"), w[g][3][:, :], ps[g][1][:, :], w[g][2][:, :], ALU.mult)
                for g in G:
                    after_(D_act, i, "relu", g)
                    after_(S, i, "x2", g)
                    tt(S.done("y3"), w[g][5][:, :], w[g][3][:, :], w[g][4][:, :], ALU.add)
                for g in G:
                    after_(D_act, i, "r3", g)
                    after_(D_pe, i - 1, "gh", g)
                    tt(S.done("x3"), w[g][6][:, :], ps[g][3][:, :], w[g][2][:, :], ALU.mult)
                for g in G:
                    after_(D_pe, i, "gh", g)
                    after_(D_act, i, "r", g)
                    stt(S.done("q"), w[g][9][:, :], ps[g][3][:, :], dg_b[:, 3:4], w[g][7][:, :], ALU.add, ALU.mult)
                for g in G:
                    after_(S, i, "q", g)
                    tt(S.done("a"), w[g][11][:, :], ps[g][2][:, :], w[g][9][:, :], ALU.add)
                for g in G:
                    after_(D_act, i, "n", g)
                    tt(S.done("xn"), w[g][9][:, :], w[g][6][:, :], w[g][10][:, :], ALU.subtract)
                for g in G:
                    after_(S, i, "xn", g)
                    tt(S.done("zxn"), w[g][9][:, :], w[g][9][:, :], w[g][8][:, :], ALU.mult)
                for g in G:
                    after_(S, i, "zxn", g)
                    tt(S.done("o"), w[g][9][:, :], w[g][9][:, :], w[g][10][:, :], ALU.add)
                for g in G:
                    after_(S, i, "o", g)
                    tt(S.done("y4"), w[g][12][:, :], w[g][9][:, :], w[g][6][:, :], ALU.add)
                for g in G:
                    after_(D_act, i, "r4", g)
                    after_(D_pe, i - 1, "out", g)
                    tt(S.done("x4"), w[g][13][:, :], ps[g][1][:, :], w[g][2][:, :], ALU.mult)
            for k in range(2):
                dve.wait_ge(L1.sca[k], ALL)
            over_pairs(dve, dense, DPAIRS)

            def l2(i):
                L = L2
                S = L.dve
                for g in G:
                    dve.wait_ge(L.mk[g], 16 * (i + 1))
                    after_chunk_before(dve.wait_ge, L.dve, i, "cnt", g)
                    scan(S.done("cnt"), sc[1][U, g, :], mk[U, g, 0:CH], ones[U, :], last_of(sc[1], g, U), ALU.mult, ALU.add)
                for g in G:
                    dve.wait_ge(L.gat[g], 128 * (i + 1))
                    ts(S.done("fsel"), sm[g][:, 4:8], gat[:, g, :, 2 * TW - 1], -float(SKIP), float(SKIP), ALU.mult, ALU.add)
                for g in G:
                    after_(S, i, "fsel", g)
                    dve.wait_ge(L.gst[g], 32 * (i + 1))
                    tt(S.done("srcf"), idx[:, I_SRCF, bass.ds((2 * i + g) * 4, 4)], sm[g][:, 4:8], gst[:, g, 1, :], ALU.add)
                for g in G:
                    after_(L.act, i, "rstd", g)
                    after_(L.pe, i - 1, "h", g)
                    tt(S.done("x2"), w[g][5][:, :], ps[g][1][:, :], w[g][2][:, :], ALU.mult)
                for g in G:
                    after_(L.pe, i, "norm", g)
                    after_(S, i, "x2", g)
                    tt(S.done("msg"), w[g][6][U, :], ps[g][3][U, :], w[g][5][U, :], ALU.mult)
                for g in G:
                    after_(S, i, "msg", g)
                    after_chunk_before(dve.wait_ge, L.dve, i, "agg", g)
                    scan(S.done("agg"), sc[0][U, g, :], mk[U, g, 0:CH], w[g][6][U, :], last_of(sc[0], g, U), ALU.mult, ALU.add)
                for g in G:
                    after_(S, i, "agg", g)
                    after_(L.act, i, "nin", g)
                    tt(S.done("aggn"), w[g][7][U, :], sc[0][U, g, :], w[g][4][U, :], ALU.mult)
                for g in G:
                    after_(L.act, i, "relu", g)
                    after_(L.pe, i - 1, "out", g)
                    tt(S.done("y3"), w[g][9][:, :], w[g][5][:, :], w[g][8][:, :], ALU.add)
            for k in range(2):
                dve.wait_ge(do_sem[k], 16 * DPAIRS)
            over_pairs(dve, l2)

            def l3(i):
                L = L3
                S = L.dve
                for g in G:
                    after_(L.act, i, "rstd", g)
                    after_(L.pe, i - 1, "g2", g)
                    tt(S.done("x3"), w[g][4][:, :], ps[g][2][:, :], w[g][2][:, :], ALU.mult)
                for g in G:
                    dve.wait_ge(L.mk[g], 16 * (i + 1))
                    after_chunk_before(dve.wait_ge, L.dve, i, "cnt", g)
                    scan(S.done("cnt"), sc[3][:, g, :], mk[:, g, 0:CH], ones[:, :], last_of(sc[3], g, slice(0, P)), ALU.mult, ALU.add)
                for g in G:
                    after_(L.pe, i, "h", g)
                    after_(L.act, i - 1, "n", g)
                    ts(S.done("ha"), w[g][5][:, :], ps[g][0][:, :], bew_col[:, :], None, ALU.add)
                for g in G:
                    after_(S, i, "ha", g)
                    after_(L.pe, i, "ew", g)
                    tt(S.done("hw"), w[g][5][:, :], ps[g][1][:, :], w[g][5][:, :], ALU.mult)
                for g in G:
                    after_(L.act, i, "h", g)
                    tt(S.done("hsq"), w[g][8][U, :], w[g][6][U, :], w[g][6][U, :], ALU.mult)
                for g in G:
                    after_(S, i, "hsq", g)
                    after_chunk_before(dve.wait_ge, L.dve, i, "s1", g)
                    scan(S.done("s1"), sc[0][:, g, :], mk[:, g, 0:CH], w[g][6][:, :], last_of(sc[0], g, slice(0, P)), ALU.mult, ALU.add)
                for g in G:
                    after_chunk_before(dve.wait_ge, L.dve, i, "s2", g)
                    scan(S.done("s2"), sc[1][U, g, :], mk[U, g, 0:CH], w[g][8][U, :], last_of(sc[1], g, U), ALU.mult, ALU.add)
                for g in G:
                    after_(L.act, i, "hneg", g)
                    after_(L.act, i, "negm", g)
                    after_chunk_before(dve.wait_ge, L.dve, i, "mx", g)
                    scan(S.done("mx"), sc[2][:, g, :], negm[g][:, 0:CH], w[g][7][:, :], last_of(sc[2], g, slice(0, P)), ALU.add, ALU.max)
                for g in G:
                    after_(S, i, "cnt", g)
                    dve.reciprocal(w[g][15][:, :], sc[3][:, g, :]).then_inc(S.done("rcnt"), 1)
                for g in G:
                    after_(S, i, "rcnt", g)
                    after_(L.pe, i - 1, "u", g)
                    tt(S.done("mean"), w[g][9][:, :], sc[0][:, g, :], w[g][15][:, :], ALU.mult)
                for g in G:
                    after_(S, i, "mean", g)
                    tt(S.done("msq"), w[g][11][U, :], w[g][9][U, :], w[g][9][U, :], ALU.mult)
                for g in G:
                    tt(S.done("ms2"), w[g][12][U, :], sc[1][U, g, :], w[g][15][U, :], ALU.mult)
                for g in G:
                    after_(S, i, "ms2", g)
                    tt(S.done("vard"), w[g][12][U, :], w[g][12][U, :], w[g][11][U, :], ALU.subtract)
                for g in G:
                    after_(S, i, "vard", g)
                    ts(S.done("var"), w[g][12][U, :], w[g][12][U, :], 0.0, None, ALU.max)
                for g in G:
                    after_(L.act, i, "logd", g)
                    ts(S.done("f2"), w[g][16][:, :], w[g][10][:, :], iavg[:, :], None, ALU.mult)
                for g in G:
                    dve.reciprocal(w[g][17][U, :], w[g][10][U, :]).then_inc(S.done("rlog"), 1)
                for g in G:
                    after_(S, i, "rlog", g)
                    stt(S.done("f3"), w[g][16][U, :], w[g][17][U, :], avg[U, :], w[g][16][U, :], ALU.mult, ALU.mult)
                for g in G:
                    after_(S, i, "f3", g)
                    after_(L.pe, i, "p", g)
                    tt(S.done("fp"), w[g][14][:, :], ps[g][2][:, :], w[g][16][:, :], ALU.mult)
                for g in G:
                    after_(L.act, i, "rz", g)
                    after_(L.pe, i, "g2", g)
                    stt(S.done("q"), w[g][15][H, :], ps[g][1][U, :], brow[U, 1, 2:3], w[g][10][U, :], ALU.add, ALU.mult)
                for g in G:
                    after_(S, i, "q", g)
                    tt(S.done("a"), w[g][11][H, :], ps[g][1][H, :], w[g][15][H, :], ALU.add)
                for g in G:
                    after_(L.act, i, "n", g)
                    tt(S.done("xn"), w[g][15][H, :], w[g][4][H, :], w[g][6][H, :], ALU.subtract)
                for g in G:
                    after_(S, i, "xn", g)
                    tt(S.done("zxn"), w[g][15][H, :], w[g][15][H, :], w[g][10][H, :], ALU.mult)
                for g in G:
                    after_(S, i, "zxn", g)
                    tt(S.done("o"), w[g][15][H, :], w[g][15][H, :], w[g][6][H, :], ALU.add)
                for g in G:
                    after_(S, i, "o", g)
                    tt(S.done("y4"), w[g][12][H, :], w[g][15][H, :], w[g][4][H, :], ALU.add)
                for g in G:
                    after_(L.act, i, "rstd4", g)
                    after_(L.pe, i - 1, "out", g)
                    tt(S.done("x4"), w[g][13][H, :], ps[g][2][H, :], w[g][2][H, :], ALU.mult)
            for k in range(2):
                dve.wait_ge(L2.sca[k], ALL)
            over_pairs(dve, l3)

        @block.tensor
        def _(pe):
            def hold(s, v):
                pe.wait_ge(s, v)
                pe.sem_inc(s_tick_pe, 1)

            def hold_after(steps, i, name, g=0):
                hold(steps.sem, steps.at(i, name, g))

            def product(dest, parts, done=None):
                for k, (lhsT, rhs) in enumerate(parts):
                    m = pe.matmul(dest, lhsT, rhs, start=(k == 0), stop=(k == len(parts) - 1))
                if done is not None:
                    m.then_inc(done, 1)

            for S in (L0.pe, L1.pe, L2.pe, L3.pe, D_pe):
                pe.sem_inc(S.sem, S.n)

            pe.wait_ge(s_wload, NW)
            pe.wait_ge(s_wdve, 3)
            product(psum[0][:, 0:C], [(w1_l[:, :], att_m[:, 0, :]), (w1_r[:, :], att_m[:, 1, :])])
            product(psum[1][:, 0:P], [(w3t_l[:, :], wpre2[:, 0, :]), (w3t_r[:, :], wpre2[:, 1, :])])
            product(psum[2][0:4, 0:P], [(wet[:, :], wpre2[:, 2, :])])
            product(psum[2][:, 256:257], [(wpre2[:, 2, :], be_col[:, :])])
            product(psum[3][0:C, 0:P], [(w3t_l[:, 0:C], wpm[:, :])])
            product(psum[3][0:C, 256:256 + C], [(wpm[:, C:P], w3t_l[:, 0:C])])
            product(psum[4][:, 0:1], [(avgmat[0:125, :], nvs[:, :])], s_wpe)
            pe.wait_ge(s_wdve, 4)
            product(psum[5][0:C, 0:1], [(wstd[:, s, :], fac0[:, 4 + s:5 + s]) for s in range(3)], s_wpe)
            pe.wait_ge(s_wdve, 5)
            for g in range(3):
                product(psum[6][:, 8 * g:8 * g + 1], [(wih2[:, g, :], out0[:, :])])
            product(psum[7][:, 0:3 * C].rearrange("p (g c) -> p g c", g=3), [(mmt2[:, :], wih2[:, :, 0:C])], s_wpe)

            for n, (src_tile, level) in enumerate(turn_plan):
                pe.wait_ge(s_sort, level)
                for s in range(2):
                    for h in range(2):
                        m = pe.transpose(psum[0][:, (2 * s + h) * P:(2 * s + h + 1) * P],
                                         src_tile[:, s, h * P:(h + 1) * P], ident)
                m.then_inc(s_sortt, 1)
            pe.wait_ge(s_lists, 1)
            for m_ in range(7):
                for h in range(2):
                    m = pe.transpose(psum[m_][:, h * P:(h + 1) * P], lists[:, m_, h * P:(h + 1) * P], ident)
                m.then_inc(s_lt, 1)

            def turn(dest, tiles, done):
                for t, a in enumerate(tiles):
                    m = pe.transpose(dest[:, blk[t]], a, ident)
                m.then_inc(done, 1)

            def turn_back(dest, a, rows, done):
                for t in range(4):
                    m = pe.transpose(dest[:, rows * t:rows * (t + 1)], a[0:rows, blk[t]], ident[0:rows, 0:rows])
                m.then_inc(done, 1)

            pe.wait_ge(s_idx, 7)
            def l0(i):
                L = L0
                for g in G:
                    hold(L.gat[g], 128 * (i + 1))
                    hold_after(L.act, i - 1, "z", g)
                    turn(ps[g][0], [gat[:, g, t, 0:P] for t in range(4)], L.pe.done("z"))
                for g in G:
                    hold(ec_sem[g], 64 * (i + 1))
                    hold_after(L.dve, i - 1, "ea", g)
                    hold_after(L.act, i - 1, "out", g)
                    turn(ps[g][1], [eca[:, g, t, 0:P] for t in range(4)], L.pe.done("ea"))
                for g in G:
                    hold_after(L.act, i, "z", g)
                    hold_after(L.dve, i, "ea", g)
                    hold_after(L.dve, i - 1, "srelu", g)
                    hold_after(L.act, i - 1, "sabs", g)
                    product(ps[g][2][:, :], [(w_fs_z[:, :], z[g][:, :]), (w_fs_e[:, :], ear[g][:, :])], L.pe.done("fs"))
                for g in G:
                    hold_after(L.dve, i, "y", g)
                    product(ps[g][3][0:C, :], [(center[0:C, 0:C], w[g][12][0:C, :])], L.pe.done("center"))
                for g in G:
                    hold_after(L.act, i, "sq", g)
                    product(ps[g][0][0:C, :], [(mean64[0:C, 0:C], w[g][3][0:C, :])], L.pe.done("var"))
                for g in G:
                    hold_after(L.dve, i, "x1", g)
                    hold_after(L.act, i - 1, "out", g)
                    turn_back(ps[g][1], w[g][13], C, L.pe.done("out"))
            over_pairs(pe, l0)

            def l1(i):
                L = L1
                for g in G:
                    hold_after(L.act, i, "pack", g)
                    turn(ps[g][0], [pk[g][:, t, :] for t in range(4)], L.pe.done("z"))
                for g in G:
                    hold_after(L.act, i, "z", g)
                    hold_after(L.dve, i - 1, "e", g)
                    product(ps[g][1][0:C, :], [(w_score[:, :], z[g][:, :])], L.pe.done("score"))
                for g in G:
                    hold_after(L.dve, i - 1, "val", g)
                    product(ps[g][2][0:C, :], [(w1t[C:P, :], z[g][C:P, :])], L.pe.done("xp"))
                for g in G:
                    hold_after(L.dve, i, "v2", g)
                    hold_after(L.act, i, "norm", g)
                    hold_after(L.act, i - 1, "out", g)
                    turn_back(ps[g][3], w[g][13], C + 1, L.pe.done("out"))
            for k in range(2):
                pe.wait_ge(L0.sca[k], ALL)
            over_pairs(pe, l1)

            def dense(i):
                for g in G:
                    hold_after(D_act, i, "pack", g)
                    hold_after(D_act, i - 1, "out", g)
                    turn(ps[g][0], [pk[g][:, k, :] for k in range(4)], D_pe.done("z"))
                for g in G:
                    hold_after(D_act, i, "z", g)
                    hold_after(D_dve, i - 1, "x4", g)
                    product(ps[g][1][:, :], [(center, z[g][:, :])], D_pe.done("c2"))
                for g in G:
                    hold_after(D_act, i, "sq2", g)
                    product(ps[g][2][:, :], [(mean64, w[g][0][:, :])], D_pe.done("v2"))
                for g in G:
                    hold_after(D_dve, i, "x2", g)
                    product(ps[g][0][:, :], [(w2_bd[:, :], w[g][3][:, :])], D_pe.done("h"))
                for g in G:
                    hold_after(D_dve, i, "y3", g)
                    product(ps[g][3][:, :], [(center, w[g][5][:, :])], D_pe.done("c3"))
                for g in G:
                    hold_after(D_act, i, "sq3", g)
                    product(ps[g][2][:, :], [(mean64, w[g][0][:, :])], D_pe.done("v3"))
                for k, name in enumerate(("gr", "gz", "gi", "gh")):
                    for g in G:
                        hold_after(D_dve, i, "x3", g)
                        product(ps[g][k][:, :], [(dg[:, k, :], w[g][6][:, :])], D_pe.done(name))
                for g in G:
                    hold_after(D_dve, i, "y4", g)
                    product(ps[g][1][:, :], [(center, w[g][12][:, :])], D_pe.done("c4"))
                for g in G:
                    hold_after(D_act, i, "sq4", g)
                    product(ps[g][2][:, :], [(mean64, w[g][0][:, :])], D_pe.done("v4"))
                for g in G:
                    hold_after(D_dve, i, "x4", g)
                    turn_back(ps[g][0], w[g][13], P, D_pe.done("out"))
            for k in range(2):
                pe.wait_ge(L1.sca[k], ALL)
            over_pairs(pe, dense, DPAIRS)

            def l2(i):
                L = L2
                for g in G:
                    hold_after(L.dve, i - 1, "msg", g)
                    hold(L.gat[g], 128 * (i + 1))
                    for t in range(4):
                        m = pe.matmul(ps[g][3][:, blk[t]], gat[:, g, t, TW + C:TW + C + 1].broadcast_to([P, P]), ident,
                                      start=True, stop=True)
                    m.then_inc(L.pe.done("norm"), 1)
                for g in G:
                    hold_after(L.act, i, "pack", g)
                    turn(ps[g][0], [pk[g][:, t, :] for t in range(4)], L.pe.done("z"))
                for g in G:
                    hold_after(L.act, i, "z", g)
                    hold_after(L.dve, i - 1, "x2", g)
                    hold_after(L.act, i - 1, "out", g)
                    product(ps[g][1][:, :], [(center, z[g][:, :])], L.pe.done("center"))
                for g in G:
                    hold_after(L.act, i, "sq", g)
                    product(ps[g][2][:, :], [(mean64, w[g][0][:, :])], L.pe.done("var"))
                for g in G:
                    hold_after(L.dve, i, "aggn", g)
                    hold_after(L.act, i - 1, "relu", g)
                    product(ps[g][0][:, :], [(w2_bd[:, :], w[g][5][:, :]), (w2_neg[C:P, :], w[g][7][C:P, :])], L.pe.done("h"))
                for g in G:
                    hold_after(L.dve, i, "y3", g)
                    hold_after(L.act, i - 1, "out", g)
                    turn_back(ps[g][1], w[g][9], P, L.pe.done("out"))
            for k in range(2):
                pe.wait_ge(do_sem[k], 16 * DPAIRS)
            over_pairs(pe, l2)

            def l3(i):
                L = L3
                for g in G:
                    hold(L.gat[g], 128 * (i + 1))
                    hold(eal_sem[g], 16 * (i + 1))
                    hold_after(L.act, i - 1, "z", g)
                    turn(ps[g][0], [gat[:, g, t, 0:P] for t in range(4)], L.pe.done("z"))
                for g in G:
                    hold_after(L.act, i - 1, "ea", g)
                    for t in range(4):
                        m = pe.transpose(ps[g][1][0:4, blk[t]], eas[:, g, t, :], ident)
                    m.then_inc(L.pe.done("ea"), 1)
                for g in G:
                    hold_after(L.act, i, "z", g)
                    product(ps[g][2][:, :], [(center, z[g][:, :])], L.pe.done("center"))
                for g in G:
                    hold_after(L.act, i, "sq", g)
                    hold_after(L.act, i - 1, "out", g)
                    product(ps[g][3][:, :], [(mean64, w[g][0][:, :])], L.pe.done("var"))
                for g in G:
                    hold_after(L.act, i, "ea", g)
                    hold_after(L.dve, i, "x3", g)
                    hold_after(L.dve, i - 1, "a", g)
                    product(ps[g][0][:, :], [(w_h[:, :], w[g][4][:, :]), (w_hea[:, :], w[g][3][0:4, :])], L.pe.done("h"))
                for g in G:
                    product(ps[g][1][:, :], [(selw[0:4, :], w[g][3][0:4, :])], L.pe.done("ew"))
                for g in G:
                    hold_after(L.act, i, "std", g)
                    hold_after(L.dve, i, "mx", g)
                    hold_after(L.dve, i - 1, "x4", g)
                    product(ps[g][2][:, :], [(wp_a1[:, :], w[g][9][:, :]), (wp_a2[:, :], sc[2][:, g, :])], L.pe.done("p"))
                for g in G:
                    hold_after(L.dve, i, "fp", g)
                    hold_after(L.act, i - 1, "out", g)
                    product(ps[g][3][:, :], [(wu_x[:, :], w[g][4][0:C, :]), (wu_a1[:, :], w[g][9][:, :]),
                                          (wu_a2[:, :], sc[2][:, g, :]), (wu_f[:, :], w[g][14][:, :])], L.pe.done("u"))
                for g in G:
                    hold_after(L.act, i, "u", g)
                    product(ps[g][0][:, :], [(w_g1[:, :], w[g][4][:, :])], L.pe.done("g1"))
                for g in G:
                    product(ps[g][1][:, :], [(w_g2[:, :], w[g][4][:, :])], L.pe.done("g2"))
                for g in G:
                    hold_after(L.dve, i, "y4", g)
                    product(ps[g][2][0:C, :], [(center[0:C, 0:C], w[g][12][0:C, :])], L.pe.done("center4"))
                for g in G:
                    hold_after(L.act, i, "sq4", g)
                    product(ps[g][3][0:C, :], [(mean64[0:C, 0:C], w[g][0][0:C, :])], L.pe.done("var4"))
                for g in G:
                    hold_after(L.dve, i, "x4", g)
                    turn_back(ps[g][3], w[g][13], C, L.pe.done("out"))
            for k in range(2):
                pe.wait_ge(L2.sca[k], ALL)
            over_pairs(pe, l3)

        @block.scalar
        def _(act):
            def run(name_done, *args, **kw):
                act.activation(*args, **kw).then_inc(name_done, 1)

            def after_act(steps, i, name, g=0):
                act.wait_ge(steps.sem, steps.at(i, name, g))

            for S in (d1_act, L0.act, L1.act, L2.act, L3.act, D_act):
                act.sem_inc(S.sem, S.n)

            act.preload_act_table_set(LN_EXP)
            act.wait_ge(s_wload, NW)
            act.wait_ge(s_const, 3)
            run(s_wact, nv[:, :], nv[:, :], ACT.Ln, bias=one_col[0:125, :])
            run(s_wact, fac0[:, 0:1], eps_col[0:C, :], ACT.Ln)
            act.wait_ge(s_wact, 2)
            run(s_wact, fac0[:, 4:5], fac0[:, 0:1], ACT.Exp, scale=0.5)
            run(s_wact, fac0[:, 1:2], one_col[0:C, :], ACT.Ln, bias=one_col[0:C, :])

            def dense1(j, r=R1, n=P, last=False):
                act.wait_ge(s_d1l, 16 * (j + 1))
                after_act(d1_dve, j - 1, "norm")
                run(d1_act.done("relu"), d1r[0:n, 0:r, :], d1x[0:n, 0:r, :], ACT.Relu)
                after_act(d1_dve, j, "centered")
                run(d1_act.done("square"), d1r[0:n, 0:r, :], d1o[0:n, 0:r, 0:C], ACT.Square)
                after_act(d1_dve, j, "sumsq")
                run(d1_act.done("ln"), d1s[0:n, 2, 0:r], d1s[0:n, 1, 0:r], ACT.Ln, scale=1.0 / C, bias=eps_col[0:n, :])
                after_act(d1_act, j, "ln")
                run(d1_act.done("rstd"), d1s[0:n, 3, 0:r], d1s[0:n, 2, 0:r], ACT.Exp, scale=-0.5)
            with act.Fori(0, ROWS1) as j:
                dense1(j)
            dense1(ROWS1, 1, TAIL1)

            def rstd(L, i, names, cbank, sq, vbank, ln, out_, rows=slice(0, P), ready="center", vready="var", pe_=None,
                     free=()):
                pe_ = pe_ or L.pe
                for g in G:
                    after_act(pe_, i, ready, g)
                    run(L.act.done(names[0]), w[g][sq][rows, :], ps[g][cbank][rows, :], ACT.Square)
                for g in G:
                    after_act(pe_, i, vready, g)
                    run(L.act.done(names[1]), w[g][ln][rows, :], ps[g][vbank][rows, :], ACT.Ln, bias=eps_col[rows, :])
                for g in G:
                    after_act(L.act, i, names[1], g)
                    for steps, j, name in free:
                        after_act(steps, j, name, g)
                    run(L.act.done(names[2]), w[g][out_][rows, :], w[g][ln][rows, :], ACT.Exp, scale=-0.5)

            H = slice(0, C)
            U = slice(C, P)

            def l0(i):
                L = L0
                for g in G:
                    after_act(L.pe, i, "z", g)
                    after_act(L.pe, i - 1, "fs", g)
                    after_act(L.dve, i - 1, "y", g)
                    run(L.act.done("z"), z[g][:, :], ps[g][0][:, :], ACT.Copy)
                for g in G:
                    after_act(L.pe, i, "fs", g)
                    after_act(L.dve, i - 1, "core", g)
                    run(L.act.done("sabs"), w[g][0][:, :], ps[g][2][:, :], ACT.Abs, bias=b_fs[:, :])
                for g in G:
                    after_act(L.act, i, "sabs", g)
                    run(L.act.done("exps"), w[g][1][:, :], w[g][0][:, :], ACT.Exp, scale=-1.0)
                for g in G:
                    after_act(L.act, i, "exps", g)
                    run(L.act.done("log"), w[g][2][:, :], w[g][1][:, :], ACT.Ln, bias=one_col[:, :])
                for g in G:
                    after_act(L.dve, i, "core", g)
                    after_act(L.dve, i - 1, "msg", g)
                    run(L.act.done("gate"), w[g][8][U, :], w[g][9][H, :], ACT.Exp, scale=-1.0)
                rstd(L, i, ("sq", "ln", "rstd"), 3, 3, 0, 4, 5, H, free=((L.dve, i - 1, "x1"),))
                for g in G:
                    after_act(L.pe, i, "out", g)
                    again(act.wait_ge, L.sca[g], 64, i)
                    run(L.act.done("out"), ot[:, g, :, 0:C], ps[g][1][:, 0:4 * C].rearrange("p (t k) -> p t k", t=4), ACT.Copy)
            over_pairs(act, l0)

            def l1(i):
                L = L1
                for g in G:
                    act.wait_ge(L.gat[g], 128 * (i + 1))
                    after_act(L.pe, i - 1, "z", g)
                    run(L.act.done("pack"), pk[g][:, :, :].rearrange("p t (a k) -> p t a k", a=2),
                        gat[:, g, :, :].rearrange("p t (a k) -> p t a k", a=2)[:, :, :, 0:C], ACT.Copy)
                for g in G:
                    after_act(L.pe, i, "z", g)
                    after_act(L.pe, i - 1, "xp", g)
                    after_act(L.dve, i - 1, "v2", g)
                    run(L.act.done("z"), z[g][:, :], ps[g][0][:, :], ACT.Copy)
                for g in G:
                    act.wait_ge(L.mk[g], 16 * (i + 1))
                    after_act(L.dve, i - 1, "mseg", g)
                    run(L.act.done("negm"), negm[g][H, 0:CH], mk[H, g, 0:CH], ACT.Copy, scale=BIG, bias=-BIG)
                for g in G:
                    after_act(L.dve, i, "cnt", g)
                    run(L.act.done("lncnt"), w[g][6][C:C + 1, :], sc[3][C:C + 1, g, :], ACT.Ln)
                for g in G:
                    after_act(L.act, i, "lncnt", g)
                    after_act(L.pe, i - 1, "out", g)
                    run(L.act.done("norm"), w[g][13][C:C + 1, :], w[g][6][C:C + 1, :], ACT.Exp, scale=-0.5)
                for g in G:
                    after_act(L.pe, i, "score", g)
                    after_act(L.dve, i - 1, "e", g)
                    run(L.act.done("lrelu"), w[g][0][H, :], ps[g][1][H, :], ACT.Copy, scale=0.2)
                for g in G:
                    after_act(L.dve, i, "dcar", g)
                    after_act(L.dve, i - 1, "carry", g)
                    run(L.act.done("carry"), sm[g][H, 1:2], sm[g][H, 0:1], ACT.Exp)
                for g in G:
                    after_act(L.dve, i, "d", g)
                    after_act(L.dve, i - 1, "val", g)
                    run(L.act.done("ex"), w[g][5][H, :], w[g][4][H, :], ACT.Exp)
                for g in G:
                    after_act(L.pe, i, "out", g)
                    again(act.wait_ge, h1_sem[g], 16, i)
                    run(L.act.done("out"), ot[:, g, :, 0:C + 1],
                        ps[g][3][:, 0:4 * (C + 1)].rearrange("p (t k) -> p t k", t=4), ACT.Copy)
            for k in range(2):
                act.wait_ge(L0.sca[k], ALL)
            over_pairs(act, l1)

            class D:
                pe, act = D_pe, D_act

            def dense(i):
                for g in G:
                    act.wait_ge(dn_sem[g], 16 * (i + 1))
                    after_act(D_pe, i - 1, "z", g)
                    run(D_act.done("pack"), pk[g][:, :, :].rearrange("p k (a c) -> p k a c", a=2),
                        dn[:, g, :, :].rearrange("p (a k) c -> p k a c", a=2)[:, :, :, 0:C], ACT.Copy)
                for g in G:
                    after_act(D_pe, i, "z", g)
                    after_act(D_pe, i - 1, "c2", g)
                    run(D_act.done("z"), z[g][:, :], ps[g][0][:, :], ACT.Copy)
                rstd(D, i, ("sq2", "ln2", "r2"), 1, 0, 2, 1, 2, ready="c2", vready="v2",
                     free=((D_dve, i - 1, "x4"), (D_pe, i - 1, "v4")))
                for g in G:
                    after_act(D_pe, i, "h", g)
                    run(D_act.done("relu"), w[g][4][:, :], ps[g][0][:, :], ACT.Relu, bias=b2_col[:, :])
                rstd(D, i, ("sq3", "ln3", "r3"), 3, 0, 2, 1, 2, ready="c3", vready="v3",
                     free=((D_dve, i, "x2"),))
                for k, (t, name) in enumerate(((7, "r"), (8, "zg"))):
                    for g in G:
                        after_act(D_pe, i, ("gr", "gz")[k], g)
                        run(D_act.done(name), w[g][t][:, :], ps[g][k][:, :], ACT.Sigmoid, bias=dg_b[:, k:k + 1])
                for g in G:
                    after_act(D_dve, i, "a", g)
                    run(D_act.done("n"), w[g][10][:, :], w[g][11][:, :], ACT.Tanh, bias=dg_b[:, 2:3])
                act.preload_act_table_set(LN_EXP)
                rstd(D, i, ("sq4", "ln4", "r4"), 1, 0, 2, 1, 2, ready="c4", vready="v4",
                     free=((D_dve, i, "x3"),))
                for g in G:
                    after_act(D_pe, i, "out", g)
                    again(act.wait_ge, do_sem[g], 16, i)
                    run(D_act.done("out"), do[:, g, :, :].rearrange("p (a k) c -> p k a c", a=2),
                        ps[g][0][:, :].rearrange("p (k a c) -> p k a c", k=4, a=2), ACT.Copy)
            for k in range(2):
                act.wait_ge(L1.sca[k], ALL)
            over_pairs(act, dense, DPAIRS)

            def l2(i):
                L = L2
                for g in G:
                    act.wait_ge(L.gat[g], 128 * (i + 1))
                    after_act(L.pe, i - 1, "z", g)
                    run(L.act.done("pack"), pk[g][:, :, :].rearrange("p t (a k) -> p t a k", a=2),
                        gat[:, g, :, :].rearrange("p t (a k) -> p t a k", a=2)[:, :, :, 0:C], ACT.Copy)
                for g in G:
                    after_act(L.pe, i, "z", g)
                    after_act(L.pe, i - 1, "center", g)
                    run(L.act.done("z"), z[g][:, :], ps[g][0][:, :], ACT.Copy)
                for g in G:
                    after_act(L.dve, i, "cnt", g)
                    run(L.act.done("lncnt"), w[g][3][U, :], sc[1][U, g, :], ACT.Ln)
                for g in G:
                    after_act(L.act, i, "lncnt", g)
                    after_act(L.dve, i - 1, "aggn", g)
                    run(L.act.done("nin"), w[g][4][U, :], w[g][3][U, :], ACT.Exp, scale=-0.5)
                rstd(L, i, ("sq", "ln", "rstd"), 1, 0, 2, 1, 2, free=((L.dve, i - 1, "x2"),))
                for g in G:
                    after_act(L.pe, i, "h", g)
                    after_act(L.dve, i - 1, "y3", g)
                    run(L.act.done("relu"), w[g][8][:, :], ps[g][0][:, :], ACT.Relu, bias=b2_col[:, :])
                for g in G:
                    after_act(L.pe, i, "out", g)
                    again(act.wait_ge, L.sca[g], 64, i)
                    again(act.wait_ge, h3_sem[g], 16, i)
                    run(L.act.done("out"), ot3[:, g, :, :], ps[g][1][:, :].rearrange("p (t k) -> p t k", t=4), ACT.Copy)
            for k in range(2):
                act.wait_ge(do_sem[k], 16 * DPAIRS)
            over_pairs(act, l2)

            def l3(i):
                L = L3
                for g in G:
                    after_act(L.pe, i, "z", g)
                    after_act(L.pe, i - 1, "center", g)
                    run(L.act.done("z"), z[g][:, :], ps[g][0][:, :], ACT.Copy)
                rstd(L, i, ("sq", "ln", "rstd"), 2, 0, 3, 1, 2, free=((L.dve, i - 1, "x4"),))
                for g in G:
                    after_act(L.pe, i, "ea", g)
                    after_act(L.pe, i - 1, "ew", g)
                    run(L.act.done("ea"), w[g][3][0:4, :], ps[g][1][0:4, :], ACT.Copy)
                for g in G:
                    act.wait_ge(L.mk[g], 16 * (i + 1))
                    after_act(L.dve, i - 1, "mx", g)
                    run(L.act.done("negm"), negm[g][:, 0:CH], mk[:, g, 0:CH], ACT.Copy, scale=BIG, bias=-BIG)
                for g in G:
                    after_act(L.dve, i, "hw", g)
                    after_act(L.dve, i - 1, "o", g)
                    run(L.act.done("h"), w[g][6][:, :], w[g][5][:, :], ACT.Identity, bias=bpre_col[:, :])
                for g in G:
                    after_act(L.act, i, "h", g)
                    run(L.act.done("hneg"), w[g][7][:, :], w[g][6][:, :], ACT.Identity, scale=sgn_col[:, :])
                for g in G:
                    after_act(L.dve, i, "var", g)
                    run(L.act.done("lnvar"), w[g][8][U, :], w[g][12][U, :], ACT.Ln, bias=eps_col[U, :])
                for g in G:
                    after_act(L.act, i, "lnvar", g)
                    run(L.act.done("std"), w[g][9][U, :], w[g][8][U, :], ACT.Exp, scale=0.5)
                for g in G:
                    after_act(L.dve, i - 1, "zxn", g)
                    run(L.act.done("logd"), w[g][10][:, :], sc[3][:, g, :], ACT.Ln, bias=one_col[:, :])
                for g in G:
                    after_act(L.pe, i, "u", g)
                    run(L.act.done("u"), w[g][4][U, :], ps[g][3][U, :], ACT.Identity, bias=bpost_col[U, :])
                for g in G:
                    after_act(L.pe, i, "g1", g)
                    after_act(L.dve, i, "rlog", g)
                    run(L.act.done("rz"), w[g][10][:, :], ps[g][0][:, :], ACT.Sigmoid, bias=b_g1[:, :])
                for g in G:
                    after_act(L.dve, i, "a", g)
                    run(L.act.done("n"), w[g][6][H, :], w[g][11][H, :], ACT.Tanh, bias=brow[H, 0, 2:3])
                act.preload_act_table_set(LN_EXP)
                rstd(L, i, ("sq4", "ln4", "rstd4"), 2, 0, 3, 1, 2, H, ready="center4", vready="var4",
                     free=((L.dve, i, "x3"),))
                for g in G:
                    after_act(L.pe, i, "out", g)
                    again(act.wait_ge, L.sca[g], 64, i)
                    run(L.act.done("out"), ot3[:, g, :, 0:C], ps[g][3][:, 0:4 * C].rearrange("p (t k) -> p t k", t=4), ACT.Copy)
            for k in range(2):
                act.wait_ge(L2.sca[k], ALL)
            over_pairs(act, l3)


def shape_constants():
    eye = np.eye(P, dtype=np.float32)
    two = np.kron(np.eye(2, dtype=np.float32), np.full((C, C), 1.0 / C, np.float32))
    heads = np.zeros((P, P), np.float32)
    heads[:C, :C] = np.kron(np.eye(HEADS, dtype=np.float32), np.ones((C // HEADS, C // HEADS), np.float32))
    row3 = np.zeros((P, P), np.float32)
    row3[3, :] = 1.0
    mats = np.stack([eye, eye - two, two, heads, row3], 1)
    place = np.arange(SN).reshape(P, SF)
    idx = np.repeat(place[:, None, :], 2, 1).astype(np.float32)
    bit = [1.0 - 2.0 * ((place >> k) & 1) for k in range(SK + 1)]
    bit[0] = np.ones_like(bit[0])
    sign = np.stack([bit[k] * bit[k - 1] for k in range(1, SK + 1)], 1).astype(np.float32)
    return np.ascontiguousarray(mats), np.ascontiguousarray(idx), np.ascontiguousarray(sign)


_INS = ["x", "src", "dst", "edge_attr_128", "edge_attr_4", "node_vec", "L0_gnn_W_f", "L0_gnn_b_f", "L0_gnn_W_s",
        "L0_gnn_b_s", "L1_gnn_W", "L1_gnn_src_attn", "L1_gnn_dst_attn", "L2_gnn_W", "L2_gnn_b", "L3_gnn_W",
        "L3_gnn_We", "L3_gnn_be", "L3_gnn_Wpre", "L3_gnn_bpre", "L3_gnn_Wpost", "L3_gnn_bpost", "L3_gnn_Wih",
        "L3_gnn_bih", "L3_gnn_Whh", "L3_gnn_bhh"]


def kernel(**inputs):
    import concourse.bacc as bacc
    from concourse.bass_utils import run_bass_kernel_spmd

    nc = bacc.Bacc("TRN2", target_bir_lowering=False, num_devices=1)
    arrays, args = {}, []
    named = [(n, np.ascontiguousarray(inputs[n])) for n in _INS]
    named += list(zip(("k_mats", "k_idx", "k_sign"), shape_constants()))
    for name, a in named:
        arrays[f"in_{name}"] = a
        args.append(nc.dram_tensor(f"in_{name}", a.shape, mybir.dt.from_np(a.dtype), kind="ExternalInput").ap())
    args.append(nc.dram_tensor("out_0", (N, C), F32, kind="ExternalOutput").ap())
    for name, shape in (("T", (N, TW)), ("X3", (N, C)), ("H1", (NCH * P, 4 * TW)), ("H3", (NCH * P, 4 * C)),
                        ("EC", (E, EW)), ("KD", (2, SN + 2)), ("MK", (2, SN))):
        args.append(nc.dram_tensor(name, shape, F32, kind="Internal").ap())
    gnn_kernel(nc, *args)
    r = run_bass_kernel_spmd(nc, [arrays], core_ids=[0])
    return r.results[0]["out_0"]
```

```python
from contextlib import ExitStack

import numpy as np

import concourse.bass as bass
from concourse import mybir

F32 = mybir.dt.float32
I32 = mybir.dt.int32
U32 = mybir.dt.uint32
ALU = mybir.AluOpType
ACT = mybir.ActivationFunctionType
AX_X = mybir.AxisListType.X

P = 128
N = 100000
E = 25000
C = 64
HEADS = 8
CH = 512
W = 3
G = range(W)
ROUNDS = -(-E // (W * CH))
NCH = W * ROUNDS
NT = 4 * NCH
TW = C + 2
EW = 2 * C + 5
SF = 256
SN = P * SF
SK = 15
SKIP = 1 << 20
BIG = 1.0e30
EPS = 1e-5
MID = N / 2 + 0.5
MARGIN = 255.5
NODES = 1000
DW = 4
DG = range(DW)
DROUNDS = N // NODES // DW
LN_EXP = "natural_log_exp_and_others"
D1P = 125
R1 = N // D1P // (ROUNDS - 1)
assert D1P * R1 * (ROUNDS - 1) == N


class Count:

    def __init__(self, sem):
        self.sem, self.n = sem, 0

    def tick(self, ins):
        ins.then_inc(self.sem, 1)
        self.n += 1


class Steps:

    def __init__(self, sem, *names, width=W):
        self.sem, self.place, self.n = sem, {}, 0
        for group in names:
            if isinstance(group, str):
                group = (group,)
            if isinstance(group, tuple):
                group = [(name, g) for g in range(width) for name in group]
            for step in group:
                self.n += 1
                self.place[step] = self.n
        self.order, self.next = sorted(self.place, key=self.place.get), 0

    def done(self, name):
        assert self.order[self.next % self.n][0] == name, (name, self.order[self.next % self.n])
        self.next += 1
        return self.sem

    def at(self, i, name, g=0):
        return (i + 1) * self.n + self.place[name, g]


def gnn_kernel(nc, x, src, dst, ea128, ea4, node_vec, Wf, bf, Ws, bs, W1, a_src, a_dst, W2, b2,
               W3, We, be, Wpre, bpre, Wpost, bpost, Wih, bih, Whh, bhh,
               k_mats, k_idx, k_sign, out, T, X3, H1, H3, EC, KD, MK, CN):
    with ExitStack() as ctx:
        ctx.enter_context(nc.allow_non_contiguous_dma(reason="small weights, loaded once, transposed"))
        def sb(name, shape, dt=F32):
            return ctx.enter_context(nc.sbuf_tensor(name, shape, dt))

        def sem(name):
            return ctx.enter_context(nc.semaphore(name))

        banks = [ctx.enter_context(nc.psum_tensor(f"ps{i}", [P, 512], F32)) for i in range(8)]
        ps = [banks[2 * g:2 * g + 2] for g in DG]

        mats = sb("mats", [P, 5, P])
        ident, center, mean64, headmask, selw = (mats[:, i, :] for i in range(5))
        eps_col = sb("eps_col", [P, 1])
        one_col = sb("one_col", [P, 1])
        ones = sb("ones", [P, CH])
        avgmat = sb("avgmat", [P, P])

        w_fs_z = sb("w_fs_z", [P, P])
        w_fs_e = sb("w_fs_e", [P, P])
        b_fs = sb("b_fs", [P, 1])
        w1_l = sb("w1_l", [C, P])
        w1_r = sb("w1_r", [C, P])
        w1t = sb("w1t", [P, C])
        att = sb("att", [C, 2])
        att_m = sb("att_m", [C, 2, C])
        w_score = sb("w_score", [P, C])
        w2_bd = sb("w2_bd", [P, P])
        w2_neg = sb("w2_neg", [P, P])
        b2_col = sb("b2_col", [P, 1])
        w3t_l = sb("w3t_l", [C, P])
        w3t_r = sb("w3t_r", [C, P])
        wpre2 = sb("wpre2", [C, 3, P])
        wet = sb("wet", [C, 4])
        be_col = sb("be_col", [C, 1])
        bpre_col = sb("bpre_col", [P, 1])
        w_h = sb("w_h", [P, P])
        w_hea = sb("w_hea", [4, P])
        bew_col = sb("bew_col", [P, 1])
        wp_a1 = sb("wp_a1", [P, P])
        wp_a2 = sb("wp_a2", [P, P])
        wu_a1 = sb("wu_a1", [P, P])
        wu_a2 = sb("wu_a2", [P, P])
        wu_f = sb("wu_f", [P, P])
        wpm = sb("wpm", [C, P])
        wu_x = sb("wu_x", [C, P])
        bpost_col = sb("bpost_col", [P, 1])
        w_g1 = sb("w_g1", [P, P])
        w_g2 = sb("w_g2", [P, P])
        wih2 = sb("wih2", [C, 3, P])
        whh2 = sb("whh2", [P, 3 * C])
        brow = sb("brow", [P, 2, 3])
        b_g1 = sb("b_g1", [P, 1])
        wstd = sb("wstd", [C, 3, C])
        nv = sb("nv", [125, N // 125])
        nvs = sb("nvs", [125, 1])
        avg = sb("avg", [P, 1])
        iavg = sb("iavg", [P, 1])
        fac0 = sb("fac0", [C, 8])
        mmt2 = sb("mmt2", [C, P])
        out0 = sb("out0", [C, 1])
        dg = sb("dg", [P, 4, P])
        dg_b = sb("dg_b", [P, 4])

        s_const = sem("s_const")
        s_wload = sem("s_wload")
        s_wzero = sem("s_wzero")
        s_wpe = sem("s_wpe")
        s_wact = sem("s_wact")
        s_wdve = sem("s_wdve")

        (I_PERMD, I_DSTC, I_DSTR, I_DSTH, I_PERMS, I_SRCC, I_SRCH, I_SRCD, I_SRCF) = range(9)
        idx = sb("idx", [P, 9, NT], U32)
        ea4d = sb("ea4d", [P, NT, 4])

        keys = sb("keys", [P, 2, SF], I32)
        kidx = sb("kidx", [P, 2, SF])
        ksign = sb("ksign", [P, SK, SF])
        sx = sb("sx", [P, 2, SF])
        sy = sb("sy", [P, 2, SF])
        sf = [sb(f"sf{i}", [P, 2, SF]) for i in range(6)]
        si = [sb(f"si{i}", [P, 2, SF], I32) for i in range(3)]
        lists = sb("lists", [P, 7, SF])
        edge_col = sb("edge_col", [2, 2])

        s_keyl = sem("s_keyl")
        s_keym = sem("s_keym")
        s_sort = sem("s_sort")
        s_sortt = sem("s_sortt")
        s_ec = sem("s_ec")
        s_kd = sem("s_kd")
        s_kr = sem("s_kr")
        s_mk = sem("s_mk")
        s_lt = sem("s_lt")
        s_idx = sem("s_idx")

        d1x = sb("d1x", [P, R1, C])
        d1r = sb("d1r", [P, R1, C])
        d1o = sb("d1o", [P, R1, TW])
        d1s = sb("d1s", [P, 4, R1])
        s_d1l = sem("s_d1l")
        s_d1o = sem("s_d1o")
        d1_act = Steps(sem("s_d1act"), "square", "ln", "rstd", width=1)
        d1_dve = Steps(sem("s_d1dve"), "y", "sum", "mean", "centered", "sumsq", "norm", width=1)

        def rows1(ap, i):
            return ap.rearrange("(p r) c -> p r c", p=D1P)[:, bass.ds((i - 1) * R1, R1), :]

        gat = sb("gat", [P, W, 4, 2 * TW])
        eca = sb("eca", [P, W, 4, EW])
        gst = sb("gst", [P, W, 3, 4], U32)
        sst = sb("sst", [P, W, 4], U32)
        pst = sb("pst", [P, W, 4], U32)
        dli = sb("dli", [P, W, 4], I32)
        eas = sb("eas", [P, W, 4, 4])
        mk = sb("mk", [P, W, CH + 1])
        ot = sb("ot", [P, W, 4, TW])
        ot3 = sb("ot3", [P, W, 4, P])

        def flat(a):
            return a[:, :, :].rearrange("p a b -> p (a b)")

        def cut(a, n, lo=0):
            return [flat(a)[:, lo + k * CH:lo + (k + 1) * CH] for k in range(n)]

        si_tiles = [flat(a).bitcast(F32) for a in si]
        z = [sb("z", [P, CH])[:, :], si_tiles[0], sb("z2", [P, CH])[:, :]]
        ear = [sb("ear", [P, CH])[:, :], si_tiles[1], sb("ear2", [P, CH])[:, :]]
        pk_tiles = [sb("pk", [P, CH])[:, :], si_tiles[2], sb("pk2", [P, CH])[:, :]]
        z += [ear[0]]
        pk_tiles += [ear[1]]
        pk = [a.rearrange("p (t k) -> p t k", t=4) for a in pk_tiles]
        negm = [sb(f"negm{g}", [P, CH + 1])[:, :] for g in G]
        sort_tiles = cut(ksign, 7) + [flat(a) for a in sf] + cut(lists, 3) + [flat(sx), flat(sy)]
        work = sort_tiles + cut(d1x, 6) + cut(d1r, 6) + cut(d1o, 6)
        w_l0 = [work[4 * g:4 * g + 4] for g in G]
        we = [work[12 * g:12 * g + 12] for g in G]
        wd = [work[9 * g:9 * g + 9] for g in DG]
        sc = [sb(f"sc{i}", [P, W, CH]) for i in range(4)]
        sm = [sb(f"sm{g}", [P, 8]) for g in G]
        s_tick_pool = sem("s_tick_pool")
        s_tick_pe = sem("s_tick_pe")
        s_tick_sp = sem("s_tick_sp")
        zeros = sb("zeros", [P, CH])
        s_x3z = sem("s_x3z")
        sgn_col = sb("sgn_col", [P, 1])
        bsum = sb("bsum", [P, 3])
        s_wd = sem("s_wd")
        s_lists = sem("s_lists")

        def par_sems(name, width=W):
            return [sem(f"{name}{g}") for g in range(width)]

        def after_chunk_before(wait, steps, i, name, g):
            wait(steps.sem, steps.at(i, name, g - 1) if g else steps.at(i - 1, name, W - 1))

        class Pass:
            def __init__(self, name, pe, act, dve):
                self.gst = par_sems(f"s_{name}_gst")
                self.sst = par_sems(f"s_{name}_sst")
                self.mk = par_sems(f"s_{name}_mk")
                self.gat = par_sems(f"s_{name}_gat")
                self.sca = par_sems(f"s_{name}_sca")
                self.pe = Steps(sem(f"s_{name}_pe"), *pe)
                self.act = Steps(sem(f"s_{name}_act"), *act)
                self.dve = Steps(sem(f"s_{name}_dve"), *dve)

        L0 = Pass("l0", ("z", "ea", "fs", "center", "var", "out"),
                  ("z", "sabs", "exps", "log", "gate", "sq", "ln", "rstd", "out"),
                  ("ea", "meta", "srelu", "core", "msg", "agg",
                   "t", "y", "x1"))
        ec_sem = par_sems("s_l0_ec")
        psg0 = par_sems("s_l0_pst")
        L1 = Pass("l1", ("z", "score", "xp", "out"),
                  ("pack", "z", "negm", "lncnt", "norm", "lrelu", "carry", "ex", "lnden", "rden", "out"),
                  ("cnt", "flag", "e", ("mrun", "mseg", "dcar"), "d", "val", ("carry", "den", "num"), "dmax", "att", "v2"))
        dl_sem = par_sems("s_l1_dst")
        h0_sem = par_sems("s_l0_h1")
        h1_sem = par_sems("s_l1_h1")
        s_l1_c = sem("s_l1_c")
        psg1 = par_sems("s_l1_pst")
        L2 = Pass("l2", ("z", "norm", "center", "var", "h", "out"),
                  ("pack", "z", "nout", "lncnt", "nin", "sq", "ln", "rstd", "logd", "lnlog", "rlog", "relu", "out"),
                  ("cnt", "fsel", "srcf", "rcnt", "x2", "msg", "agg", "aggn", "y3", "f2", "f3"))
        cn_sem = par_sems("s_l2_cn")
        cl_sem = par_sems("s_l3_cn")
        h3_sem = par_sems("s_l2_h3")
        sums3, spread3 = ("s1", "s2"), ("mean", "msq", "ms2", "vard", "var", "mx")
        heavy = [(name, g) for names, g in ((sums3 + spread3, 0), (sums3, 1), (("fp",), 0), (spread3, 1), (sums3, 2),
                                            (("fp",), 1), (spread3, 2), (("fp",), 2)) for name in names]
        L3 = Pass("l3", ("z", "ea", "h", "ew",
                          [("p", 0), ("u", 0), ("p", 1), ("g1", 0), ("g2", 0), ("u", 1), ("p", 2), ("g1", 1), ("g2", 1),
                           ("u", 2), ("g1", 2), ("g2", 2)], "center4", "var4", "out"),
                  ("z", "ea", "negm", "ha", "h", "hneg",
                   "hsq", [("lnvar", 0), ("std", 0), ("lnvar", 1), ("std", 1), ("u", 0), ("lnvar", 2), ("std", 2),
                    ("u", 1), ("u", 2)],
                   "rz", "n", "sq4", "ln4", "rstd4", "out"),
                  ("hw", heavy, "q", "a", "xn", "zxn", "o", "y4", "x4"))
        Q_act = Steps(sem("s_l3_ract"), "square", "ln", "rstd")
        Q_dve = Steps(sem("s_l3_rdve"), "sum", "mean", "centered", "sumsq", "norm")
        eal_sem = par_sems("s_l3_ea")

        dn = sb("dn", [P, DW, 8, TW])
        do = [sc[g][:, 0, :].rearrange("p (r c) -> p r c", r=8) for g in DG]
        dn_sem = par_sems("s_dn_in", DW)
        do_sem = par_sems("s_dn_out", DW)
        R_act = Steps(sem("s_dn_ract"), "square", "ln", "rstd", width=DW)
        R_dve = Steps(sem("s_dn_rdve"), "sum", "mean", "centered", "sumsq", "norm", width=DW)
        ds = flat(d1s)[:, 0:DW * 32].rearrange("p (g k r) -> p g k r", g=DW, k=4)
        pkr = [a.rearrange("p (r c) -> p r c", r=8) for a in pk_tiles]
        zr = [a.rearrange("p (r c) -> p r c", r=8) for a in z]
        D_pe = Steps(sem("s_dn_pe"), "z", "h", "c3", "v3", "gr", "gz", "gh", "gi", "c4", "v4", "out",
                     width=DW)
        D_act = Steps(sem("s_dn_act"), "z", "relu", "sq3", "ln3", "r3", "r", "zg", "n",
                      "sq4", "ln4", "r4", "out", width=DW)
        D_dve = Steps(sem("s_dn_dve"), "y3", "x3", "q", "a",
                      "xn", "zxn", "o", "y4", "x4", width=DW)

        DP = NODES // 8

        def dense_rows(i, g, ap):
            return ap[bass.ds((DW * i + g) * NODES, NODES), :].rearrange("(p r) c -> p r c", r=8)

        src_f = src.bitcast(F32).rearrange("(e a) -> e a", a=1)
        dst_r = dst.rearrange("(e a) -> e a", a=1)
        full, rest = E // SF, E % SF

        def col(ap):
            return ap.rearrange("(a b) -> a b", b=1)

        wloads = [
            (mats[:, :, :], k_mats),
            (w_fs_z[:, 0:C], Wf[0:P, :]), (w_fs_z[:, C:P], Ws[0:P, :]),
            (w_fs_e[:, 0:C], Wf[P:2 * P, :]), (w_fs_e[:, C:P], Ws[P:2 * P, :]),
            (b_fs[0:C, :], col(bf)), (b_fs[C:P, :], col(bs)),
            (w1_l[:, 0:C], W1), (w1_r[:, C:P], W1),
            (w1t[C:P, :], W1.rearrange("a b -> b a")),
            (att[:, 0:1], a_src.rearrange("a h d -> (h d) a")), (att[:, 1:2], a_dst.rearrange("a h d -> (h d) a")),
            (w2_bd[0:C, 0:C], W2.rearrange("a b -> b a")), (w2_bd[C:P, C:P], W2.rearrange("a b -> b a")),
            (b2_col[0:C, :], col(b2)), (b2_col[C:P, :], col(b2)),
            (w3t_l[:, 0:C], W3.rearrange("a b -> b a")), (w3t_r[:, C:P], W3.rearrange("a b -> b a")),
            (wpre2[:, :, 0:C], Wpre.rearrange("(k p) c -> p k c", k=3)),
            (wpre2[:, :, C:P], Wpre.rearrange("(k p) c -> p k c", k=3)),
            (wet[:, 0:3], We.rearrange("a b -> b a")),
            (be_col[:, :], col(be)), (bpre_col[0:C, :], col(bpre)), (bpre_col[C:P, :], col(bpre)),
            (wpm[:, C:P], Wpost[0:C, :]),
            (bpost_col[0:C, :], col(bpost)), (bpost_col[C:P, :], col(bpost)),
            (whh2[0:C, :], Whh), (whh2[C:P, :], Whh),
            (w_g1[0:C, 0:C], Whh[:, C:2 * C]), (w_g1[0:C, C:P], Whh[:, 0:C]),
            (w_g1[C:P, 0:C], Wih[:, C:2 * C]), (w_g1[C:P, C:P], Wih[:, 0:C]),
            (w_g2[0:C, C:P], Whh[:, 2 * C:3 * C]), (w_g2[C:P, 0:C], Wih[:, 2 * C:3 * C]),
            (wih2[:, :, 0:C], Wih.rearrange("p (g c) -> p g c", g=3)),
            (wih2[:, :, C:P], Wih.rearrange("p (g c) -> p g c", g=3)),
            (nv[:, :], node_vec.rearrange("(p a) -> p a", p=125)),
        ]
        post = {(s, k): C + 4 * C * s + C * k for s in range(3) for k in range(4)}
        MEAN, MIN, MAX, STD = range(4)
        for half, a1, a2 in ((0, MEAN, MIN), (C, STD, MAX)):
            for s, cols in ((1, slice(0, C)), (2, slice(C, P))):
                wloads.append((wp_a1[half:half + C, cols], Wpost[post[s, a1]:post[s, a1] + C, :]))
                wloads.append((wp_a2[half:half + C, cols], Wpost[post[s, a2]:post[s, a2] + C, :]))
            wloads.append((wu_a1[half:half + C, C:P], Wpost[post[0, a1]:post[0, a1] + C, :]))
            wloads.append((wu_a2[half:half + C, C:P], Wpost[post[0, a2]:post[0, a2] + C, :]))
        for s in range(3):
            wloads.append((wstd[:, s, :], Wpost[post[s, STD]:post[s, STD] + C, :]))
        for h in (0, C):
            for g in range(3):
                wloads.append((brow[h:h + C, 0, g:g + 1], col(bih[g * C:(g + 1) * C])))
                wloads.append((brow[h:h + C, 1, g:g + 1], col(bhh[g * C:(g + 1) * C])))
        NW = 16 * len(wloads)

        zeroed = [w1_l, w1_r, w2_bd, w2_neg, w3t_l, w3t_r, wet, wu_a1, wu_a2, wu_f, wpm, w_g2, dg]

        turn_plan = []

        block = ctx.enter_context(nc.Block())

        ALL = 64 * ROUNDS

        def again(wait, s, count, i):
            if not (isinstance(i, int) and i == 0):
                wait(s, count * i)

        def fills(i):
            return not (isinstance(i, int) and i == 0)

        def over_rounds(eng, body, last=ROUNDS, peel=1):
            for i in range(peel):
                body(i)
            with eng.Fori(peel, last) as i:
                body(i)

        @block.sync
        def _(sp):
            H, U = slice(0, C), slice(C, P)

            def hold(s, v):
                sp.wait_ge(s, v)
                sp.sem_inc(s_tick_sp, 1)

            def after(steps, i, name, g=0):
                hold(steps.sem, steps.at(i, name, g))

            sp.wait_ge(s_keym, 1)
            for s, a in ((0, dst), (1, src)):
                sp.dma_start(keys[0:full, s, :], a[0:full * SF].rearrange("(p f) -> p f", f=SF)).then_inc(s_keyl, 16)
                sp.dma_start(keys[full:full + 1, s, 0:rest], a[full * SF:E].rearrange("(p f) -> p f", p=1)).then_inc(s_keyl, 16)
            sp.dma_start(kidx[:, :, :], k_idx).then_inc(s_keyl, 16)
            sp.dma_start(ksign[:, :, :], k_sign).then_inc(s_keyl, 16)
            sp.wait_ge(s_wzero, len(zeroed))
            for d, s in wloads:
                sp.dma_start(d, s).then_inc(s_wload, 16)
            sp.dma_start(EC[:, 0:2 * C], ea128).then_inc(s_ec, 16)
            sp.dma_start(EC[:, 2 * C:2 * C + 4], ea4).then_inc(s_ec, 16)
            sp.dma_start(EC[:, 2 * C + 4:EW], src_f).then_inc(s_ec, 16)

            sp.wait_ge(s_const, 3)
            per = N // P * C
            x3_rows = X3[0:P * (N // P), :].rearrange("(p r) c -> p (r c)", p=P)
            sp.dma_start(x3_rows[:, 0:per // CH * CH].rearrange("p (a b) -> p a b", b=CH),
                         zeros[:, :].unsqueeze(1).broadcast_to([P, per // CH, CH])).then_inc(s_x3z, 16)
            sp.dma_start(x3_rows[:, per // CH * CH:per], zeros[:, 0:per % CH]).then_inc(s_x3z, 16)
            sp.dma_start(X3[P * (N // P):N, :], zeros[0:N % P, 0:C]).then_inc(s_x3z, 16)

            sp.wait_ge(s_kd, 1)
            for s in range(2):
                sp.dma_start(KD[s, 1:SN + 1].rearrange("(p f) -> p f", p=P), sf[0][:, s, :]).then_inc(s_kr, 16)
                sp.dma_start(KD[s:s + 1, 0:1], edge_col[0:1, 0:1]).then_inc(s_kr, 16)
                sp.dma_start(KD[s:s + 1, SN + 1:SN + 2], edge_col[0:1, 1:2]).then_inc(s_kr, 16)
            sp.wait_ge(s_kr, 6 * 16)
            for s in range(2):
                sp.dma_start(sf[1][:, s, :], KD[s, 0:SN].rearrange("(p f) -> p f", p=P)).then_inc(s_kr, 16)
                sp.dma_start(sf[2][:, s, :], KD[s, 2:SN + 2].rearrange("(p f) -> p f", p=P)).then_inc(s_kr, 16)
            sp.wait_ge(s_kd, 2)
            for s in range(2):
                sp.dma_start(MK[s, 0:SN].rearrange("(p f) -> p f", p=P), sf[3][:, s, :]).then_inc(s_mk, 16)
            sp.wait_ge(s_mk, 32)
            sp.wait_ge(s_idx, 7)

            def stage(tile, g, row, i, done):
                sp.dma_start(tile, idx[:, row, bass.ds((W * i + g) * 4, 4)]).then_inc(done[g], 16)

            def heads(L, row, i):
                for g in G:
                    again(hold, L.sca[g], 64, i)
                    stage(sst[:, g, :], g, row, i, L.sst)

            def load_mask(L, g, s, i):
                sp.dma_start(mk[:, g, 0:CH], MK[s, bass.ds((W * i + g) * CH, CH)].partition_broadcast(P)).then_inc(L.mk[g], 16)

            def rows_of(table, i, g):
                return table[bass.ds((W * i + g) * P, P), :].rearrange("p (t k) -> p t k", t=4)

            def l0_in(i):
                for g in G:
                    again(hold, ec_sem[g], 64, i)
                    stage(pst[:, g, :], g, I_PERMD, i, psg0)
                for g in G:
                    again(hold, L0.gat[g], 128, i)
                    stage(gst[:, g, 0, :], g, I_DSTC, i, L0.gst)
                for g in G:
                    after(L0.dve, i - 1, "agg", g)
                    load_mask(L0, g, 0, i)

            def l0_out(i):
                for g in G:
                    after(L0.act, i, "out", g)
                    sp.dma_start(rows_of(H1, i, g), ot[:, g, :, :]).then_inc(h0_sem[g], 16)

            def dense1_in(i):
                after(d1_dve, i - 1, "y")
                sp.dma_start(d1x[0:D1P, :, :], rows1(x, i)).then_inc(s_d1l, 16)

            def dense1_out(i):
                after(d1_dve, i, "norm")
                sp.dma_start(rows1(T, i), d1o[0:D1P, :, :]).then_inc(s_d1o, 16)

            def l0(i):
                l0_in(i + 1)
                dense1_in(i + 1)
                if fills(i):
                    dense1_out(i)
                l0_out(i)
            l0_in(0)
            over_rounds(sp, l0, ROUNDS - 1)
            dense1_out(ROUNDS - 1)
            l0_out(ROUNDS - 1)
            for g in G:
                sp.wait_ge(h0_sem[g], 16 * ROUNDS)

            def scatter_in(L, row):
                def rows_in(i):
                    for g in G:
                        again(hold, L.sca[g], 64, i)
                        sp.dma_start(ot[:, g, :, :], rows_of(H1, i, g)).then_inc(L.sst[g], 16)
                        stage(sst[:, g, :], g, row, i, L.sst)
                over_rounds(sp, rows_in)
                for g in G:
                    sp.wait_ge(L.sca[g], ALL)
            scatter_in(L0, I_DSTH)

            def l1_in(i):
                for g in G:
                    again(hold, dl_sem[g], 64, i)
                    stage(pst[:, g, :], g, I_PERMS, i, psg1)
                for g in G:
                    again(hold, L1.gat[g], 128, i)
                    stage(gst[:, g, 0, :], g, I_SRCC, i, L1.gst)
                for g in G:
                    after(L1.dve, i - 1, "num", g)
                    load_mask(L1, g, 1, i)

            def l1_out(i):
                for g in G:
                    after(L1.act, i, "out", g)
                    after(L1.dve, i, "flag", g)
                    sp.dma_start(rows_of(H1, i, g), ot[:, g, :, :]).then_inc(h1_sem[g], 16)

            def l1(i):
                l1_in(i + 1)
                l1_out(i)
            l1_in(0)
            over_rounds(sp, l1, ROUNDS - 1)
            l1_out(ROUNDS - 1)
            for g in G:
                sp.wait_ge(h1_sem[g], 16 * ROUNDS)

            scatter_in(L1, I_SRCH)

            def dense_in(i):
                for g in DG:
                    after(R_dve, i - 1, "centered", g)
                    sp.dma_start(dn[0:DP, g, :, :], dense_rows(i, g, T)).then_inc(dn_sem[g], 16)

            def dense_out(i):
                for g in DG:
                    after(D_act, i, "out", g)
                    sp.dma_start(dense_rows(i, g, out), do[g][0:DP, :, :]).then_inc(do_sem[g], 16)

            def dense(i):
                dense_in(i + 1)
                dense_out(i)
            dense_in(0)
            over_rounds(sp, dense, DROUNDS - 1)
            dense_out(DROUNDS - 1)
            for g in DG:
                sp.wait_ge(do_sem[g], 16 * DROUNDS)

            def l2_in(i):
                for g in G:
                    again(hold, L2.gat[g], 128, i)
                    after(L2.dve, i - 1, "srcf", g)
                    stage(gst[:, g, 0, :], g, I_DSTC, i, L2.gst)
                    stage(gst[:, g, 1, :], g, I_SRCD, i, L2.gst)
                for g in G:
                    after(L2.dve, i - 1, "agg", g)
                    load_mask(L2, g, 0, i)

            def l2_out(i):
                heads(L2, I_DSTH, i)
                for g in G:
                    after(L2.act, i, "out", g)
                    sp.dma_start(rows_of(H3, i, g), ot3[:, g, :, C:P]).then_inc(h3_sem[g], 16)
                for g in G:
                    after(L2.dve, i, "f3", g)
                    for k, tile in enumerate((11, 7, 10)):
                        sp.dma_start(CN[k:k + 1, bass.ds((W * i + g) * CH, CH)], we[g][tile][0:1, :]).then_inc(cn_sem[g], 16)

            def l2(i):
                l2_in(i + 1)
                l2_out(i)
            l2_in(0)
            over_rounds(sp, l2, ROUNDS - 1)
            l2_out(ROUNDS - 1)
            for g in G:
                sp.wait_ge(h3_sem[g], 16 * ROUNDS)
                sp.wait_ge(cn_sem[g], 48 * ROUNDS)
                sp.wait_ge(L2.sca[g], ALL)

            def rows_in(i):
                for g in G:
                    after(Q_dve, i - 1, "centered", g)
                    sp.dma_start(gat[:, g, :, C:P], rows_of(H3, i, g)).then_inc(L3.gst[g], 16)
                    stage(gst[:, g, 0, :], g, I_DSTR, i, L3.gst)
                    stage(gst[:, g, 1, :], g, I_SRCF, i, L3.gst)

            def l3_in(i):
                for g in G:
                    after(L3.pe, i - 1, "ea", g)
                    sp.dma_start(eas[:, g, :, :], ea4d[:, bass.ds((W * i + g) * 4, 4), :]).then_inc(eal_sem[g], 16)
                for g in G:
                    after(L3.dve, i - 1, "mx", g)
                    load_mask(L3, g, 0, i)
                for g in G:
                    after(L3.dve, i - 1, "fp", g)
                    row = bass.ds((W * i + g) * CH, CH)
                    for k, dest in enumerate((sc[3][:, g, :], ear[g][H, :], ear[g][U, :])):
                        sp.dma_start(dest, CN[k, row].partition_broadcast(P if k == 0 else C)).then_inc(cl_sem[g], 16)

            rows_in(0)
            l3_in(0)
            rows_in(1)

            def l3(i):
                heads(L3, I_DSTH, i)
                l3_in(i + 1)
                rows_in(i + 2)
            over_rounds(sp, l3, ROUNDS - 2)
            heads(L3, I_DSTH, ROUNDS - 2)
            l3_in(ROUNDS - 1)
            heads(L3, I_DSTH, ROUNDS - 1)
            for g in G:
                sp.wait_ge(L3.sca[g], ALL)

        @block.gpsimd
        def _(pool):
            for a in zeroed:
                pool.memset(a[(slice(None),) * len(a.shape)], 0.0).then_inc(s_wzero, 1)
            def hold(s, v):
                pool.wait_ge(s, v)
                pool.sem_inc(s_tick_pool, 1)

            def hold_after(steps, i, name, g=0):
                hold(steps.sem, steps.at(i, name, g))

            node_bound = pool.to_reg(N - 1)

            def gather(dest, table, index, done):
                pool.indirect_dma_start(out=dest, out_offset=None, in_=table,
                                        in_offset=bass.IndirectOffsetOnAxis(ap=index, axis=0),
                                        bounds_check=node_bound, oob_is_err=False).then_inc(done, 16)

            def scatter(table, index, source, done):
                pool.indirect_dma_start(out=table, out_offset=bass.IndirectOffsetOnAxis(ap=index, axis=0),
                                        in_=source, in_offset=None,
                                        bounds_check=node_bound, oob_is_err=False).then_inc(done, 16)

            pool.wait_ge(s_ec, 48)

            def edge_rows(i):
                for g in G:
                    hold(psg0[g], 16 * (i + 1))
                    hold_after(L0.pe, i - 1, "ea", g)
                    hold_after(L0.dve, i - 1, "meta", g)
                    for t in range(4):
                        gather(eca[:, g, t, :], EC, pst[:, g, t:t + 1], ec_sem[g])

            def gathers0(i):
                for g in G:
                    hold(L0.gst[g], 16 * (i + 1))
                    hold_after(L0.pe, i - 1, "z", g)
                    for t in range(4):
                        gather(gat[:, g, t, 0:C], x, gst[:, g, 0, t:t + 1], L0.gat[g])
                for g in G:
                    hold(ec_sem[g], 64 * (i + 1))
                    for t in range(4):
                        gather(gat[:, g, t, C:P], x, eca[:, g, t, EW - 1:EW].bitcast(U32), L0.gat[g])

            def l0(i):
                edge_rows(i)
                gathers0(i)
            over_rounds(pool, l0)

            def scatter_kept(L):
                def rows_out(i):
                    for g in G:
                        hold(L.sst[g], 32 * (i + 1))
                        for t in range(4):
                            scatter(T, sst[:, g, t:t + 1], ot[:, g, t, :], L.sca[g])
                over_rounds(pool, rows_out)
                for g in G:
                    pool.wait_ge(L.sca[g], ALL)
            pool.wait_ge(s_d1o, 16 * (ROUNDS - 1))
            scatter_kept(L0)

            def dst_rows(i):
                for g in G:
                    hold(psg1[g], 16 * (i + 1))
                    again(hold, L1.gat[g], 128, i)
                    for t in range(4):
                        gather(dli[:, g, t:t + 1], dst_r, pst[:, g, t:t + 1], dl_sem[g])

            def gathers1(i):
                for g in G:
                    hold(L1.gst[g], 16 * (i + 1))
                    hold_after(L1.act, i - 1, "pack", g)
                    hold_after(L1.dve, i - 1, "flag", g)
                    for t in range(4):
                        gather(gat[:, g, t, 0:TW], T, gst[:, g, 0, t:t + 1], L1.gat[g])
                    hold(dl_sem[g], 64 * (i + 1))
                    for t in range(4):
                        gather(gat[:, g, t, TW:2 * TW], T, dli[:, g, t:t + 1].bitcast(U32), L1.gat[g])

            def l1(i):
                gathers1(i)
                dst_rows(i + 1)
            dst_rows(0)
            over_rounds(pool, l1, ROUNDS - 1)
            gathers1(ROUNDS - 1)

            scatter_kept(L1)

            def gathers2(i):
                for g in G:
                    hold(L2.gst[g], 32 * (i + 1))
                    hold_after(L2.act, i - 1, "pack", g)
                    hold_after(L2.pe, i - 1, "norm", g)
                    hold_after(L2.dve, i - 1, "fsel", g)
                    for t in range(4):
                        gather(gat[:, g, t, 0:TW], T, gst[:, g, 0, t:t + 1], L2.gat[g])
                        gather(gat[:, g, t, TW:2 * TW], T, gst[:, g, 1, t:t + 1], L2.gat[g])

            def scatters2(i):
                for g in G:
                    hold_after(L2.act, i, "out", g)
                    hold(L2.sst[g], 16 * (i + 1))
                    for t in range(4):
                        scatter(X3, sst[:, g, t:t + 1], ot3[:, g, t, 0:C], L2.sca[g])

            def l2(i):
                gathers2(i + 1)
                scatters2(i)
            pool.wait_ge(s_x3z, 48)
            gathers2(0)
            over_rounds(pool, l2, ROUNDS - 1)
            scatters2(ROUNDS - 1)
            for g in G:
                pool.wait_ge(L2.sca[g], ALL)

            for g in DG:
                pool.wait_ge(do_sem[g], 16 * DROUNDS)

            def gathers3(i):
                for g in G:
                    hold(L3.gst[g], 48 * (i + 1))
                    hold_after(Q_dve, i - 1, "centered", g)
                    for t in range(4):
                        gather(gat[:, g, t, 0:C], X3, gst[:, g, 0, t:t + 1], L3.gat[g])
                        gather(gat[:, g, t, C:P], X3, gst[:, g, 1, t:t + 1], L3.gat[g])

            def scatters3(i):
                for g in G:
                    hold_after(L3.act, i, "out", g)
                    hold(L3.sst[g], 16 * (i + 1))
                    for t in range(4):
                        scatter(out, sst[:, g, t:t + 1], ot3[:, g, t, 0:C], L3.sca[g])

            def l3(i):
                gathers3(i + 2)
                scatters3(i)
            gathers3(0)
            gathers3(1)
            over_rounds(pool, l3, ROUNDS - 2)
            scatters3(ROUNDS - 2)
            scatters3(ROUNDS - 1)
            for g in G:
                pool.wait_ge(L3.sca[g], ALL)

        blk = [slice(128 * t, 128 * (t + 1)) for t in range(4)]

        @block.vector
        def _(dve):
            H = slice(0, C)
            U = slice(C, P)

            def after_(steps, i, name, g=0):
                dve.wait_ge(steps.sem, steps.at(i, name, g))

            def tt(done, out_, a, b, op):
                dve.tensor_tensor(out_, a, b, op).then_inc(done, 1)

            def ts(done, out_, a, s1, s2, op0, op1=None):
                if op1 is None:
                    dve.tensor_scalar(out_, a, s1, None, op0).then_inc(done, 1)
                else:
                    dve.tensor_scalar(out_, a, s1, s2, op0, op1).then_inc(done, 1)

            def stt(done, out_, a, s, b, op0, op1):
                dve.scalar_tensor_tensor(out=out_, in0=a, scalar=s, in1=b, op0=op0, op1=op1).then_inc(done, 1)

            def scan(done, out_, d0, d1, initial, op0, op1):
                dve.tensor_tensor_scan(out=out_, data0=d0, data1=d1, initial=initial, op0=op0, op1=op1).then_inc(done, 1)

            for S in (L0.dve, L1.dve, L2.dve, L3.dve, D_dve, R_dve, Q_dve):
                dve.sem_inc(S.sem, S.n)
            dve.sem_inc(d1_dve.sem, 2 * d1_dve.n)

            dve.memset(keys[:, :, :], N).then_inc(s_keym, 1)
            dve.memset(eps_col[:, :], EPS).then_inc(s_const, 1)
            dve.memset(one_col[:, :], 1.0).then_inc(s_const, 1)
            dve.memset(sgn_col[0:C, :], -1.0)
            dve.memset(sgn_col[C:P, :], 1.0)
            for a in (gat, ot, ot3, dn):
                dve.memset(a[:, :, :, :], 0.0)
            dve.memset(ones[:, :], 1.0)
            dve.memset(zeros[:, :], 0.0)
            for a in sc:
                dve.memset(a[:, :, :], 0.0)
            for g in G:
                dve.memset(negm[g][:, CH:CH + 1], 0.0)
            dve.memset(edge_col[0:1, 0:1], -1.0)
            dve.memset(edge_col[0:1, 1:2], -2.0)
            dve.memset(d1o[:, :, C:TW], 0.0).then_inc(s_const, 1)

            setup = Count(s_wd)
            dve.wait_ge(s_wload, NW)
            dve.wait_ge(s_const, 3)
            for a in (w_fs_z[:, 0:C], w_fs_e[:, 0:C], b_fs[0:C, :]):
                setup.tick(dve.tensor_scalar(a, a, -1.0, None, ALU.mult))
            setup.tick(dve.memset(ot[:, :, :, TW - 1:TW], 1.0))
            for k in range(2):
                setup.tick(dve.tensor_scalar(att_m[:, k, :], headmask[0:C, 0:C], att[:, k:k + 1], None, ALU.mult))
            dve.memset(avgmat[:, :], 1.0 / N).then_inc(s_wdve, 1)
            dve.wait_ge(s_wact, 1)
            dve.reduce_sum(nvs[:, :], nv[:, :], AX_X).then_inc(s_wdve, 1)
            dve.wait_ge(s_wd, setup.n)
            dve.tensor_scalar(w2_neg[C:P, 0:C], w2_bd[C:P, C:P], -1.0, None, ALU.mult).then_inc(s_wdve, 1)
            for a in (wp_a2[0:C, :], wu_a2[0:C, C:P]):
                setup.tick(dve.tensor_scalar(a, a, -1.0, None, ALU.mult))
            for h in (0, C):
                setup.tick(dve.tensor_copy(wu_f[h:h + C, C:P], ident[h:h + C, h:h + C]))
            setup.tick(dve.tensor_tensor(bsum[:, :], brow[:, 0, :], brow[:, 1, :], ALU.add))
            dve.wait_ge(s_wd, setup.n)
            setup.tick(dve.tensor_copy(b_g1[0:C, :], bsum[0:C, 1:2]))
            setup.tick(dve.tensor_copy(b_g1[C:P, :], bsum[C:P, 0:1]))
            dve.wait_ge(s_wpe, 1)
            setup.tick(dve.tensor_copy(w_score[:, :], banks[0][:, 0:C]))
            setup.tick(dve.tensor_copy(w_h[:, :], banks[1][:, 0:P]))
            setup.tick(dve.tensor_copy(w_hea[:, :], banks[2][0:4, 0:P]))
            setup.tick(dve.tensor_copy(bew_col[:, :], banks[2][:, 256:257]))
            setup.tick(dve.tensor_copy(wu_x[:, :], banks[3][0:C, 0:P]))
            setup.tick(dve.tensor_copy(avg[:, :], banks[4][:, 0:1]))
            setup.tick(dve.reciprocal(iavg[:, :], banks[4][:, 0:1]))
            dve.wait_ge(s_wact, 4)
            dve.wait_ge(s_wd, setup.n)
            setup.tick(dve.tensor_scalar(fac0[:, 2:3], fac0[:, 1:2], iavg[0:C, :], None, ALU.mult))
            setup.tick(dve.reciprocal(fac0[:, 3:4], fac0[:, 1:2]))
            dve.wait_ge(s_wd, setup.n)
            setup.tick(dve.tensor_scalar(fac0[:, 5:6], fac0[:, 2:3], fac0[:, 4:5], None, ALU.mult))
            setup.tick(dve.tensor_scalar(fac0[:, 7:8], fac0[:, 3:4], avg[0:C, :], None, ALU.mult))
            dve.wait_ge(s_wd, setup.n)
            dve.tensor_scalar(fac0[:, 6:7], fac0[:, 7:8], fac0[:, 5:6], None, ALU.mult).then_inc(s_wdve, 1)
            setup.tick(dve.tensor_copy(mmt2[:, 0:C], banks[3][0:C, 256:256 + C]))
            setup.tick(dve.tensor_copy(mmt2[:, C:P], banks[3][0:C, 256:256 + C]))
            dve.wait_ge(s_wd, setup.n)
            dve.wait_ge(s_wpe, 2)
            dve.tensor_tensor(out0[:, :], banks[5][0:C, 0:1], bpost_col[0:C, :], ALU.add).then_inc(s_wdve, 1)
            dve.wait_ge(s_wpe, 3)
            for g in range(2):
                setup.tick(dve.tensor_scalar(dg_b[:, g:g + 1], banks[6][:, 8 * g:8 * g + 1], bsum[:, g:g + 1], None, ALU.add))
            setup.tick(dve.tensor_scalar(dg_b[:, 2:3], banks[6][:, 16:17], brow[:, 0, 2:3], None, ALU.add))
            setup.tick(dve.tensor_copy(dg_b[:, 3:4], brow[:, 1, 2:3]))
            for h in (0, C):
                r = slice(h, h + C)
                for g in range(2):
                    setup.tick(dve.tensor_tensor(dg[r, g, r], banks[7][r, g * C:(g + 1) * C], whh2[r, g * C:(g + 1) * C], ALU.add))
                setup.tick(dve.tensor_copy(dg[r, 2, r], banks[7][r, 2 * C:3 * C]))
                setup.tick(dve.tensor_copy(dg[r, 3, r], whh2[r, 2 * C:3 * C]))
            dve.wait_ge(s_wd, setup.n)

            cnt_ = Count(s_sort)

            def go(ins):
                cnt_.tick(ins)
                dve.wait_ge(s_sort, cnt_.n)

            dve.wait_ge(s_keyl, 96)
            f = [a[:, :, :] for a in sf]
            i_ = [a[:, :, :] for a in si]
            go(dve.tensor_copy(f[0], keys[:, :, :]))
            go(dve.tensor_scalar(f[1], f[0], MID, None, ALU.subtract))
            go(dve.tensor_scalar(f[2], f[0], MID, None, ALU.is_lt))
            go(dve.scalar_tensor_tensor(out=f[5], in0=f[1], scalar=-1.0, in1=f[1], op0=ALU.mult, op1=ALU.max))
            go(dve.tensor_scalar(i_[0], f[5], MARGIN, None, ALU.add))
            go(dve.tensor_scalar(f[3], kidx[:, :, :], -2.0, float(SN - 1), ALU.mult, ALU.add))
            go(dve.tensor_tensor(f[4], f[3], f[2], ALU.mult))
            go(dve.tensor_tensor(i_[1], f[4], kidx[:, :, :], ALU.add))
            go(dve.tensor_copy(i_[2], f[2]))
            go(dve.tensor_scalar(i_[0], i_[0], SK, None, ALU.logical_shift_left))
            go(dve.tensor_scalar(i_[2], i_[2], 31, None, ALU.logical_shift_left))
            go(dve.tensor_tensor(i_[0], i_[0], i_[1], ALU.bitwise_or))
            go(dve.tensor_tensor(sx[:, :, :].bitcast(I32), i_[0], i_[2], ALU.bitwise_or))
            cur, oth = sx, sy
            turns = 0

            def compare(view, d):
                nonlocal cur, oth
                a, b = view(cur, d), view(oth, d)
                cnt_.tick(dve.tensor_tensor(b[:, :, 0, :], a[:, :, 0, :], a[:, :, 1, :], ALU.min))
                go(dve.tensor_tensor(b[:, :, 1, :], a[:, :, 0, :], a[:, :, 1, :], ALU.max))
                cur, oth = oth, cur

            def view(a, d):
                return a[:, :, :].rearrange("p s (n two d) -> p (s n) two d", two=2, d=d)

            def view_t(a, d):
                return a[:, :, :].rearrange("p s (h n two d) -> p (s h n) two d", h=2, two=2, d=d)

            def turn():
                nonlocal cur, oth, turns
                turn_plan.append((cur, cnt_.n))
                turns += 1
                dve.wait_ge(s_sortt, turns)
                go(dve.tensor_copy(oth[:, :, :].rearrange("p s f -> p (s f)"), banks[0][:, :]))
                cur, oth = oth, cur

            for k in range(1, SK + 1):
                cnt_.tick(dve.tensor_tensor(oth[:, 0, :], cur[:, 0, :], ksign[:, k - 1, :], ALU.mult))
                go(dve.tensor_tensor(oth[:, 1, :], cur[:, 1, :], ksign[:, k - 1, :], ALU.mult))
                cur, oth = oth, cur
                if k > 8:
                    turn()
                    for b in range(k - 9, -1, -1):
                        compare(view_t, 1 << b)
                    turn()
                for b in range(min(k, 8) - 1, -1, -1):
                    compare(view, 1 << b)

            bits = cur[:, :, :].bitcast(I32)
            go(dve.tensor_scalar(i_[0], bits, SK, 0xFFFF, ALU.logical_shift_right, ALU.bitwise_and))
            go(dve.tensor_scalar(i_[1], bits, SN - 1, None, ALU.bitwise_and))
            go(dve.tensor_scalar(i_[2], bits, 31, 1, ALU.logical_shift_right, ALU.bitwise_and))
            go(dve.tensor_scalar(f[1], i_[0], MARGIN, None, ALU.subtract))
            go(dve.tensor_copy(f[2], i_[2]))
            go(dve.tensor_scalar(f[3], f[2], -2.0, 1.0, ALU.mult, ALU.add))
            go(dve.tensor_tensor(f[4], f[1], f[3], ALU.mult))
            go(dve.tensor_copy(f[5], i_[1]))
            go(dve.tensor_scalar(f[3], f[5], -2.0, float(SN - 1), ALU.mult, ALU.add))
            go(dve.tensor_tensor(f[3], f[3], f[2], ALU.mult))
            go(dve.tensor_tensor(f[5], f[5], f[3], ALU.add))
            for s, k in ((0, I_PERMD), (1, I_PERMS)):
                go(dve.tensor_scalar(lists[:, k, :], sf[5][:, s, :], float(E - 1), None, ALU.min))
            dve.tensor_scalar(f[0], f[4], MID, None, ALU.add).then_inc(s_kd, 1)
            dve.wait_ge(s_kd, 1)
            dve.wait_ge(s_kr, 160)
            dve.tensor_tensor(f[3], f[0], f[1], ALU.is_equal).then_inc(s_kd, 1)
            go(dve.tensor_tensor(f[4], f[0], f[2], ALU.is_equal))
            for s, k in ((0, I_DSTC), (1, I_SRCC)):
                go(dve.tensor_scalar(lists[:, k, :], sf[0][:, s, :], float(N - 1), None, ALU.min))
            go(dve.tensor_copy(lists[:, I_DSTR, :], sf[0][:, 0, :]))
            for s, k in ((0, I_DSTH), (1, I_SRCH)):
                ins = dve.scalar_tensor_tensor(out=lists[:, k, :], in0=sf[4][:, s, :], scalar=float(SKIP),
                                               in1=sf[0][:, s, :], op0=ALU.mult, op1=ALU.add)
                go(ins)
            dve.sem_inc(s_lists, 1)
            for k in range(7):
                dve.wait_ge(s_lt, k + 1)
                dve.tensor_copy(idx[:, k, :].rearrange("q (p h) -> q h p", h=2),
                                banks[k][:, 0:2 * P].rearrange("q (h p) -> q h p", h=2)[:, :, 0:NT // 2]).then_inc(s_idx, 1)

            def last_of(a, g, rows):
                return a[rows, (g - 1) % W, CH - 1:CH]

            rows, xs = d1o[0:D1P, :, 0:C], d1x[0:D1P, :, :]

            def per_row(a):
                return a.unsqueeze(2).broadcast_to([D1P, R1, C])

            def l0(i):
                L = L0
                for g in G:
                    after_(L.pe, i, "ea", g)
                    after_(L.pe, i - 1, "fs", g)
                    dve.tensor_copy(ear[g][:, :], ps[g][1][:, :]).then_inc(L.dve.done("ea"), 1)
                for g in G:
                    dve.wait_ge(ec_sem[g], 64 * (i + 1))
                    dve.tensor_copy(ea4d[:, bass.ds((W * i + g) * 4, 4), :], eca[:, g, :, 2 * C:2 * C + 4])
                    dve.tensor_copy(idx[:, I_SRCD, bass.ds((W * i + g) * 4, 4)],
                                    eca[:, g, :, EW - 1].bitcast(U32)).then_inc(L.dve.done("meta"), 1)
                if fills(i):
                    dve.wait_ge(s_d1l, 16 * i)
                    after_(d1_act, i - 1, "square")
                    if not isinstance(i, int):
                        dve.wait_ge(s_d1o, 16 * i - 16)
                    stt(d1_dve.done("y"), rows, xs, 0.0, xs, ALU.max, ALU.add)
                    after_(d1_dve, i, "y")
                    dve.reduce_sum(d1s[0:D1P, 0, :], rows, AX_X).then_inc(d1_dve.done("sum"), 1)
                for g in G:
                    after_(L.pe, i, "fs", g)
                    after_(L.act, i, "sabs", g)
                    after_(L.dve, i - 1, "core", g)
                    ts(L.dve.done("srelu"), w_l0[g][1][:, :], ps[g][0][:, :], b_fs[:, :], 0.0, ALU.add, ALU.max)
                for g in G:
                    after_(L.act, i, "log", g)
                    after_(L.dve, i, "srelu", g)
                    after_(L.act, i - 1, "gate", g)
                    tt(L.dve.done("core"), w_l0[g][1][:, :], w_l0[g][1][:, :], w_l0[g][0][:, :], ALU.add)
                for g in G:
                    after_(L.act, i, "gate", g)
                    after_(L.dve, i, "core", g)
                    tt(L.dve.done("msg"), w_l0[g][3][H, :], w_l0[g][1][U, :], w_l0[g][2][U, :], ALU.mult)
                if fills(i):
                    after_(d1_dve, i, "sum")
                    ts(d1_dve.done("mean"), d1s[0:D1P, 0, :], d1s[0:D1P, 0, :], 1.0 / C, None, ALU.mult)
                    after_(d1_dve, i, "mean")
                    tt(d1_dve.done("centered"), rows, rows, per_row(d1s[0:D1P, 0, :]), ALU.subtract)
                for g in G:
                    dve.wait_ge(L.mk[g], 16 * (i + 1))
                    after_(L.dve, i, "msg", g)
                    after_chunk_before(dve.wait_ge, L.dve, i, "agg", g)
                    scan(L.dve.done("agg"), sc[0][H, g, :], mk[H, g, 0:CH], w_l0[g][3][H, :], last_of(sc[0], g, H), ALU.mult, ALU.add)
                for g in G:
                    after_(L.dve, i, "agg", g)
                    after_(L.act, i, "z", g)
                    tt(L.dve.done("t"), w_l0[g][0][H, :], sc[0][H, g, :], z[g][H, :], ALU.add)
                for g in G:
                    after_(L.dve, i, "t", g)
                    after_(L.pe, i - 1, "center", g)
                    stt(L.dve.done("y"), w_l0[g][1][H, :], w_l0[g][0][H, :], 0.0, z[g][H, :], ALU.max, ALU.add)
                if fills(i):
                    after_(d1_act, i, "square")
                    dve.reduce_sum(d1s[0:D1P, 1, :], d1r[0:D1P, :, :], AX_X).then_inc(d1_dve.done("sumsq"), 1)
                for g in G:
                    after_(L.act, i, "rstd", g)
                    after_(L.pe, i - 1, "out", g)
                    tt(L.dve.done("x1"), w_l0[g][2][H, :], ps[g][1][H, :], w_l0[g][0][H, :], ALU.mult)
                if fills(i):
                    after_(d1_act, i, "rstd")
                    tt(d1_dve.done("norm"), rows, rows, per_row(d1s[0:D1P, 3, :]), ALU.mult)
            over_rounds(dve, l0, peel=2)

            def l1(i):
                L = L1
                for g in G:
                    dve.wait_ge(L.mk[g], 16 * (i + 1))
                    after_(L.pe, i - 1, "out", g)
                    after_chunk_before(dve.wait_ge, L.dve, i, "cnt", g)
                    scan(L.dve.done("cnt"), sc[3][C:C + 1, g, :], mk[C:C + 1, g, 0:CH], ones[C:C + 1, :],
                         last_of(sc[3], g, slice(C, C + 1)), ALU.mult, ALU.add)
                for g in G:
                    again(dve.wait_ge, h1_sem[g], 16, i)
                    dve.wait_ge(L.gat[g], 128 * (i + 1))
                    dve.tensor_copy(ot[:, g, :, TW - 1:TW], gat[:, g, :, TW - 1:TW]).then_inc(L.dve.done("flag"), 1)
                for g in G:
                    after_(L.act, i, "lrelu", g)
                    after_(L.dve, i - 1, "d", g)
                    tt(L.dve.done("e"), we[g][1][H, :], ps[g][1][H, :], we[g][0][H, :], ALU.max)
                for g in G:
                    after_(L.dve, i, "e", g)
                    after_(L.act, i, "negm", g)
                    after_chunk_before(dve.wait_ge, L.dve, i, "dcar", g)
                    scan(L.dve.done("mrun"), sc[0][H, g, :], negm[g][H, 0:CH], we[g][1][H, :], last_of(sc[0], g, H), ALU.add, ALU.max)
                    after_(L.dve, i, "mrun", g)
                    scan(L.dve.done("mseg"), we[g][3][H, ::-1], negm[g][H, CH:0:-1], sc[0][H, g, ::-1], -BIG, ALU.add, ALU.max)
                    after_(L.dve, i, "mseg", g)
                    after_(L.act, i - 1, "carry", g)
                    ts(L.dve.done("dcar"), sm[g][H, 0:1], last_of(sc[0], g, H), we[g][3][H, 0:1], 0.0, ALU.subtract, ALU.min)
                for g in G:
                    after_(L.dve, i, "mseg", g)
                    after_(L.act, i - 1, "ex", g)
                    tt(L.dve.done("d"), we[g][4][H, :], we[g][1][H, :], we[g][3][H, :], ALU.subtract)
                for g in G:
                    after_(L.pe, i, "xp", g)
                    after_(L.act, i, "ex", g)
                    after_(L.dve, i - 1, "num", g)
                    tt(L.dve.done("val"), we[g][7][H, :], ps[g][0][H, :], we[g][5][H, :], ALU.mult)
                for g in G:
                    after_chunk_before(dve.wait_ge, L.dve, i, "num", g)
                    after_(L.act, i, "carry", g)
                    tt(s_l1_c, sm[g][H, 2:3], last_of(sc[1], g, H), sm[g][H, 1:2], ALU.mult)
                    tt(L.dve.done("carry"), sm[g][H, 3:4], last_of(sc[2], g, H), sm[g][H, 1:2], ALU.mult)
                    after_(L.dve, i, "carry", g)
                    after_(L.act, i, "ex", g)
                    dve.wait_ge(L.mk[g], 16 * (i + 1))
                    scan(L.dve.done("den"), sc[1][H, g, :], mk[H, g, 0:CH], we[g][5][H, :], sm[g][H, 2:3], ALU.mult, ALU.add)
                    after_(L.dve, i, "carry", g)
                    after_(L.dve, i, "val", g)
                    scan(L.dve.done("num"), sc[2][H, g, :], mk[H, g, 0:CH], we[g][7][H, :], sm[g][H, 3:4], ALU.mult, ALU.add)
                for g in G:
                    after_(L.dve, i, "den", g)
                    ts(L.dve.done("dmax"), we[g][8][H, :], sc[1][H, g, :], 1e-30, None, ALU.max)
                for g in G:
                    after_(L.act, i, "rden", g)
                    tt(L.dve.done("att"), we[g][10][H, :], sc[2][H, g, :], we[g][8][H, :], ALU.mult)
                for g in G:
                    after_(L.dve, i, "att", g)
                    after_(L.pe, i - 1, "out", g)
                    after_(L.act, i, "z", g)
                    tt(L.dve.done("v2"), we[g][2][H, :], we[g][10][H, :], z[g][H, :], ALU.add)
            for k in G:
                dve.wait_ge(L0.sca[k], ALL)
            over_rounds(dve, l1)

            def per_node(a):
                return a.unsqueeze(2).broadcast_to([P, 8, C])

            def rows_mean(i):
                for g in DG:
                    dve.wait_ge(dn_sem[g], 16 * (i + 1))
                    after_(R_dve, i - 1, "norm", g)
                    dve.reduce_sum(ds[:, g, 0, :], dn[:, g, :, 0:C], AX_X).then_inc(R_dve.done("sum"), 1)
                for g in DG:
                    after_(R_dve, i, "sum", g)
                    ts(R_dve.done("mean"), ds[:, g, 0, :], ds[:, g, 0, :], 1.0 / C, None, ALU.mult)
                for g in DG:
                    after_(R_dve, i, "mean", g)
                    tt(R_dve.done("centered"), zr[g], dn[:, g, :, 0:C], per_node(ds[:, g, 0, :]), ALU.subtract)

            def rows_var(i):
                for g in DG:
                    after_(R_act, i, "square", g)
                    after_(R_act, i - 1, "ln", g)
                    dve.reduce_sum(ds[:, g, 1, :], pkr[g], AX_X).then_inc(R_dve.done("sumsq"), 1)

            def rows_norm(i):
                for g in DG:
                    after_(R_act, i, "rstd", g)
                    tt(R_dve.done("norm"), pk[g].rearrange("p k (a c) -> p a k c", a=2),
                       zr[g].rearrange("p (a k) c -> p a k c", a=2),
                       ds[:, g, 3, :].rearrange("p (a k) -> p a k", a=2).unsqueeze(3).broadcast_to([P, 2, 4, C]), ALU.mult)

            def dense(i, ahead=True):
                S = D_dve
                for g in DG:
                    after_(D_act, i, "relu", g)
                    after_(D_act, i, "z", g)
                    tt(S.done("y3"), wd[g][5][:, :], wd[g][3][:, :], wd[g][4][:, :], ALU.add)
                for g in DG:
                    after_(D_act, i, "r3", g)
                    after_(D_pe, i - 1, "gi", g)
                    tt(S.done("x3"), wd[g][6][:, :], ps[g][1][:, :], wd[g][2][:, :], ALU.mult)
                if ahead:
                    rows_mean(i + 1)
                for g in DG:
                    after_(D_pe, i, "gh", g)
                    after_(D_act, i, "r", g)
                    stt(S.done("q"), wd[g][3][:, :], ps[g][0][:, :], dg_b[:, 3:4], wd[g][7][:, :], ALU.add, ALU.mult)
                for g in DG:
                    after_(S, i, "q", g)
                    after_(D_pe, i, "gi", g)
                    tt(S.done("a"), wd[g][4][:, :], ps[g][1][:, :], wd[g][3][:, :], ALU.add)
                for g in DG:
                    after_(D_act, i, "n", g)
                    tt(S.done("xn"), wd[g][3][:, :], wd[g][6][:, :], wd[g][5][:, :], ALU.subtract)
                for g in DG:
                    after_(S, i, "xn", g)
                    tt(S.done("zxn"), wd[g][3][:, :], wd[g][3][:, :], wd[g][8][:, :], ALU.mult)
                for g in DG:
                    after_(S, i, "zxn", g)
                    tt(S.done("o"), wd[g][3][:, :], wd[g][3][:, :], wd[g][5][:, :], ALU.add)
                for g in DG:
                    after_(S, i, "o", g)
                    tt(S.done("y4"), wd[g][7][:, :], wd[g][3][:, :], wd[g][6][:, :], ALU.add)
                if ahead:
                    rows_var(i + 1)
                for g in DG:
                    after_(D_act, i, "r4", g)
                    after_(D_pe, i - 1, "out", g)
                    tt(S.done("x4"), wd[g][3][:, :], ps[g][0][:, :], wd[g][2][:, :], ALU.mult)
                if ahead:
                    rows_norm(i + 1)
            for k in G:
                dve.wait_ge(L1.sca[k], ALL)
            rows_mean(0)
            rows_var(0)
            rows_norm(0)
            over_rounds(dve, dense, DROUNDS - 1)
            dense(DROUNDS - 1, ahead=False)

            def l2(i):
                L = L2
                S = L.dve
                for g in G:
                    dve.wait_ge(L.mk[g], 16 * (i + 1))
                    after_chunk_before(dve.wait_ge, L.dve, i, "cnt", g)
                    scan(S.done("cnt"), sc[1][U, g, :], mk[U, g, 0:CH], ones[U, :], last_of(sc[1], g, U), ALU.mult, ALU.add)
                for g in G:
                    dve.wait_ge(L.gat[g], 128 * (i + 1))
                    ts(S.done("fsel"), sm[g][:, 4:8], gat[:, g, :, 2 * TW - 1], -float(SKIP), float(SKIP), ALU.mult, ALU.add)
                for g in G:
                    after_(S, i, "fsel", g)
                    dve.wait_ge(L.gst[g], 32 * (i + 1))
                    tt(S.done("srcf"), idx[:, I_SRCF, bass.ds((W * i + g) * 4, 4)], sm[g][:, 4:8], gst[:, g, 1, :], ALU.add)
                for g in G:
                    again(dve.wait_ge, cn_sem[g], 48, i)
                    after_(S, i, "cnt", g)
                    dve.reciprocal(we[g][11][0:1, :], sc[1][C:C + 1, g, :]).then_inc(S.done("rcnt"), 1)
                for g in G:
                    after_(L.act, i, "rstd", g)
                    after_(L.pe, i - 1, "h", g)
                    tt(S.done("x2"), we[g][5][:, :], ps[g][1][:, :], we[g][2][:, :], ALU.mult)
                for g in G:
                    after_(L.act, i, "nout", g)
                    after_(S, i, "x2", g)
                    tt(S.done("msg"), we[g][6][U, :], we[g][10][U, :], we[g][5][U, :], ALU.mult)
                for g in G:
                    after_(S, i, "msg", g)
                    after_chunk_before(dve.wait_ge, L.dve, i, "agg", g)
                    scan(S.done("agg"), sc[0][U, g, :], mk[U, g, 0:CH], we[g][6][U, :], last_of(sc[0], g, U), ALU.mult, ALU.add)
                for g in G:
                    after_(S, i, "agg", g)
                    after_(L.act, i, "nin", g)
                    tt(S.done("aggn"), we[g][7][U, :], sc[0][U, g, :], we[g][4][U, :], ALU.mult)
                for g in G:
                    after_(L.act, i, "relu", g)
                    after_(L.pe, i - 1, "out", g)
                    tt(S.done("y3"), we[g][9][:, :], we[g][5][:, :], we[g][8][:, :], ALU.add)
                for g in G:
                    after_(L.act, i, "logd", g)
                    ts(S.done("f2"), we[g][7][0:1, :], we[g][3][0:1, :], iavg[0:1, :], None, ALU.mult)
                for g in G:
                    after_(L.act, i, "rlog", g)
                    after_(S, i, "f2", g)
                    stt(S.done("f3"), we[g][10][0:1, :], we[g][6][0:1, :], avg[0:1, :], we[g][7][0:1, :], ALU.mult, ALU.mult)
            for k in DG:
                dve.wait_ge(do_sem[k], 16 * DROUNDS)
            over_rounds(dve, l2)

            def per_end(a):
                return a.rearrange("p (t a) -> p t a", a=2).unsqueeze(3).broadcast_to([P, 4, 2, C])

            def ends(a):
                return a.rearrange("p t (a c) -> p t a c", a=2)

            def ends_mean(i):
                for g in G:
                    dve.wait_ge(L3.gat[g], 128 * (i + 1))
                    after_(Q_dve, i - 1, "norm", g)
                    dve.reduce_sum(ds[:, g, 0, :].rearrange("p (t a) -> p t a", a=2), ends(gat[:, g, :, 0:P]),
                                   AX_X).then_inc(Q_dve.done("sum"), 1)
                for g in G:
                    after_(Q_dve, i, "sum", g)
                    ts(Q_dve.done("mean"), ds[:, g, 0, :], ds[:, g, 0, :], 1.0 / C, None, ALU.mult)
                for g in G:
                    after_(Q_dve, i, "mean", g)
                    tt(Q_dve.done("centered"), ends(z[g].rearrange("p (t k) -> p t k", t=4)), ends(gat[:, g, :, 0:P]),
                       per_end(ds[:, g, 0, :]), ALU.subtract)

            def ends_var(i):
                for g in G:
                    after_(Q_act, i, "square", g)
                    after_(Q_act, i - 1, "ln", g)
                    dve.reduce_sum(ds[:, g, 1, :], pkr[g], AX_X).then_inc(Q_dve.done("sumsq"), 1)

            def ends_norm(i):
                for g in G:
                    after_(Q_act, i, "rstd", g)
                    tt(Q_dve.done("norm"), ends(pk[g]), ends(z[g].rearrange("p (t k) -> p t k", t=4)),
                       per_end(ds[:, g, 3, :]), ALU.mult)

            def l3(i, ahead=True):
                L = L3
                S = L.dve
                for g in G:
                    after_(L.act, i, "ha", g)
                    after_(L.pe, i, "ew", g)
                    tt(S.done("hw"), we[g][5][:, :], ps[g][1][:, :], we[g][5][:, :], ALU.mult)
                def sums(g):
                    dve.wait_ge(L.mk[g], 16 * (i + 1))
                    after_(L.act, i, "h", g)
                    after_chunk_before(dve.wait_ge, L.dve, i, "s1", g)
                    scan(S.done("s1"), sc[0][:, g, :], mk[:, g, 0:CH], we[g][6][:, :], last_of(sc[0], g, slice(0, P)), ALU.mult, ALU.add)
                    after_(L.act, i, "hsq", g)
                    after_chunk_before(dve.wait_ge, L.dve, i, "s2", g)
                    scan(S.done("s2"), sc[1][U, g, :], mk[U, g, 0:CH], we[g][1][U, :], last_of(sc[1], g, U), ALU.mult, ALU.add)

                def spread(g):
                    dve.wait_ge(cl_sem[g], 48 * (i + 1))
                    after_(S, i, "s1", g)
                    after_(L.pe, i - 1, "u", g)
                    tt(S.done("mean"), we[g][9][:, :], sc[0][:, g, :], sc[3][:, g, :], ALU.mult)
                    after_(S, i, "mean", g)
                    tt(S.done("msq"), we[g][2][U, :], we[g][9][U, :], we[g][9][U, :], ALU.mult)
                    tt(S.done("ms2"), we[g][11][U, :], sc[1][U, g, :], sc[3][U, g, :], ALU.mult)
                    after_(S, i, "ms2", g)
                    tt(S.done("vard"), we[g][11][U, :], we[g][11][U, :], we[g][2][U, :], ALU.subtract)
                    after_(S, i, "vard", g)
                    ts(S.done("var"), we[g][11][U, :], we[g][11][U, :], 0.0, None, ALU.max)
                    after_(L.act, i, "hneg", g)
                    after_(L.act, i, "negm", g)
                    after_chunk_before(dve.wait_ge, L.dve, i, "mx", g)
                    scan(S.done("mx"), sc[2][:, g, :], negm[g][:, 0:CH], we[g][7][:, :], last_of(sc[2], g, slice(0, P)), ALU.add, ALU.max)

                def scaled(g):
                    after_(L.pe, i, "p", g)
                    tt(S.done("fp"), we[g][5][:, :], ps[g][1][:, :], ear[g][:, :], ALU.mult)

                sums(0)
                spread(0)
                sums(1)
                scaled(0)
                spread(1)
                sums(2)
                scaled(1)
                spread(2)
                scaled(2)
                if ahead:
                    ends_mean(i + 1)
                for g in G:
                    after_(L.act, i, "rz", g)
                    after_(L.pe, i, "g2", g)
                    stt(S.done("q"), we[g][8][H, :], ps[g][1][U, :], brow[U, 1, 2:3], we[g][10][U, :], ALU.add, ALU.mult)
                for g in G:
                    after_(S, i, "q", g)
                    tt(S.done("a"), we[g][2][H, :], ps[g][1][H, :], we[g][8][H, :], ALU.add)
                for g in G:
                    after_(L.act, i, "n", g)
                    tt(S.done("xn"), we[g][8][H, :], we[g][4][H, :], we[g][6][H, :], ALU.subtract)
                for g in G:
                    after_(S, i, "xn", g)
                    tt(S.done("zxn"), we[g][8][H, :], we[g][8][H, :], we[g][10][H, :], ALU.mult)
                for g in G:
                    after_(S, i, "zxn", g)
                    tt(S.done("o"), we[g][8][H, :], we[g][8][H, :], we[g][6][H, :], ALU.add)
                for g in G:
                    after_(S, i, "o", g)
                    tt(S.done("y4"), we[g][11][H, :], we[g][8][H, :], we[g][4][H, :], ALU.add)
                if ahead:
                    ends_var(i + 1)
                for g in G:
                    after_(L.act, i, "rstd4", g)
                    after_(L.pe, i - 1, "out", g)
                    tt(S.done("x4"), we[g][3][H, :], ps[g][0][H, :], we[g][2][H, :], ALU.mult)
                if ahead:
                    ends_norm(i + 1)
            for k in G:
                dve.wait_ge(L2.sca[k], ALL)
            ends_mean(0)
            ends_var(0)
            ends_norm(0)
            over_rounds(dve, l3, ROUNDS - 1)
            l3(ROUNDS - 1, ahead=False)

        @block.tensor
        def _(pe):
            def hold(s, v):
                pe.wait_ge(s, v)
                pe.sem_inc(s_tick_pe, 1)

            def hold_after(steps, i, name, g=0):
                hold(steps.sem, steps.at(i, name, g))

            def product(dest, parts, done=None):
                for k, (lhsT, rhs) in enumerate(parts):
                    m = pe.matmul(dest, lhsT, rhs, start=(k == 0), stop=(k == len(parts) - 1))
                if done is not None:
                    m.then_inc(done, 1)

            for S in (L0.pe, L1.pe, L2.pe, L3.pe, D_pe):
                pe.sem_inc(S.sem, S.n)

            pe.wait_ge(s_wload, NW)
            pe.wait_ge(s_wdve, 3)
            product(banks[0][:, 0:C], [(w1_l[:, :], att_m[:, 0, :]), (w1_r[:, :], att_m[:, 1, :])])
            product(banks[1][:, 0:P], [(w3t_l[:, :], wpre2[:, 0, :]), (w3t_r[:, :], wpre2[:, 1, :])])
            product(banks[2][0:4, 0:P], [(wet[:, :], wpre2[:, 2, :])])
            product(banks[2][:, 256:257], [(wpre2[:, 2, :], be_col[:, :])])
            product(banks[3][0:C, 0:P], [(w3t_l[:, 0:C], wpm[:, :])])
            product(banks[3][0:C, 256:256 + C], [(wpm[:, C:P], w3t_l[:, 0:C])])
            product(banks[4][:, 0:1], [(avgmat[0:125, :], nvs[:, :])], s_wpe)
            pe.wait_ge(s_wdve, 4)
            product(banks[5][0:C, 0:1], [(wstd[:, s, :], fac0[:, 4 + s:5 + s]) for s in range(3)], s_wpe)
            pe.wait_ge(s_wdve, 5)
            for g in range(3):
                product(banks[6][:, 8 * g:8 * g + 1], [(wih2[:, g, :], out0[:, :])])
            product(banks[7][:, 0:3 * C].rearrange("p (g c) -> p g c", g=3), [(mmt2[:, :], wih2[:, :, 0:C])], s_wpe)

            for n, (src_tile, level) in enumerate(turn_plan):
                pe.wait_ge(s_sort, level)
                for s in range(2):
                    for h in range(2):
                        m = pe.transpose(banks[0][:, (2 * s + h) * P:(2 * s + h + 1) * P],
                                         src_tile[:, s, h * P:(h + 1) * P], ident)
                m.then_inc(s_sortt, 1)
            pe.wait_ge(s_lists, 1)
            for m_ in range(7):
                for h in range(2):
                    m = pe.transpose(banks[m_][:, h * P:(h + 1) * P], lists[:, m_, h * P:(h + 1) * P], ident)
                m.then_inc(s_lt, 1)

            def turn(dest, tiles, done):
                for t, a in enumerate(tiles):
                    m = pe.transpose(dest[:, blk[t]], a, ident)
                m.then_inc(done, 1)

            def turn_back(dest, a, rows, done):
                for t in range(4):
                    m = pe.transpose(dest[:, rows * t:rows * (t + 1)], a[0:rows, blk[t]], ident[0:rows, 0:rows])
                m.then_inc(done, 1)

            pe.wait_ge(s_idx, 7)
            def l0(i):
                L = L0
                for g in G:
                    hold(L.gat[g], 128 * (i + 1))
                    hold_after(L.act, i - 1, "z", g)
                    turn(ps[g][0], [gat[:, g, t, 0:P] for t in range(4)], L.pe.done("z"))
                for g in G:
                    hold(ec_sem[g], 64 * (i + 1))
                    hold_after(L.dve, i - 1, "ea", g)
                    hold_after(L.act, i - 1, "out", g)
                    turn(ps[g][1], [eca[:, g, t, 0:P] for t in range(4)], L.pe.done("ea"))
                for g in G:
                    hold_after(L.act, i, "z", g)
                    hold_after(L.dve, i, "ea", g)
                    hold_after(L.dve, i - 1, "srelu", g)
                    hold_after(L.act, i - 1, "sabs", g)
                    product(ps[g][0][:, :], [(w_fs_z[:, :], z[g][:, :]), (w_fs_e[:, :], ear[g][:, :])], L.pe.done("fs"))
                for g in G:
                    hold_after(L.dve, i, "y", g)
                    product(ps[g][1][0:C, :], [(center[0:C, 0:C], w_l0[g][1][0:C, :])], L.pe.done("center"))
                for g in G:
                    hold_after(L.act, i, "sq", g)
                    product(ps[g][0][0:C, :], [(mean64[0:C, 0:C], w_l0[g][2][0:C, :])], L.pe.done("var"))
                for g in G:
                    hold_after(L.dve, i, "x1", g)
                    hold_after(L.act, i - 1, "out", g)
                    turn_back(ps[g][1], w_l0[g][2], C, L.pe.done("out"))
            over_rounds(pe, l0)

            def l1(i):
                L = L1
                for g in G:
                    hold_after(L.act, i, "pack", g)
                    turn(ps[g][0], [pk[g][:, t, :] for t in range(4)], L.pe.done("z"))
                for g in G:
                    hold_after(L.act, i, "z", g)
                    hold_after(L.dve, i - 1, "e", g)
                    product(ps[g][1][0:C, :], [(w_score[:, :], z[g][:, :])], L.pe.done("score"))
                for g in G:
                    hold_after(L.dve, i - 1, "val", g)
                    product(ps[g][0][0:C, :], [(w1t[C:P, :], z[g][C:P, :])], L.pe.done("xp"))
                for g in G:
                    hold_after(L.dve, i, "v2", g)
                    hold_after(L.act, i, "norm", g)
                    hold_after(L.act, i - 1, "out", g)
                    turn_back(ps[g][1], we[g][2], C + 1, L.pe.done("out"))
            for k in G:
                pe.wait_ge(L0.sca[k], ALL)
            over_rounds(pe, l1)

            def dense(i):
                for g in DG:
                    hold_after(R_dve, i, "norm", g)
                    hold_after(D_act, i - 1, "out", g)
                    turn(ps[g][0], [pk[g][:, k, :] for k in range(4)], D_pe.done("z"))
                for g in DG:
                    hold_after(D_act, i, "z", g)
                    product(ps[g][0][:, :], [(w2_bd[:, :], wd[g][3][:, :])], D_pe.done("h"))
                for g in DG:
                    hold_after(D_dve, i, "y3", g)
                    product(ps[g][1][:, :], [(center, wd[g][5][:, :])], D_pe.done("c3"))
                for g in DG:
                    hold_after(D_act, i, "sq3", g)
                    product(ps[g][0][:, :], [(mean64, wd[g][0][:, :])], D_pe.done("v3"))
                for b, k, name in ((0, 0, "gr"), (1, 1, "gz"), (0, 3, "gh"), (1, 2, "gi")):
                    for g in DG:
                        hold_after(D_dve, i, "x3", g)
                        if name in ("gh", "gi"):
                            hold_after(D_act, i, ("r", "zg")[b], g)
                        product(ps[g][b][:, :], [(dg[:, k, :], wd[g][6][:, :])], D_pe.done(name))
                for g in DG:
                    hold_after(D_dve, i, "y4", g)
                    product(ps[g][0][:, :], [(center, wd[g][7][:, :])], D_pe.done("c4"))
                for g in DG:
                    hold_after(D_act, i, "sq4", g)
                    product(ps[g][1][:, :], [(mean64, wd[g][0][:, :])], D_pe.done("v4"))
                for g in DG:
                    hold_after(D_dve, i, "x4", g)
                    turn_back(ps[g][1], wd[g][3], P, D_pe.done("out"))
            for k in G:
                pe.wait_ge(L1.sca[k], ALL)
            over_rounds(pe, dense, DROUNDS)

            def l2(i):
                L = L2
                for g in G:
                    hold_after(L.act, i, "pack", g)
                    turn(ps[g][0], [pk[g][:, t, :] for t in range(4)], L.pe.done("z"))
                for g in G:
                    hold_after(L.dve, i - 1, "msg", g)
                    hold(L.gat[g], 128 * (i + 1))
                    for t in range(4):
                        m = pe.matmul(ps[g][1][:, blk[t]], gat[:, g, t, TW + C:TW + C + 1].broadcast_to([P, P]), ident,
                                      start=True, stop=True)
                    m.then_inc(L.pe.done("norm"), 1)
                for g in G:
                    hold_after(L.act, i, "z", g)
                    hold_after(L.act, i, "nout", g)
                    hold_after(L.dve, i - 1, "x2", g)
                    hold_after(L.act, i - 1, "out", g)
                    product(ps[g][1][:, :], [(center, z[g][:, :])], L.pe.done("center"))
                for g in G:
                    hold_after(L.act, i, "sq", g)
                    product(ps[g][0][:, :], [(mean64, we[g][0][:, :])], L.pe.done("var"))
                for g in G:
                    hold_after(L.dve, i, "aggn", g)
                    hold_after(L.act, i - 1, "relu", g)
                    product(ps[g][0][:, :], [(w2_bd[:, :], we[g][5][:, :]), (w2_neg[C:P, :], we[g][7][C:P, :])], L.pe.done("h"))
                for g in G:
                    hold_after(L.dve, i, "y3", g)
                    hold_after(L.act, i - 1, "out", g)
                    turn_back(ps[g][1], we[g][9], P, L.pe.done("out"))
            for k in DG:
                pe.wait_ge(do_sem[k], 16 * DROUNDS)
            over_rounds(pe, l2)

            def l3(i):
                L = L3
                for g in G:
                    hold_after(Q_dve, i, "norm", g)
                    hold_after(L.act, i - 1, "z", g)
                    turn(ps[g][0], [pk[g][:, t, :] for t in range(4)], L.pe.done("z"))
                for g in G:
                    hold_after(L.act, i - 1, "ea", g)
                    hold_after(L.act, i - 1, "out", g)
                    hold(eal_sem[g], 16 * (i + 1))
                    for t in range(4):
                        m = pe.transpose(ps[g][1][0:4, blk[t]], eas[:, g, t, :], ident)
                    m.then_inc(L.pe.done("ea"), 1)
                for g in G:
                    hold_after(L.act, i, "ea", g)
                    hold_after(L.act, i, "z", g)
                    hold_after(L.dve, i - 1, "a", g)
                    product(ps[g][0][:, :], [(w_h[:, :], we[g][4][:, :]), (w_hea[:, :], we[g][3][0:4, :])], L.pe.done("h"))
                for g in G:
                    product(ps[g][1][:, :], [(selw[0:4, :], we[g][3][0:4, :])], L.pe.done("ew"))
                def scaled(g):
                    hold_after(L.act, i, "std", g)
                    hold_after(L.dve, i, "mx", g)
                    hold_after(L.dve, i - 1, "x4", g)
                    product(ps[g][1][:, :], [(wp_a1[:, :], we[g][9][:, :]), (wp_a2[:, :], sc[2][:, g, :])], L.pe.done("p"))

                def update(g):
                    hold_after(L.dve, i, "fp", g)
                    hold_after(L.act, i - 1, "out", g)
                    product(ps[g][0][:, :], [(wu_x[:, :], we[g][4][0:C, :]), (wu_a1[:, :], we[g][9][:, :]),
                                          (wu_a2[:, :], sc[2][:, g, :]), (wu_f[:, :], we[g][5][:, :])], L.pe.done("u"))

                def gates(g):
                    hold_after(L.act, i, "u", g)
                    product(ps[g][0][:, :], [(w_g1[:, :], we[g][4][:, :])], L.pe.done("g1"))
                    product(ps[g][1][:, :], [(w_g2[:, :], we[g][4][:, :])], L.pe.done("g2"))

                scaled(0)
                update(0)
                scaled(1)
                gates(0)
                update(1)
                scaled(2)
                gates(1)
                update(2)
                gates(2)
                for g in G:
                    hold_after(L.dve, i, "y4", g)
                    product(ps[g][0][0:C, :], [(center[0:C, 0:C], we[g][11][0:C, :])], L.pe.done("center4"))
                for g in G:
                    hold_after(L.act, i, "sq4", g)
                    product(ps[g][1][0:C, :], [(mean64[0:C, 0:C], we[g][0][0:C, :])], L.pe.done("var4"))
                for g in G:
                    hold_after(L.dve, i, "x4", g)
                    turn_back(ps[g][1], we[g][3], C, L.pe.done("out"))
            for k in G:
                pe.wait_ge(L2.sca[k], ALL)
            over_rounds(pe, l3)

        @block.scalar
        def _(act):
            def run(name_done, *args, **kw):
                act.activation(*args, **kw).then_inc(name_done, 1)

            def after_act(steps, i, name, g=0):
                act.wait_ge(steps.sem, steps.at(i, name, g))

            for S in (L0.act, L1.act, L2.act, L3.act, D_act, R_act, Q_act):
                act.sem_inc(S.sem, S.n)
            act.sem_inc(d1_act.sem, 2 * d1_act.n)

            act.preload_act_table_set(LN_EXP)
            act.wait_ge(s_wload, NW)
            act.wait_ge(s_const, 3)
            run(s_wact, nv[:, :], nv[:, :], ACT.Ln, bias=one_col[0:125, :])
            run(s_wact, fac0[:, 0:1], eps_col[0:C, :], ACT.Ln)
            act.wait_ge(s_wact, 2)
            run(s_wact, fac0[:, 4:5], fac0[:, 0:1], ACT.Exp, scale=0.5)
            run(s_wact, fac0[:, 1:2], one_col[0:C, :], ACT.Ln, bias=one_col[0:C, :])

            def rstd(L, i, names, cbank, sq, vbank, ln, out_, rows=slice(0, P), ready="center", vready="var", pe_=None,
                     free=(), w=we, streams=G):
                pe_ = pe_ or L.pe
                for g in streams:
                    after_act(pe_, i, ready, g)
                    run(L.act.done(names[0]), w[g][sq][rows, :], ps[g][cbank][rows, :], ACT.Square)
                for g in streams:
                    after_act(pe_, i, vready, g)
                    run(L.act.done(names[1]), w[g][ln][rows, :], ps[g][vbank][rows, :], ACT.Ln, bias=eps_col[rows, :])
                for g in streams:
                    after_act(L.act, i, names[1], g)
                    for steps, j, name in free:
                        after_act(steps, j, name, g)
                    run(L.act.done(names[2]), w[g][out_][rows, :], w[g][ln][rows, :], ACT.Exp, scale=-0.5)

            H = slice(0, C)
            U = slice(C, P)

            def l0(i):
                L = L0
                for g in G:
                    after_act(L.pe, i, "z", g)
                    after_act(L.pe, i - 1, "fs", g)
                    after_act(L.dve, i - 1, "y", g)
                    run(L.act.done("z"), z[g][:, :], ps[g][0][:, :], ACT.Copy)
                for g in G:
                    after_act(L.pe, i, "fs", g)
                    after_act(L.dve, i - 1, "core", g)
                    run(L.act.done("sabs"), w_l0[g][0][:, :], ps[g][0][:, :], ACT.Abs, bias=b_fs[:, :])
                for g in G:
                    after_act(L.act, i, "sabs", g)
                    run(L.act.done("exps"), w_l0[g][0][:, :], w_l0[g][0][:, :], ACT.Exp, scale=-1.0)
                for g in G:
                    after_act(L.act, i, "exps", g)
                    run(L.act.done("log"), w_l0[g][0][:, :], w_l0[g][0][:, :], ACT.Ln, bias=one_col[:, :])
                for g in G:
                    after_act(L.dve, i, "core", g)
                    after_act(L.dve, i - 1, "msg", g)
                    run(L.act.done("gate"), w_l0[g][2][U, :], w_l0[g][1][H, :], ACT.Exp, scale=-1.0)
                if fills(i):
                    after_act(d1_dve, i, "centered")
                    after_act(d1_dve, i - 1, "sumsq")
                    run(d1_act.done("square"), d1r[0:D1P, :, :], d1o[0:D1P, :, 0:C], ACT.Square)
                rstd(L, i, ("sq", "ln", "rstd"), 1, 2, 0, 3, 0, H, free=((L.dve, i - 1, "x1"),), w=w_l0)
                if fills(i):
                    after_act(d1_dve, i, "sumsq")
                    run(d1_act.done("ln"), d1s[0:D1P, 2, :], d1s[0:D1P, 1, :], ACT.Ln, scale=1.0 / C, bias=eps_col[0:D1P, :])
                    after_act(d1_act, i, "ln")
                    run(d1_act.done("rstd"), d1s[0:D1P, 3, :], d1s[0:D1P, 2, :], ACT.Exp, scale=-0.5)
                for g in G:
                    after_act(L.pe, i, "out", g)
                    again(act.wait_ge, h0_sem[g], 16, i)
                    run(L.act.done("out"), ot[:, g, :, 0:C], ps[g][1][:, 0:4 * C].rearrange("p (t k) -> p t k", t=4), ACT.Copy)
            over_rounds(act, l0)

            def l1(i):
                L = L1
                for g in G:
                    act.wait_ge(L.gat[g], 128 * (i + 1))
                    after_act(L.pe, i - 1, "z", g)
                    run(L.act.done("pack"), pk[g].rearrange("p t (a k) -> p t a k", a=2),
                        gat[:, g, :, :].rearrange("p t (a k) -> p t a k", a=2)[:, :, :, 0:C], ACT.Copy)
                for g in G:
                    after_act(L.pe, i, "z", g)
                    after_act(L.pe, i - 1, "xp", g)
                    after_act(L.dve, i - 1, "v2", g)
                    run(L.act.done("z"), z[g][:, :], ps[g][0][:, :], ACT.Copy)
                for g in G:
                    act.wait_ge(L.mk[g], 16 * (i + 1))
                    after_act(L.dve, i - 1, "mseg", g)
                    run(L.act.done("negm"), negm[g][H, 0:CH], mk[H, g, 0:CH], ACT.Copy, scale=BIG, bias=-BIG)
                for g in G:
                    after_act(L.dve, i, "cnt", g)
                    run(L.act.done("lncnt"), we[g][6][C:C + 1, :], sc[3][C:C + 1, g, :], ACT.Ln)
                for g in G:
                    after_act(L.act, i, "lncnt", g)
                    after_act(L.pe, i - 1, "out", g)
                    run(L.act.done("norm"), we[g][2][C:C + 1, :], we[g][6][C:C + 1, :], ACT.Exp, scale=-0.5)
                for g in G:
                    after_act(L.pe, i, "score", g)
                    after_act(L.dve, i - 1, "e", g)
                    run(L.act.done("lrelu"), we[g][0][H, :], ps[g][1][H, :], ACT.Copy, scale=0.2)
                for g in G:
                    after_act(L.dve, i, "dcar", g)
                    after_act(L.dve, i - 1, "carry", g)
                    run(L.act.done("carry"), sm[g][H, 1:2], sm[g][H, 0:1], ACT.Exp)
                for g in G:
                    after_act(L.dve, i, "d", g)
                    after_act(L.dve, i - 1, "val", g)
                    run(L.act.done("ex"), we[g][5][H, :], we[g][4][H, :], ACT.Exp)
                for g in G:
                    after_act(L.dve, i, "dmax", g)
                    run(L.act.done("lnden"), we[g][9][H, :], we[g][8][H, :], ACT.Ln)
                for g in G:
                    after_act(L.act, i, "lnden", g)
                    run(L.act.done("rden"), we[g][8][H, :], we[g][9][H, :], ACT.Exp, scale=-1.0)
                for g in G:
                    after_act(L.pe, i, "out", g)
                    again(act.wait_ge, h1_sem[g], 16, i)
                    run(L.act.done("out"), ot[:, g, :, 0:C + 1],
                        ps[g][1][:, 0:4 * (C + 1)].rearrange("p (t k) -> p t k", t=4), ACT.Copy)
            for k in G:
                act.wait_ge(L0.sca[k], ALL)
            over_rounds(act, l1)

            class D:
                pe, act = D_pe, D_act

            def rows_square(i):
                for g in DG:
                    after_act(R_dve, i, "centered", g)
                    after_act(D_pe, i - 1, "z", g)
                    run(R_act.done("square"), pkr[g], zr[g], ACT.Square)

            def rows_rstd(i):
                for g in DG:
                    after_act(R_dve, i, "sumsq", g)
                    run(R_act.done("ln"), ds[:, g, 2, :], ds[:, g, 1, :], ACT.Ln, scale=1.0 / C, bias=eps_col[:, :])
                for g in DG:
                    after_act(R_act, i, "ln", g)
                    after_act(R_dve, i - 1, "norm", g)
                    run(R_act.done("rstd"), ds[:, g, 3, :], ds[:, g, 2, :], ACT.Exp, scale=-0.5)

            def dense(i, ahead=True):
                for g in DG:
                    after_act(D_pe, i, "z", g)
                    after_act(D_dve, i - 1, "x4", g)
                    after_act(D_pe, i - 1, "out", g)
                    run(D_act.done("z"), wd[g][3][:, :], ps[g][0][:, :], ACT.Copy)
                for g in DG:
                    after_act(D_pe, i, "h", g)
                    run(D_act.done("relu"), wd[g][4][:, :], ps[g][0][:, :], ACT.Relu, bias=b2_col[:, :])
                rstd(D, i, ("sq3", "ln3", "r3"), 1, 0, 0, 1, 2, ready="c3", vready="v3",
                     free=((D_dve, i - 1, "x4"),), w=wd, streams=DG)
                for k, (t, name) in enumerate(((7, "r"), (8, "zg"))):
                    for g in DG:
                        after_act(D_pe, i, ("gr", "gz")[k], g)
                        run(D_act.done(name), wd[g][t][:, :], ps[g][k][:, :], ACT.Sigmoid, bias=dg_b[:, k:k + 1])
                for g in DG:
                    after_act(D_dve, i, "a", g)
                    run(D_act.done("n"), wd[g][5][:, :], wd[g][4][:, :], ACT.Tanh, bias=dg_b[:, 2:3])
                act.preload_act_table_set(LN_EXP)
                if ahead:
                    rows_square(i + 1)
                rstd(D, i, ("sq4", "ln4", "r4"), 0, 0, 1, 1, 2, ready="c4", vready="v4",
                     free=((D_dve, i, "x3"),), w=wd, streams=DG)
                if ahead:
                    rows_rstd(i + 1)
                for g in DG:
                    after_act(D_pe, i, "out", g)
                    again(act.wait_ge, do_sem[g], 16, i)
                    run(D_act.done("out"), do[g].rearrange("p (a k) c -> p k a c", a=2),
                        ps[g][1][:, :].rearrange("p (k a c) -> p k a c", k=4, a=2), ACT.Copy)
            for k in G:
                act.wait_ge(L1.sca[k], ALL)
            rows_square(0)
            rows_rstd(0)
            over_rounds(act, dense, DROUNDS - 1)
            dense(DROUNDS - 1, ahead=False)

            def l2(i):
                L = L2
                for g in G:
                    act.wait_ge(L.gat[g], 128 * (i + 1))
                    after_act(L.pe, i - 1, "z", g)
                    run(L.act.done("pack"), pk[g].rearrange("p t (a k) -> p t a k", a=2),
                        gat[:, g, :, :].rearrange("p t (a k) -> p t a k", a=2)[:, :, :, 0:C], ACT.Copy)
                for g in G:
                    after_act(L.pe, i, "z", g)
                    after_act(L.pe, i - 1, "center", g)
                    run(L.act.done("z"), z[g][:, :], ps[g][0][:, :], ACT.Copy)
                for g in G:
                    after_act(L.pe, i, "norm", g)
                    after_act(L.dve, i - 1, "msg", g)
                    run(L.act.done("nout"), we[g][10][U, :], ps[g][1][U, :], ACT.Copy)
                for g in G:
                    after_act(L.dve, i, "cnt", g)
                    run(L.act.done("lncnt"), we[g][3][U, :], sc[1][U, g, :], ACT.Ln)
                for g in G:
                    after_act(L.act, i, "lncnt", g)
                    after_act(L.dve, i - 1, "aggn", g)
                    run(L.act.done("nin"), we[g][4][U, :], we[g][3][U, :], ACT.Exp, scale=-0.5)
                rstd(L, i, ("sq", "ln", "rstd"), 1, 0, 0, 1, 2, free=((L.dve, i - 1, "x2"),))
                for g in G:
                    after_act(L.dve, i, "cnt", g)
                    after_act(L.dve, i - 1, "f3", g)
                    run(L.act.done("logd"), we[g][3][0:1, :], sc[1][C:C + 1, g, :], ACT.Ln, bias=one_col[C:C + 1, :])
                for g in G:
                    after_act(L.act, i, "logd", g)
                    run(L.act.done("lnlog"), we[g][4][0:1, :], we[g][3][0:1, :], ACT.Ln)
                for g in G:
                    after_act(L.act, i, "lnlog", g)
                    run(L.act.done("rlog"), we[g][6][0:1, :], we[g][4][0:1, :], ACT.Exp, scale=-1.0)
                for g in G:
                    after_act(L.pe, i, "h", g)
                    after_act(L.dve, i - 1, "y3", g)
                    run(L.act.done("relu"), we[g][8][:, :], ps[g][0][:, :], ACT.Relu, bias=b2_col[:, :])
                for g in G:
                    after_act(L.pe, i, "out", g)
                    again(act.wait_ge, L.sca[g], 64, i)
                    again(act.wait_ge, h3_sem[g], 16, i)
                    run(L.act.done("out"), ot3[:, g, :, :], ps[g][1][:, :].rearrange("p (t k) -> p t k", t=4), ACT.Copy)
            for k in DG:
                act.wait_ge(do_sem[k], 16 * DROUNDS)
            over_rounds(act, l2)

            def ends_square(i):
                for g in G:
                    after_act(Q_dve, i, "centered", g)
                    after_act(L3.pe, i - 1, "z", g)
                    run(Q_act.done("square"), pkr[g], zr[g], ACT.Square)

            def ends_rstd(i):
                for g in G:
                    after_act(Q_dve, i, "sumsq", g)
                    run(Q_act.done("ln"), ds[:, g, 2, :], ds[:, g, 1, :], ACT.Ln, scale=1.0 / C, bias=eps_col[:, :])
                for g in G:
                    after_act(Q_act, i, "ln", g)
                    after_act(Q_dve, i - 1, "norm", g)
                    run(Q_act.done("rstd"), ds[:, g, 3, :], ds[:, g, 2, :], ACT.Exp, scale=-0.5)

            def l3(i, ahead=True):
                L = L3
                for g in G:
                    after_act(L.pe, i, "z", g)
                    after_act(L.pe, i - 1, "out", g)
                    after_act(L.dve, i - 1, "x4", g)
                    run(L.act.done("z"), we[g][4][:, :], ps[g][0][:, :], ACT.Copy)
                for g in G:
                    after_act(L.pe, i, "ea", g)
                    after_act(L.pe, i - 1, "ew", g)
                    run(L.act.done("ea"), we[g][3][0:4, :], ps[g][1][0:4, :], ACT.Copy)
                for g in G:
                    act.wait_ge(L.mk[g], 16 * (i + 1))
                    after_act(L.dve, i - 1, "mx", g)
                    run(L.act.done("negm"), negm[g][:, 0:CH], mk[:, g, 0:CH], ACT.Copy, scale=BIG, bias=-BIG)
                for g in G:
                    after_act(L.pe, i, "h", g)
                    run(L.act.done("ha"), we[g][5][:, :], ps[g][0][:, :], ACT.Identity, bias=bew_col[:, :])
                for g in G:
                    after_act(L.dve, i, "hw", g)
                    after_act(L.dve, i - 1, "o", g)
                    run(L.act.done("h"), we[g][6][:, :], we[g][5][:, :], ACT.Identity, bias=bpre_col[:, :])
                for g in G:
                    after_act(L.act, i, "h", g)
                    run(L.act.done("hneg"), we[g][7][:, :], we[g][6][:, :], ACT.Identity, scale=sgn_col[:, :])
                for g in G:
                    after_act(L.act, i, "h", g)
                    run(L.act.done("hsq"), we[g][1][U, :], we[g][6][U, :], ACT.Square)
                def deviation(g):
                    after_act(L.dve, i, "var", g)
                    run(L.act.done("lnvar"), we[g][1][U, :], we[g][11][U, :], ACT.Ln, bias=eps_col[U, :])
                    after_act(L.act, i, "lnvar", g)
                    run(L.act.done("std"), we[g][9][U, :], we[g][1][U, :], ACT.Exp, scale=0.5)

                def update(g):
                    after_act(L.pe, i, "u", g)
                    run(L.act.done("u"), we[g][4][U, :], ps[g][0][U, :], ACT.Identity, bias=bpost_col[U, :])

                deviation(0)
                deviation(1)
                update(0)
                deviation(2)
                update(1)
                update(2)
                for g in G:
                    after_act(L.pe, i, "g1", g)
                    run(L.act.done("rz"), we[g][10][:, :], ps[g][0][:, :], ACT.Sigmoid, bias=b_g1[:, :])
                for g in G:
                    after_act(L.dve, i, "a", g)
                    run(L.act.done("n"), we[g][6][H, :], we[g][2][H, :], ACT.Tanh, bias=brow[H, 0, 2:3])
                act.preload_act_table_set(LN_EXP)
                if ahead:
                    ends_square(i + 1)
                rstd(L, i, ("sq4", "ln4", "rstd4"), 0, 0, 1, 1, 2, H, ready="center4", vready="var4",
                     free=((L.act, i, "n"),))
                if ahead:
                    ends_rstd(i + 1)
                for g in G:
                    after_act(L.pe, i, "out", g)
                    again(act.wait_ge, L.sca[g], 64, i)
                    run(L.act.done("out"), ot3[:, g, :, 0:C], ps[g][1][:, 0:4 * C].rearrange("p (t k) -> p t k", t=4), ACT.Copy)
            for k in G:
                act.wait_ge(L2.sca[k], ALL)
            ends_square(0)
            ends_rstd(0)
            over_rounds(act, l3, ROUNDS - 1)
            l3(ROUNDS - 1, ahead=False)


def shape_constants():
    eye = np.eye(P, dtype=np.float32)
    two = np.kron(np.eye(2, dtype=np.float32), np.full((C, C), 1.0 / C, np.float32))
    heads = np.zeros((P, P), np.float32)
    heads[:C, :C] = np.kron(np.eye(HEADS, dtype=np.float32), np.ones((C // HEADS, C // HEADS), np.float32))
    row3 = np.zeros((P, P), np.float32)
    row3[3, :] = 1.0
    mats = np.stack([eye, eye - two, two, heads, row3], 1)
    place = np.arange(SN).reshape(P, SF)
    idx = np.repeat(place[:, None, :], 2, 1).astype(np.float32)
    bit = [1.0 - 2.0 * ((place >> k) & 1) for k in range(SK + 1)]
    bit[0] = np.ones_like(bit[0])
    sign = np.stack([bit[k] * bit[k - 1] for k in range(1, SK + 1)], 1).astype(np.float32)
    return np.ascontiguousarray(mats), np.ascontiguousarray(idx), np.ascontiguousarray(sign)


_INS = ["x", "src", "dst", "edge_attr_128", "edge_attr_4", "node_vec", "L0_gnn_W_f", "L0_gnn_b_f", "L0_gnn_W_s",
        "L0_gnn_b_s", "L1_gnn_W", "L1_gnn_src_attn", "L1_gnn_dst_attn", "L2_gnn_W", "L2_gnn_b", "L3_gnn_W",
        "L3_gnn_We", "L3_gnn_be", "L3_gnn_Wpre", "L3_gnn_bpre", "L3_gnn_Wpost", "L3_gnn_bpost", "L3_gnn_Wih",
        "L3_gnn_bih", "L3_gnn_Whh", "L3_gnn_bhh"]


def kernel(**inputs):
    import concourse.bacc as bacc
    from concourse.bass_utils import run_bass_kernel_spmd

    nc = bacc.Bacc("TRN2", target_bir_lowering=False, num_devices=1)
    arrays, args = {}, []
    named = [(n, np.ascontiguousarray(inputs[n])) for n in _INS]
    named += list(zip(("k_mats", "k_idx", "k_sign"), shape_constants()))
    for name, a in named:
        arrays[f"in_{name}"] = a
        args.append(nc.dram_tensor(f"in_{name}", a.shape, mybir.dt.from_np(a.dtype), kind="ExternalInput").ap())
    args.append(nc.dram_tensor("out_0", (N, C), F32, kind="ExternalOutput").ap())
    for name, shape in (("T", (N, TW)), ("X3", (N, C)), ("H1", (NCH * P, 4 * TW)), ("H3", (NCH * P, 4 * C)),
                        ("EC", (E, EW)), ("KD", (2, SN + 2)), ("MK", (2, SN)), ("CN", (3, NCH * CH))):
        args.append(nc.dram_tensor(name, shape, F32, kind="Internal").ap())
    gnn_kernel(nc, *args)
    r = run_bass_kernel_spmd(nc, [arrays], core_ids=[0])
    return r.results[0]["out_0"]
```
